# Optimizing a Trainium2 kernel written in Bass

```python
import numpy as np
import jax
import jax.numpy as jnp

def _softmax(x, axis=-1):
    return jax.nn.softmax(x, axis=axis)

def _gelu(x):
    return jax.nn.gelu(x, approximate=True)

def _silu(x):
    return jax.nn.silu(x)

def _sigmoid(x):
    return jax.nn.sigmoid(x)

def _layernorm(x, axis=-1, eps=1e-05):
    m = jnp.mean(x, axis=axis, keepdims=True)
    v = jnp.var(x, axis=axis, keepdims=True)
    return (x - m) / jnp.sqrt(v + eps)

def _scatter_add(tgt, idx, src, axis=0):
    return tgt.at[idx].add(src)

def _segment_sum(src, seg, n):
    return jax.ops.segment_sum(src, seg, n)
kernel_name = 'mk_seq_postln_d1_jaxref_r8_bedf1a'

def setup_inputs(seed: int=0):
    np.random.seed(seed)
    _w = jnp.asarray

    def _L0_attn_setup():
        import jax, jax.numpy as jnp
        import numpy as np
        HIDDEN = 256
        HEADS = 8
        HEAD_DIM = HIDDEN // HEADS
        EPS = 1e-05

        def _position_thetas(head_dim, scale=10000.0):
            x = jnp.linspace(0.0, 1.0, head_dim // 2)
            thetas = 1.0 / scale ** x
            return jnp.repeat(thetas, 2)

        def _decay_gammas(num_heads):
            x = jnp.linspace(np.log(1 / 32), np.log(1 / 64), num_heads)
            return 1.0 - jnp.exp(x)

        def _decay_mask(n, s, gammas):
            qpos = jnp.arange(n, dtype=jnp.float32)[:, None]
            kpos = jnp.arange(s, dtype=jnp.float32)[None, :]
            dist = qpos - kpos
            dist = jnp.where(dist < 0, jnp.inf, dist)
            return gammas[:, None, None] ** dist[None]

        def _multiply_by_i(x):
            xe = x[..., ::2]
            xo = x[..., 1::2]
            return jnp.stack((-xo, xe), axis=-1).reshape(x.shape)

        def _theta_shift(x, sin, cos):
            return x * cos + _multiply_by_i(x) * sin
        key = jax.random.key(seed)
        ks = jax.random.split(key, 10)
        std = 0.02
        x = jax.random.normal(ks[0], (2, 512, HIDDEN), dtype=jnp.float32)

        def lin(k):
            return jax.random.normal(k, (HIDDEN, HIDDEN), dtype=jnp.float32) * std
        return {'x': x, 'w_q': lin(ks[1]), 'b_q': jnp.zeros((HIDDEN,), jnp.float32), 'w_k': lin(ks[2]), 'b_k': jnp.zeros((HIDDEN,), jnp.float32), 'w_v': lin(ks[3]), 'b_v': jnp.zeros((HIDDEN,), jnp.float32), 'w_g': lin(ks[4]), 'b_g': jnp.zeros((HIDDEN,), jnp.float32), 'w_o': lin(ks[5]), 'b_o': jnp.zeros((HIDDEN,), jnp.float32), 'gn_weight': jnp.ones((HIDDEN,), jnp.float32), 'gn_bias': jnp.zeros((HIDDEN,), jnp.float32)}
    _L0_attn_in = _L0_attn_setup()

    def _L0_ffn_setup():
        import jax, jax.numpy as jnp
        import numpy as np
        E, H, I = (8, 256, 512)
        TOP_K = 1
        B, S = (1, 256)
        key = jax.random.key(seed)
        ks = jax.random.split(key, 7)
        std = 0.02
        return {'hidden_states': jax.random.normal(ks[0], (B, S, H), dtype=jnp.float32), 'router_w': jax.random.normal(ks[1], (E, H), dtype=jnp.float32) * std, 'gate_up_proj': jax.random.normal(ks[2], (E, H, 2 * I), dtype=jnp.float32) * std, 'down_proj': jax.random.normal(ks[3], (E, I, H), dtype=jnp.float32) * std, 'shared_gate_w': jax.random.normal(ks[4], (H, I), dtype=jnp.float32) * std, 'shared_up_w': jax.random.normal(ks[5], (H, I), dtype=jnp.float32) * std, 'shared_down_w': jax.random.normal(ks[6], (I, H), dtype=jnp.float32) * std}
    _L0_ffn_in = _L0_ffn_setup()
    _d = {'L0_attn_x': _L0_attn_in['x'], 'L0_attn_w_q': _L0_attn_in['w_q'], 'L0_attn_b_q': _L0_attn_in['b_q'], 'L0_attn_w_k': _L0_attn_in['w_k'], 'L0_attn_b_k': _L0_attn_in['b_k'], 'L0_attn_w_v': _L0_attn_in['w_v'], 'L0_attn_b_v': _L0_attn_in['b_v'], 'L0_attn_w_g': _L0_attn_in['w_g'], 'L0_attn_b_g': _L0_attn_in['b_g'], 'L0_attn_w_o': _L0_attn_in['w_o'], 'L0_attn_b_o': _L0_attn_in['b_o'], 'L0_attn_gn_weight': _L0_attn_in['gn_weight'], 'L0_attn_gn_bias': _L0_attn_in['gn_bias'], 'L0_ffn_router_w': _L0_ffn_in['router_w'], 'L0_ffn_gate_up_proj': _L0_ffn_in['gate_up_proj'], 'L0_ffn_down_proj': _L0_ffn_in['down_proj'], 'L0_ffn_shared_gate_w': _L0_ffn_in['shared_gate_w'], 'L0_ffn_shared_up_w': _L0_ffn_in['shared_up_w'], 'L0_ffn_shared_down_w': _L0_ffn_in['shared_down_w']}
    _x0 = _d['L0_attn_x']
    _d['L0_attn_x'] = jax.random.normal(jax.random.fold_in(jax.random.key(seed), 1), (16, 256, 256), dtype=_x0.dtype)
    del _x0
    return _d

def reference(L0_attn_x, L0_attn_w_q, L0_attn_b_q, L0_attn_w_k, L0_attn_b_k, L0_attn_w_v, L0_attn_b_v, L0_attn_w_g, L0_attn_b_g, L0_attn_w_o, L0_attn_b_o, L0_attn_gn_weight, L0_attn_gn_bias, L0_ffn_router_w, L0_ffn_gate_up_proj, L0_ffn_down_proj, L0_ffn_shared_gate_w, L0_ffn_shared_up_w, L0_ffn_shared_down_w):

    def _L0_attn_ref(x, w_q, b_q, w_k, b_k, w_v, b_v, w_g, b_g, w_o, b_o, gn_weight, gn_bias):
        import jax, jax.numpy as jnp
        import numpy as np
        HIDDEN = 256
        HEADS = 8
        HEAD_DIM = HIDDEN // HEADS
        EPS = 1e-05

        def _position_thetas(head_dim, scale=10000.0):
            x = jnp.linspace(0.0, 1.0, head_dim // 2)
            thetas = 1.0 / scale ** x
            return jnp.repeat(thetas, 2)

        def _decay_gammas(num_heads):
            x = jnp.linspace(np.log(1 / 32), np.log(1 / 64), num_heads)
            return 1.0 - jnp.exp(x)

        def _decay_mask(n, s, gammas):
            qpos = jnp.arange(n, dtype=jnp.float32)[:, None]
            kpos = jnp.arange(s, dtype=jnp.float32)[None, :]
            dist = qpos - kpos
            dist = jnp.where(dist < 0, jnp.inf, dist)
            return gammas[:, None, None] ** dist[None]

        def _multiply_by_i(x):
            xe = x[..., ::2]
            xo = x[..., 1::2]
            return jnp.stack((-xo, xe), axis=-1).reshape(x.shape)

        def _theta_shift(x, sin, cos):
            return x * cos + _multiply_by_i(x) * sin
        B, N, _ = x.shape
        q = x @ w_q + b_q
        k = x @ w_k + b_k
        v = x @ w_v + b_v
        g = x @ w_g + b_g

        def split(t):
            return t.reshape(B, N, HEADS, HEAD_DIM).transpose(0, 2, 1, 3)
        q, k, v = (split(q), split(k), split(v))
        thetas = _position_thetas(HEAD_DIM)
        pos = jnp.arange(N, dtype=jnp.float32)[:, None] * thetas[None, :]
        sin = jnp.sin(pos)[None, None]
        cos = jnp.cos(pos)[None, None]
        q = _theta_shift(q, sin, cos)
        k = _theta_shift(k, sin, cos)
        gammas = _decay_gammas(HEADS)
        mask = _decay_mask(N, N, gammas)
        scale = HEAD_DIM ** 0.5
        sim = jnp.einsum('bhnd,bhsd->bhns', q, k / scale) * mask[None]
        ret = jnp.einsum('bhns,bhsd->bhnd', sim, v)
        ret = ret.transpose(0, 2, 1, 3).reshape(B, N, HIDDEN)
        r = ret.reshape(B, N, HEADS, HEAD_DIM)
        mean = r.mean(axis=-1, keepdims=True)
        var = r.var(axis=-1, keepdims=True)
        r = (r - mean) / jnp.sqrt(var + EPS)
        ret = r.reshape(B, N, HIDDEN) * gn_weight + gn_bias
        gate = jax.nn.silu(g) * ret
        return gate @ w_o + b_o

    def _L0_ffn_ref(hidden_states, router_w, gate_up_proj, down_proj, shared_gate_w, shared_up_w, shared_down_w):
        import jax, jax.numpy as jnp
        import numpy as np
        E, H, I = (8, 256, 512)
        TOP_K = 1
        B, S = (1, 256)
        orig_shape = hidden_states.shape
        x = hidden_states.reshape(-1, H)
        T = x.shape[0]
        logits = x @ router_w.T
        top_vals, top_idx = jax.lax.top_k(logits, TOP_K)
        scores = jnp.full_like(logits, -jnp.inf)
        scores = scores.at[jnp.arange(T)[:, None], top_idx].set(top_vals)
        scores = jax.nn.sigmoid(scores.astype(jnp.float32)).astype(logits.dtype)
        xr = x[None, :, :] * scores.T[:, :, None]
        gate_up = jnp.einsum('eth,ehf->etf', xr, gate_up_proj)
        gate, up = jnp.split(gate_up, 2, axis=-1)
        routed = jnp.einsum('etf,efh->eth', up * jax.nn.silu(gate), down_proj)
        routed_sum = routed.sum(axis=0)
        shared = jax.nn.silu(x @ shared_gate_w) * (x @ shared_up_w) @ shared_down_w
        return (shared + routed_sum).reshape(orig_shape)
    x = L0_attn_x
    x = _layernorm(x + _L0_attn_ref(x, L0_attn_w_q, L0_attn_b_q, L0_attn_w_k, L0_attn_b_k, L0_attn_w_v, L0_attn_b_v, L0_attn_w_g, L0_attn_b_g, L0_attn_w_o, L0_attn_b_o, L0_attn_gn_weight, L0_attn_gn_bias), axis=-1)
    x = _layernorm(x + _L0_ffn_ref(x, L0_ffn_router_w, L0_ffn_gate_up_proj, L0_ffn_down_proj, L0_ffn_shared_gate_w, L0_ffn_shared_up_w, L0_ffn_shared_down_w), axis=-1)
    return x

_drawn_inputs = setup_inputs


def setup_inputs(seed=0):
    import zlib

    import numpy as np

    out = dict(_drawn_inputs(seed))
    spreads = {'L0_attn_b_q': (0.0, 0.409),
     'L0_attn_b_k': (0.0, 0.1),
     'L0_attn_b_v': (0.0, 0.1),
     'L0_attn_b_g': (0.0, 0.441),
     'L0_attn_b_o': (0.0, 0.1),
     'L0_attn_gn_weight': (1.0, 0.6),
     'L0_attn_gn_bias': (0.0, 0.8)}
    factors = {'L0_ffn_router_w': 6.642,
     'L0_ffn_gate_up_proj': 6.261,
     'L0_ffn_down_proj': 6.254,
     'L0_ffn_shared_gate_w': 8.0,
     'L0_ffn_shared_up_w': 8.0,
     'L0_ffn_shared_down_w': 8.0}
    for name, (base, spread) in spreads.items():
        noise = np.random.default_rng([zlib.crc32(name.encode()), seed]).standard_normal(out[name].shape)
        drawn = base * np.exp(spread * noise) if base else spread * noise
        out[name] = jnp.asarray(drawn.astype(out[name].dtype))
    for name, factor in factors.items():
        out[name] = (out[name] * factor).astype(out[name].dtype)
    return out
```

```python
from contextlib import ExitStack

import numpy as np
import concourse.bass as bass
from concourse import mybir

F32 = mybir.dt.float32
F32R = mybir.dt.float32r
I32 = mybir.dt.int32
ALU = mybir.AluOpType
ACT = mybir.ActivationFunctionType
X = mybir.AxisListType.X

P = 128
SEQS, SEQ, D = 16, 256, 256
HEADS = 8
HD = D // HEADS
HALF = HD // 2
PAIRS = SEQS // 2
TOK = 2 * SEQ
TILES = TOK // P
NTILE = SEQS * SEQ // P
KT = D // P
EXPERTS, FF = 8, 512
FT = FF // P
SLOTS = NTILE + EXPERTS - 1
XROW = D + 1
EPS = 1e-5
N_IN = 14
PASSES = ((0, 0), (0, 1), (1, 0))


def build(nc, x, w_q, b_q, w_k, b_k, w_v, b_v, w_g, b_g, w_o, b_o, gn_w, gn_b, router_w,
          gate_up, down, sh_gate, sh_up, sh_down, rotation, squares, out):
    ctx = ExitStack()
    with ctx:
        def scratch(name, shape, dt=F32):
            return nc.dram_tensor(name, shape, dt, kind="Internal").ap()

        def f32(ap):
            return ap.bitcast(F32)

        def tensors(stack):
            return lambda name, shape, dt=F32: stack.enter_context(nc.sbuf_tensor(name, shape, dt))

        rot_d = scratch("rot_d", [2, 2, 2, P, TOK])
        x1_d = scratch("x1_d", [SEQS * SEQ, D])
        zs_d = scratch("zs_d", [SEQS * SEQ, D])
        slot_x = scratch("slot_x", [SLOTS * P, XROW])
        slot_y = scratch("slot_y", [SLOTS * P, D])

        sb = tensors(ctx)
        ident = sb("ident", [P, P])
        causal = sb("causal", [P, P])
        before = sb("before", [P, P])
        ones = sb("ones", [P, P])
        priority = sb("priority", [P, EXPERTS])
        slot_no = sb("slot_no", [P, SLOTS])
        minus_half = sb("minus_half", [P, TILES * HEADS])
        rot = sb("rot", [P, 4, SEQ])
        bias_qk = sb("bias_qk", [P, 2, 2])
        bias_vg = sb("bias_vg", [P, 2 * D])
        bias_o = sb("bias_o", [P, D])
        norm_w = sb("norm_w", [P, D])
        norm_b = sb("norm_b", [P, D])
        wqk = sb("wqk", [P, 2, 2, KT, D], F32R)
        wvg = sb("wvg", [P, 2, KT, 2 * D], F32R)
        wo = sb("wo", [P, 2, KT, D], F32R)
        wsgu = sb("wsgu", [P, 2, 2, KT, FF], F32R)
        wsd = sb("wsd", [P, 2, FT, D], F32R)
        wr = sb("wr", [P, 2, KT, EXPERTS], F32R)
        logits = sb("logits", [P, NTILE * EXPERTS])

        first = ExitStack()
        with first:
            sb = tensors(first)
            with ExitStack() as early:
                e_sb = tensors(early)
                raw_qk = e_sb("raw_qk", [P, 2, KT, D])
                raw_vg = e_sb("raw_vg", [P, KT, 2 * D])
                raw_o = e_sb("raw_o", [P, KT, D])
                raw_gu = e_sb("raw_gu", [P, 2, KT, FF])
                raw_d = e_sb("raw_d", [P, FT, D])
                raw_r = e_sb("raw_r", [EXPERTS, D])
                mean_v = e_sb("mean_v", [P, KT, HEADS])
                mean_b = e_sb("mean_b", [P, HEADS])
            hT = sb("hT", [P, 2, FT, TOK], F32R)
            s_act = sb("s_act", [P, 2, TOK])
            h = sb("h", [P, 2, TOK])
            x1 = sb("x1", [P, TILES, D])
            x_in = sb("x_in", [P, TILES, D])
            x_res = sb("x_res", [P, TILES, D])
            xT = sb("xT", [P, 2, KT, TOK], F32R)
            prod = sb("prod", [P, 2, 4, TOK])
            split = sb("split", [P, 2, 2, TOK], F32R)
            stack = [sb("stack_q", [96, HEADS, TOK], F32R),
                     sb("stack_k", [96, HEADS, TOK], F32R)]
            vg = sb("vg", [P, TILES, 2 * D])
            gate = sb("gate", [P, TILES, D])
            sims = sb("sims", [P, 4, 2, 3, P])
            retT = sb("retT", [P, 2, TOK])
            var = sb("var", [P, TILES * HEADS])
            var_e = sb("var_e", [P, TILES * HEADS])
            rstd = sb("rstd", [P, TILES * HEADS])
            y = sb("y", [P, TILES, D])
            yT = sb("yT", [P, 2, KT, TOK], F32R)
            stats = sb("stats", [P, TILES, 6])
            mv = sb("mv", [P, TILES, 2])
            ln_e = sb("ln_e", [P, TILES])
            ln_r = sb("ln_r", [P, TILES])
            x1T = sb("x1T", [P, 2, KT, TOK], F32R)
            lgT = sb("lgT", [EXPERTS, TOK])
        second = ExitStack()
        with second:
            sb = tensors(second)
            w_gu = sb("w_gu", [P, EXPERTS, KT, 2 * FF])
            w_dn = sb("w_dn", [P, EXPERTS, FT, D])
            xs = sb("xs", [P, 2, XROW])
            xsT = sb("xsT", [P, KT, P])
            e_act = sb("e_act", [P, FF])
            eh = sb("eh", [P, FF])
            ehT = sb("ehT", [P, FT, P])
            ys = sb("ys", [P, 2, D])
            x1s = sb("x1s", [P, TILES, XROW])
            idx = sb("idx", [P, TILES], I32)
            top = sb("top", [P, NTILE])
            score = sb("score", [P, NTILE])
            hot = sb("hot", [P, NTILE, EXPERTS])
            ranked = sb("ranked", [P, NTILE, EXPERTS])
            first_of = sb("first_of", [P, NTILE])
            total = sb("total", [P, EXPERTS, NTILE])
            upto = sb("upto", [P, EXPERTS, NTILE])
            spot = sb("spot", [P, NTILE, EXPERTS])
            nil = sb("nil", [P, EXPERTS * NTILE])
            count = sb("count", [P, EXPERTS])
            count_up = sb("count_up", [P, EXPERTS], I32)
            slots_i = sb("slots_i", [P, EXPERTS], I32)
            slots_f = sb("slots_f", [P, EXPERTS])
            slot_end = sb("slot_end", [P, EXPERTS])
            count_end = sb("count_end", [P, EXPERTS])
            shift = sb("shift", [P, EXPERTS])
            place = sb("place", [P, NTILE])
            place_i = sb("place_i", [P, NTILE], I32)
            passed = sb("passed", [P, SLOTS, EXPERTS])
            slot_e = sb("slot_e", [P, SLOTS])
            slot_ei = sb("slot_ei", [P, SLOTS], I32)
            zf = sb("zf", [P, TILES, D])
            yf = sb("yf", [P, TILES, D])
            of = sb("of", [P, TILES, D])
            st2 = sb("st2", [P, TILES, 6])
            mv2 = sb("mv2", [P, TILES, 2])
            ln2_e = sb("ln2_e", [P, TILES])
            ln2_r = sb("ln2_r", [P, TILES])

        duo = [ctx.enter_context(nc.psum_tensor(f"duo{i}", [P, 2, 512], F32)) for i in range(4)]

        def new(name):
            return ctx.enter_context(nc.semaphore(name))

        class sig:
            apart = new("apart")
            c_in = new("c_in")
            raw_in = new("raw_in")
            wrT_ps = new("wrT_ps")
            w_hi = new("w_hi")
            w_lo = new("w_lo")
            center = new("center")
            xin = new("xin")
            xres_in = new("xres_in")
            xT_ps = new("xT_ps")
            xT_hi = new("xT_hi")
            xT_lo = new("xT_lo")
            qk_ps = new("qk_ps")
            prod_ok = new("prod_ok")
            turned_ok = new("turned_ok")
            split_hi = new("split_hi")
            split_lo = new("split_lo")
            rot_out = new("rot_out")
            stack_in = new("stack_in")
            vg_ps = new("vg_ps")
            vg_ok = new("vg_ok")
            gate_ok = new("gate_ok")
            s_ps = new("s_ps")
            s_off = new("s_off")
            s_diag = new("s_diag")
            av_ps = new("av_ps")
            retT_ok = new("retT_ok")
            rn_ps = new("rn_ps")
            sq_ok = new("sq_ok")
            var_ok = new("var_ok")
            eps_ok = new("eps_ok")
            rstd_ok = new("rstd_ok")
            rn_ok = new("rn_ok")
            y_w = new("y_w")
            y_b = new("y_b")
            y_ok = new("y_ok")
            yT_ps = new("yT_ps")
            yT_hi = new("yT_hi")
            yT_lo = new("yT_lo")
            xb_ok = new("xb_ok")
            o_ps = new("o_ps")
            z_ok = new("z_ok")
            st_ok = new("st_ok")
            mv_ok = new("mv_ok")
            lne_ok = new("lne_ok")
            lnr_ok = new("lnr_ok")
            x1_ok = new("x1_ok")
            x1_out = new("x1_out")
            x1T_ps = new("x1T_ps")
            x1T_hi = new("x1T_hi")
            x1T_lo = new("x1T_lo")
            gu_ps = new("gu_ps")
            sact_ok = new("sact_ok")
            h_ok = new("h_ok")
            h_hi = new("h_hi")
            h_lo = new("h_lo")
            lgT_ps = new("lgT_ps")
            lgT_ok = new("lgT_ok")
            lg_ps = new("lg_ps")
            lg_ok = new("lg_ok")
            dn_ps = new("dn_ps")
            zs_ok = new("zs_ok")
            zs_out = new("zs_out")
            zero_ok = new("zero_ok")
            zfill = new("zfill")
            chain = new("chain")
            hot_ok = new("hot_ok")
            nil_ok = new("nil_ok")
            place_ok = new("place_ok")
            slot_e_ok = new("slot_e_ok")
            rank_ps = new("rank_ps")
            score_ok = new("score_ok")
            ew_in = new("ew_in")
            x1s_in = new("x1s_in")
            x1s_sc = new("x1s_sc")
            idx_ok = new("idx_ok")
            scat = new("scat")
            xsT_ps = new("xsT_ps")
            xsT_ok = new("xsT_ok")
            eg_ps = new("eg_ps")
            e_act_ok = new("e_act_ok")
            eh_ok = new("eh_ok")
            ehT_ps = new("ehT_ps")
            ehT_ok = new("ehT_ok")
            ed_ps = new("ed_ps")
            ys_ok = new("ys_ok")
            zf_in = new("zf_in")
            yf_in = new("yf_in")
            sum_ok = new("sum_ok")
            st2_ok = new("st2_ok")
            mv2_ok = new("mv2_ok")
            lne2_ok = new("lne2_ok")
            lnr2_ok = new("lnr2_ok")
            of_ok = new("of_ok")
            out_done = new("out_done")
            xs_in = [new("xs_in0"), new("xs_in1")]
            ys_out = [new("ys_out0"), new("ys_out1")]

        def at(value):
            return max(value, 0) if isinstance(value, int) else value

        def apart(eng):
            eng.sem_inc(sig.apart, 1)

        def has(i):
            return not isinstance(i, int) or 0 <= i < PAIRS

        def pipeline(eng, step):
            for t in range(3):
                step(t)
            with eng.Fori(3, PAIRS - 1) as t:
                step(t)
            for t in range(PAIRS - 1, PAIRS + 2):
                step(t)

        def slot_pipeline(eng, step):
            for s in range(4):
                step(s, s % 2, s // 2)
            with eng.Fori(2, SLOTS // 2) as u:
                step(2 * u, 0, u)
                step(2 * u + 1, 1, u)
            for s in range(SLOTS - 1, SLOTS + 1):
                step(s, s % 2, s // 2)

        def groups(eng, body):
            body(0)
            with eng.Fori(1, PAIRS) as t:
                body(t)

        def is_slot(s):
            return not isinstance(s, int) or 0 <= s < SLOTS

        def tile_rows(dram, t, q):
            v = dram.rearrange("(t q p) d -> t p q d", q=q, p=P)
            return v[t] if isinstance(t, int) else v[bass.ds(t, 1)].rearrange("a p q d -> (a p) q d")

        def one(t):
            return slice(t, t + 1) if isinstance(t, int) else bass.ds(t, 1)

        def spread(vector, n=D):
            return bass.AP(vector.tensor, 0, [[0, P], [1, n]])

        def over(ap, n):
            return bass.AP(ap.tensor, ap.offset, [list(ap.ap[0]), [0, n], *[list(a) for a in ap.ap[1:]]])

        def each(ap, n):
            return bass.AP(ap.tensor, ap.offset, [*[list(a) for a in ap.ap], [0, n]])

        block = ctx.enter_context(nc.Block())

        @block.sync
        def _(sp):
            sp.dma_start(ident[:, :], squares[:, 0:P]).then_inc(sig.c_in, 16)
            sp.dma_start(x_in[:, :, :], tile_rows(x, 0, TILES)).then_inc(sig.xin, 16)
            sp.dma_start(causal[:, :], squares[:, P:2 * P]).then_inc(sig.c_in, 16)
            sp.dma_start(before[:, :], squares[:, 2 * P:3 * P]).then_inc(sig.c_in, 16)
            sp.dma_start(ones[:, :], squares[:, 3 * P:4 * P]).then_inc(sig.c_in, 16)
            sp.dma_start(priority[:, :], squares[:, 4 * P:4 * P + EXPERTS]).then_inc(sig.c_in, 16)
            sp.dma_start(slot_no[:, :], squares[:, 4 * P + EXPERTS:4 * P + EXPERTS + SLOTS]).then_inc(sig.c_in, 16)
            sp.dma_start(rot[:, :, :], rotation.rearrange("p (f n) -> p f n", f=4)).then_inc(sig.c_in, 16)
            sp.dma_start(bias_qk[:, 0, :], b_q.rearrange("(p two) -> p two", two=2)).then_inc(sig.c_in, 16)
            sp.dma_start(bias_qk[:, 1, :], b_k.rearrange("(p two) -> p two", two=2)).then_inc(sig.c_in, 16)
            sp.dma_start(bias_vg[:, 0:D], spread(b_v)).then_inc(sig.c_in, 16)
            sp.dma_start(bias_vg[:, D:2 * D], spread(b_g)).then_inc(sig.c_in, 16)
            sp.dma_start(bias_o[:, :], spread(b_o)).then_inc(sig.c_in, 16)
            sp.dma_start(norm_w[:, :], spread(gn_w)).then_inc(sig.c_in, 16)
            sp.dma_start(norm_b[:, :], spread(gn_b)).then_inc(sig.c_in, 16)

            def step(t):
                if has(t + 1):
                    sp.wait_ge(sig.xT_ps, at(t + 1))
                    sp.dma_start(x_in[:, :, :], tile_rows(x, t + 1, TILES)).then_inc(sig.xin, 16)
                if has(t - 1):
                    sp.wait_ge(sig.x1_ok, at(TILES * (t - 1)))
                    sp.dma_start(x_res[:, :, :], tile_rows(x, t - 1, TILES)).then_inc(sig.xres_in, 16)
                if has(t):
                    for side in range(2):
                        sp.wait_ge(sig.split_hi, at(4 * t + 2 * side + 2))
                        apart(sp)
                        sp.wait_ge(sig.split_lo, at(4 * t + 2 * side + 2))
                        apart(sp)
                        sp.wait_ge(sig.stack_in, at(192 * t))
                        for part in range(2):
                            sp.dma_start(rot_d[side, part].rearrange("e p n -> p e n"),
                                         f32(split[:, part, :, :])).then_inc(sig.rot_out, 16)
                        sp.wait_ge(sig.rot_out, at(64 * t + 32 * side + 32))
                        apart(sp)
                        sp.wait_ge(sig.s_ps, at(8 * t))
                        for group, part in enumerate(((0, 1, 0), (0, 0, 1))[side]):
                            for e in range(2):
                                lo = HD * group + HALF * e
                                sp.dma_start(f32(stack[side][lo:lo + HALF, :, :]),
                                             rot_d[side, part, e].rearrange("(h i) n -> i h n", i=HALF))\
                                    .then_inc(sig.stack_in, 16)
                if has(t - 2):
                    sp.wait_ge(sig.zs_ok, at(2 * (t - 1)))
                    sp.dma_start(tile_rows(zs_d, t - 2, TILES), x1[:, :, :]).then_inc(sig.zs_out, 16)
                if has(t - 1):
                    sp.wait_ge(sig.x1_ok, at(TILES * t))
                    sp.dma_start(tile_rows(x1_d, t - 1, TILES), x1[:, :, :]).then_inc(sig.x1_out, 16)

            pipeline(sp, step)

            sp.wait_ge(sig.zs_out, at(16 * PAIRS))
            sp.wait_ge(sig.x1_out, at(16 * PAIRS))
            sp.wait_ge(sig.lg_ok, at(PAIRS))
            sp.wait_ge(sig.dn_ps, at(2 * PAIRS))
            for e in range(EXPERTS):
                sp.dma_start(w_gu[:, e, :, :], gate_up[e].rearrange("(k p) n -> p k n", p=P)).then_inc(sig.ew_in, 16)
                sp.dma_start(w_dn[:, e, :, :], down[e].rearrange("(k p) n -> p k n", p=P)).then_inc(sig.ew_in, 16)

            def rows_again(t):
                sp.wait_ge(sig.scat, at(16 * TILES * t))
                sp.dma_start(x1s[:, :, 0:D], tile_rows(x1_d, t, TILES)).then_inc(sig.x1s_in, 16)

            groups(sp, rows_again)

            sp.wait_ge(sig.scat, at(16 * NTILE))

            def slot_in(s, parity):
                if is_slot(s):
                    sp.wait_ge(sig.eh_ok, at(s - 1))
                    sp.wait_ge(sig.xsT_ps, at(s - 1))
                    sp.dma_start(xs[:, parity, :], slot_x.rearrange("(s p) d -> s p d", p=P)[one(s)]
                         .rearrange("a p d -> (a p) d")).then_inc(sig.xs_in[parity], 16)

            def slot_step(s, parity, u):
                slot_in(s + 1, 1 - parity)
                if is_slot(s - 1):
                    sp.wait_ge(sig.ys_ok, at(s))
                    sp.dma_start(slot_y.rearrange("(s p) d -> s p d", p=P)[one(s - 1)]
                                 .rearrange("a p d -> (a p) d"), ys[:, 1 - parity, :])\
                        .then_inc(sig.ys_out[1 - parity], 16)

            slot_in(0, 0)
            slot_pipeline(sp, slot_step)

            def finish(t):
                sp.wait_ge(sig.sum_ok, at(t))
                sp.dma_start(zf[:, :, :], tile_rows(zs_d, t, TILES)).then_inc(sig.zf_in, 16)
                sp.wait_ge(sig.of_ok, at(TILES * (t + 1)))
                sp.dma_start(tile_rows(out, t, TILES), of[:, :, :]).then_inc(sig.out_done, 16)

            groups(sp, finish)
            sp.wait_ge(sig.out_done, at(16 * PAIRS))

        @block.scalar
        def _(act):
            def k_rows(w):
                return w.rearrange("(k p) n -> p k n", p=P)

            act.dma_start(raw_qk[:, 0, :, :], k_rows(w_q)).then_inc(sig.raw_in, 16)
            act.dma_start(raw_qk[:, 1, :, :], k_rows(w_k)).then_inc(sig.raw_in, 16)
            act.dma_start(raw_vg[:, :, 0:D], k_rows(w_v)).then_inc(sig.raw_in, 16)
            act.dma_start(raw_vg[:, :, D:2 * D], k_rows(w_g)).then_inc(sig.raw_in, 16)
            act.dma_start(raw_o[:, :, :], k_rows(w_o)).then_inc(sig.raw_in, 16)
            act.dma_start(raw_gu[:, 0, :, :], k_rows(sh_gate)).then_inc(sig.raw_in, 16)
            act.dma_start(raw_gu[:, 1, :, :], k_rows(sh_up)).then_inc(sig.raw_in, 16)
            act.dma_start(raw_d[:, :, :], k_rows(sh_down)).then_inc(sig.raw_in, 16)
            act.dma_start(raw_r[:, :], router_w).then_inc(sig.raw_in, 16)

            def x_hi(t):
                for k in range(KT):
                    act.wait_ge(sig.xT_ps, at(t + 1))
                    act.wait_ge(sig.vg_ps, at(TILES * t))
                    nc.scalar.activation(xT[:, 0, k, :], duo[3][:, k, :], ACT.Copy)\
                        .then_inc(sig.xT_hi, 1)

            x_hi(0)
            act.wait_ge(sig.raw_in, at(16 * 9))
            nc.scalar.activation(wqk[:, :, 0, :, :], raw_qk[:, :, :, :], ACT.Copy)\
                .then_inc(sig.w_hi, 1)
            act.wait_ge(sig.center, at(5))
            nc.scalar.activation(wvg[:, 0, :, :], raw_vg[:, :, :], ACT.Copy)\
                .then_inc(sig.w_hi, 1)
            nc.scalar.activation(wo[:, 0, :, :], raw_o[:, :, :], ACT.Copy)\
                .then_inc(sig.w_hi, 1)
            nc.scalar.activation(wsgu[:, :, 0, :, :], raw_gu[:, :, :, :], ACT.Copy)\
                .then_inc(sig.w_hi, 1)
            nc.scalar.activation(wsd[:, 0, :, :], raw_d[:, :, :], ACT.Copy)\
                .then_inc(sig.w_hi, 1)
            act.wait_ge(sig.wrT_ps, at(1))
            nc.scalar.activation(wr[:, 0, :, :], duo[2][:, 0, 0:KT * EXPERTS].rearrange("p (k e) -> p k e", k=KT), ACT.Copy)\
                .then_inc(sig.w_hi, 1)

            def step(t):
                if has(t - 1):
                    p = t - 1
                    for j in range(8):
                        act.wait_ge(sig.s_ps, at(8 * p + j + 1))
                        act.wait_ge(sig.av_ps, at(4 * p + j // 2 - 1))
                        nc.scalar.activation(sims[:, j % 4, :, 1, :], duo[j % 2][:, :, P:2 * P], ACT.Copy)\
                            .then_inc(sig.s_off, 1)
                    for g in range(2):
                        act.wait_ge(sig.av_ps, at(4 * p + 3 + g))
                        act.wait_ge(sig.var_ok, at(2 * p))
                        nc.scalar.activation(retT[:, g, :], duo[2][:, g, :], ACT.Copy)\
                            .then_inc(sig.retT_ok, 1)
                if has(t):
                    split_hi(t, 0)
                if has(t - 1):
                    for i in range(2):
                        act.wait_ge(sig.rn_ps, at(t))
                        nc.scalar.activation(retT[:, i, :], duo[3][:, i, :], ACT.Square, scale=float(HD) ** -0.5)\
                            .then_inc(sig.sq_ok, 1)
                if has(t):
                    split_hi(t, 1)
                if has(t - 2):
                    p = t - 2
                    for k in range(KT):
                        act.wait_ge(sig.x1T_ps, at(p + 1))
                        act.wait_ge(sig.gu_ps, at(2 * FT * p))
                        act.wait_ge(sig.lgT_ps, at(p))
                        nc.scalar.activation(x1T[:, 0, k, :], duo[2][:, k, :], ACT.Copy)\
                            .then_inc(sig.x1T_hi, 1)
                    for j in range(FT):
                        act.wait_ge(sig.gu_ps, at(2 * FT * p + 2 * j + 1))
                        act.wait_ge(sig.h_ok, at(FT * p + j - 1))
                        nc.scalar.activation(s_act[:, j % 2, :], duo[j % 2][:, 0, :], ACT.Silu)\
                            .then_inc(sig.sact_ok, 1)
                        if j:
                            h_hi(p, j - 1)
                    h_hi(p, FT - 1)
                    act.wait_ge(sig.lgT_ps, at(p + 1))
                    act.wait_ge(sig.lg_ps, at(p))
                    nc.scalar.activation(lgT[:, :], duo[2][0:EXPERTS, 0, :], ACT.Copy)\
                        .then_inc(sig.lgT_ok, 1)
                if has(t - 1):
                    p = t - 1
                    for k in range(KT):
                        act.wait_ge(sig.yT_ps, at(p + 1))
                        act.wait_ge(sig.o_ps, at(2 * p))
                        nc.scalar.activation(yT[:, 0, k, :], duo[3][:, k, :], ACT.Copy)\
                            .then_inc(sig.yT_hi, 1)
                if has(t):
                    for q in range(TILES):
                        act.wait_ge(sig.vg_ok, at(TILES * t + q + 1))
                        act.wait_ge(sig.y_ok, at(t))
                        nc.scalar.activation(gate[:, q, :], vg[:, q, D:2 * D], ACT.Silu)\
                            .then_inc(sig.gate_ok, 1)
                if has(t + 1):
                    x_hi(t + 1)

            def split_hi(t, side):
                for e in range(2):
                    act.wait_ge(sig.turned_ok, at(4 * t + 2 * side + e + 1))
                    act.wait_ge(sig.rot_out, at(64 * t + 32 * side))
                    nc.scalar.activation(split[:, 0, e, :], prod[:, side, 3 * e, :], ACT.Copy)\
                        .then_inc(sig.split_hi, 1)

            def h_hi(p, j):
                act.wait_ge(sig.h_ok, at(FT * p + j + 1))
                act.wait_ge(sig.dn_ps, at(2 * p))
                nc.scalar.activation(hT[:, 0, j, :], h[:, j % 2, :], ACT.Copy)\
                    .then_inc(sig.h_hi, 1)

            pipeline(act, step)

            act.wait_ge(sig.chain, at(1))
            nc.scalar.activation(score[:, :], top[:, :], ACT.Sigmoid)\
                .then_inc(sig.score_ok, 1)

            def slot_step(s, parity, u):
                if is_slot(s - 1):
                    act.wait_ge(sig.ehT_ps, at(s))
                    act.wait_ge(sig.ed_ps, at(s - 1))
                    nc.scalar.activation(ehT[:, :, :], duo[2][:, 0, :].rearrange("p (f n) -> p f n", f=FT), ACT.Copy)\
                        .then_inc(sig.ehT_ok, 1)
                if is_slot(s):
                    act.wait_ge(sig.eg_ps, at(2 * s + 1))
                    act.wait_ge(sig.eh_ok, at(s))
                    nc.scalar.activation(e_act[:, :], duo[parity][:, 0, :], ACT.Silu, scale=xs[:, parity, D:XROW])\
                        .then_inc(sig.e_act_ok, 1)

            slot_pipeline(act, slot_step)

        @block.gpsimd
        def _(pool):
            nc.gpsimd.memset(minus_half[:, :], -0.5).then_inc(sig.zero_ok, 1)
            nc.gpsimd.memset(y[:, :, :], 0.0).then_inc(sig.zero_ok, 1)
            pool.wait_ge(sig.zero_ok, 2)
            flat = y[:, :, :].rearrange("p q d -> p (q d)")
            for s in range(0, SLOTS, 3):
                pool.dma_start(slot_x[s * P:(s + 3) * P, :].rearrange("(s p) d -> p s d", p=P),
                               flat[:, 0:3 * XROW].rearrange("p (s d) -> p s d", s=3)).then_inc(sig.zfill, 16)
            pool.wait_ge(sig.c_in, at(16 * N_IN))

            def step(t):
                if has(t):
                    for side in range(2):
                        pool.wait_ge(sig.prod_ok, at(4 * t + 2 * side + 2))
                        nc.gpsimd.tensor_tensor(prod[:, side, 0, :], prod[:, side, 0, :], prod[:, side, 2, :],
                                                ALU.subtract).then_inc(sig.turned_ok, 1)
                        nc.gpsimd.tensor_tensor(prod[:, side, 3, :], prod[:, side, 3, :], prod[:, side, 1, :],
                                                ALU.add).then_inc(sig.turned_ok, 1)
                if has(t - 1):
                    p = t - 1
                    pool.wait_ge(sig.var_ok, at(2 * p + 2))
                    apart(pool)
                    nc.gpsimd.tensor_scalar(var_e[:, :], var[:, :], EPS, None, ALU.add).then_inc(sig.eps_ok, 1)
                    pool.wait_ge(sig.eps_ok, at(p + 1))
                    pool.wait_ge(sig.rn_ok, at(2 * p))
                    nc.gpsimd.tensor_tensor(rstd[:, :], var_e[:, :], minus_half[:, :], ALU.pow).then_inc(sig.rstd_ok, 1)
                    pool.wait_ge(sig.xres_in, at(16 * (p + 1)))
                    nc.gpsimd.tensor_tensor(x_res[:, :, :], x_res[:, :, :], over(bias_o[:, :], TILES),
                                            ALU.add).then_inc(sig.xb_ok, 1)
                    pool.wait_ge(sig.rn_ok, at(2 * p + 2))
                    nc.gpsimd.tensor_tensor(y[:, :, :], y[:, :, :], over(norm_w[:, :], TILES), ALU.mult)\
                        .then_inc(sig.y_w, 1)
                    pool.wait_ge(sig.y_w, at(p + 1))
                    nc.gpsimd.tensor_tensor(y[:, :, :], y[:, :, :], over(norm_b[:, :], TILES), ALU.add)\
                        .then_inc(sig.y_b, 1)
                    pool.wait_ge(sig.y_b, at(p + 1))
                    pool.wait_ge(sig.gate_ok, at(TILES * (p + 1)))
                    nc.gpsimd.tensor_tensor(y[:, :, :], y[:, :, :], gate[:, :, :], ALU.mult).then_inc(sig.y_ok, 1)
                    pool.wait_ge(sig.mv_ok, at(TILES * (p + 1)))
                    apart(pool)
                    nc.gpsimd.tensor_scalar(ln_e[:, :], mv[:, :, 1], EPS, None, ALU.add).then_inc(sig.lne_ok, 1)
                    pool.wait_ge(sig.lne_ok, at(p + 1))
                    pool.wait_ge(sig.x1_ok, at(TILES * p))
                    nc.gpsimd.tensor_tensor(ln_r[:, :], ln_e[:, :], minus_half[:, 0:TILES], ALU.pow)\
                        .then_inc(sig.lnr_ok, 1)

            pipeline(pool, step)

            pool.wait_ge(sig.score_ok, at(1))
            pool.wait_ge(sig.place_ok, at(1))
            pool.wait_ge(sig.zfill, at(16 * (SLOTS // 3)))

            def scatter(t):
                pool.wait_ge(sig.scat, at(16 * TILES * t))
                if isinstance(t, int):
                    sl = slice(TILES * t, TILES * t + TILES)
                else:
                    sl = bass.ds(TILES * t, TILES)
                nc.gpsimd.tensor_copy(idx[:, :], place_i[:, sl]).then_inc(sig.idx_ok, 1)
                nc.gpsimd.tensor_copy(x1s[:, :, D], score[:, sl]).then_inc(sig.x1s_sc, 1)
                pool.wait_ge(sig.x1s_in, at(16 * (t + 1)))
                apart(pool)
                pool.wait_ge(sig.idx_ok, at(t + 1))
                apart(pool)
                pool.wait_ge(sig.x1s_sc, at(t + 1))
                apart(pool)
                for q in range(TILES):
                    pool.indirect_dma_start(slot_x, bass.IndirectOffsetOnAxis(ap=idx[:, q:q + 1], axis=0),
                                            x1s[:, q, :], None).then_inc(sig.scat, 16)
            groups(pool, scatter)

            pool.wait_ge(sig.ys_out[0], at(16 * ((SLOTS + 1) // 2)))
            pool.wait_ge(sig.ys_out[1], at(16 * (SLOTS // 2)))

            def gather(t):
                pool.wait_ge(sig.sum_ok, at(t))
                sl = slice(TILES * t, TILES * t + TILES) if isinstance(t, int) else bass.ds(TILES * t, TILES)
                nc.gpsimd.tensor_copy(idx[:, :], place_i[:, sl]).then_inc(sig.idx_ok, 1)
                pool.wait_ge(sig.idx_ok, at(PAIRS + t + 1))
                apart(pool)
                for q in range(TILES):
                    pool.indirect_dma_start(yf[:, q, :], None, slot_y,
                                            bass.IndirectOffsetOnAxis(ap=idx[:, q:q + 1], axis=0))\
                        .then_inc(sig.yf_in, 16)
                pool.wait_ge(sig.mv2_ok, at(TILES * (t + 1)))
                apart(pool)
                nc.gpsimd.tensor_scalar(ln2_e[:, :], mv2[:, :, 1], EPS, None, ALU.add).then_inc(sig.lne2_ok, 1)
                pool.wait_ge(sig.lne2_ok, at(t + 1))
                pool.wait_ge(sig.of_ok, at(TILES * t))
                nc.gpsimd.tensor_tensor(ln2_r[:, :], ln2_e[:, :], minus_half[:, 0:TILES], ALU.pow)\
                    .then_inc(sig.lnr2_ok, 1)
            groups(pool, gather)

        @block.vector
        def _(dve):
            def x_lo(t):
                for k in range(KT):
                    dve.wait_ge(sig.xT_hi, at(2 * t + k + 1))
                    dve.wait_ge(sig.vg_ps, at(TILES * t))
                    nc.vector.tensor_tensor(xT[:, 1, k, :], duo[3][:, k, :], f32(xT[:, 0, k, :]), ALU.subtract)\
                        .then_inc(sig.xT_lo, 1)

            x_lo(0)
            dve.wait_ge(sig.raw_in, at(16 * 9))
            dve.wait_ge(sig.c_in, at(16 * N_IN))
            v_heads = raw_vg[:, :, 0:D].rearrange("p k (h d) -> p k h d", d=HD)
            b_heads = bias_vg[:, 0:D].rearrange("p (h d) -> p h d", d=HD)
            nc.vector.tensor_reduce(mean_v[:, :, :], v_heads, X, ALU.add).then_inc(sig.center, 1)
            nc.vector.tensor_reduce(mean_b[:, :], b_heads, X, ALU.add).then_inc(sig.center, 1)
            dve.wait_ge(sig.center, at(2))
            for k in range(KT):
                nc.vector.scalar_tensor_tensor(out=v_heads[:, k], in0=each(mean_v[:, k, :], HD), scalar=-1.0 / HD,
                                               in1=v_heads[:, k], op0=ALU.mult, op1=ALU.add).then_inc(sig.center, 1)
            nc.vector.scalar_tensor_tensor(out=b_heads, in0=each(mean_b[:, :], HD), scalar=-1.0 / HD,
                                           in1=b_heads, op0=ALU.mult, op1=ALU.add).then_inc(sig.center, 1)
            for n, (lo_, raw_, hi_) in enumerate((
                    (wqk[:, :, 1, :, :], raw_qk[:, :, :, :], wqk[:, :, 0, :, :]),
                    (wvg[:, 1, :, :], raw_vg[:, :, :], wvg[:, 0, :, :]),
                    (wo[:, 1, :, :], raw_o[:, :, :], wo[:, 0, :, :]),
                    (wsgu[:, :, 1, :, :], raw_gu[:, :, :, :], wsgu[:, :, 0, :, :]),
                    (wsd[:, 1, :, :], raw_d[:, :, :], wsd[:, 0, :, :]),
                    (wr[:, 1, :, :], duo[2][:, 0, 0:KT * EXPERTS].rearrange("p (k e) -> p k e", k=KT), wr[:, 0, :, :]))):
                dve.wait_ge(sig.w_hi, at(n + 1))
                nc.vector.tensor_tensor(lo_, raw_, f32(hi_), ALU.subtract)\
                    .then_inc(sig.w_lo, 1)

            def step(t):
                if has(t - 1):
                    p = t - 1
                    for j in range(8):
                        dve.wait_ge(sig.s_off, at(8 * p + j + 1))
                        dve.wait_ge(sig.av_ps, at(4 * p + j // 2 - 1))
                        src = duo[j % 2][:, :, :].rearrange("p h (b q) -> p h b q", q=P)[:, :, 0::3, :]
                        mask = bass.AP(causal[:, :].tensor, 0, [[P, P], [0, 2], [0, 2], [1, P]])
                        nc.vector.tensor_tensor(sims[:, j % 4, :, 0::2, :], src, mask, ALU.mult)\
                            .then_inc(sig.s_diag, 1)
                if has(t):
                    for s in range(4):
                        side, e = s // 2, s % 2
                        dve.wait_ge(sig.qk_ps, at(4 * t + s + 1))
                        dve.wait_ge(sig.split_hi, at(4 * (t - 1) + 2 * side + 2))
                        dve.wait_ge(sig.split_lo, at(4 * (t - 1) + 2 * side + 2))
                        for f in range(2):
                            place_ = (0, 1)[f] if e == 0 else (3, 2)[f]
                            last = nc.vector.scalar_tensor_tensor(
                                out=prod[:, side, place_, :].rearrange("p (b n) -> p b n", b=2),
                                in0=duo[side][:, e, :].rearrange("p (b n) -> p b n", b=2),
                                scalar=bias_qk[:, side, e:e + 1],
                                in1=over(rot[:, 2 * side + f, :], 2), op0=ALU.add, op1=ALU.mult)
                        last.then_inc(sig.prod_ok, 1)
                    split_lo(t, 0)
                if has(t - 1):
                    p = t - 1
                    for i in range(2):
                        dve.wait_ge(sig.sq_ok, at(2 * p + i + 1))
                        dve.wait_ge(sig.eps_ok, at(p))
                        nc.vector.tensor_reduce(var[:, 16 * i:16 * i + 16],
                                                retT[:, i, :].rearrange("p (h d) -> p h d", d=HD), X, ALU.add)\
                            .then_inc(sig.var_ok, 1)
                if has(t):
                    split_lo(t, 1)
                    for q in range(TILES):
                        dve.wait_ge(sig.vg_ps, at(TILES * t + q + 1))
                        dve.wait_ge(sig.av_ps, at(4 * t))
                        dve.wait_ge(sig.gate_ok, at(TILES * t))
                        nc.vector.tensor_tensor(vg[:, q, :], duo[q // 2][:, q % 2, :], bias_vg[:, :], ALU.add)\
                            .then_inc(sig.vg_ok, 1)
                if has(t - 1):
                    p = t - 1
                    if isinstance(p, int) and p == 0:
                        dve.wait_ge(sig.zfill, at(16 * (SLOTS // 3)))
                    for i in range(2):
                        dve.wait_ge(sig.rstd_ok, at(p + 1))
                        dve.wait_ge(sig.yT_ps, at(p))
                        nc.vector.tensor_tensor(
                            y[:, 2 * i:2 * i + 2, :].rearrange("p q (h d) -> p (q h) d", d=HD),
                            duo[3][:, i, :].rearrange("p (h d) -> p h d", d=HD),
                            each(rstd[:, 16 * i:16 * i + 16], HD), ALU.mult)\
                            .then_inc(sig.rn_ok, 1)
                if has(t - 2):
                    p = t - 2
                    for k in range(KT):
                        dve.wait_ge(sig.x1T_hi, at(KT * p + k + 1))
                        nc.vector.tensor_tensor(x1T[:, 1, k, :], duo[2][:, k, :], f32(x1T[:, 0, k, :]), ALU.subtract)\
                            .then_inc(sig.x1T_lo, 1)
                    for j in range(FT):
                        dve.wait_ge(sig.gu_ps, at(2 * FT * p + 2 * j + 2))
                        dve.wait_ge(sig.sact_ok, at(FT * p + j + 1))
                        dve.wait_ge(sig.h_hi, at(FT * p + j - 1))
                        dve.wait_ge(sig.h_lo, at(FT * p + j - 1))
                        nc.vector.tensor_tensor(h[:, j % 2, :], duo[j % 2][:, 1, :], s_act[:, j % 2, :], ALU.mult)\
                            .then_inc(sig.h_ok, 1)
                        if j:
                            h_lo(p, j - 1)
                    h_lo(p, FT - 1)
                    dve.wait_ge(sig.lg_ps, at(p + 1))
                    w = TILES * EXPERTS
                    sl = slice(w * p, w * p + w) if isinstance(p, int) else bass.ds(w * p, w)
                    nc.vector.tensor_copy(logits[:, sl], duo[2][:, 1, 0:w]).then_inc(sig.lg_ok, 1)
                if has(t - 1):
                    p = t - 1
                    for k in range(KT):
                        dve.wait_ge(sig.yT_hi, at(KT * p + k + 1))
                        nc.vector.tensor_tensor(yT[:, 1, k, :], duo[3][:, k, :], f32(yT[:, 0, k, :]), ALU.subtract)\
                            .then_inc(sig.yT_lo, 1)
                if has(t - 2):
                    p = t - 2
                    for i in range(2):
                        dve.wait_ge(sig.dn_ps, at(2 * p + i + 1))
                        dve.wait_ge(sig.x1_out, at(16 * (p + 1)))
                        nc.vector.tensor_tensor(
                            x1[:, 2 * i:2 * i + 2, :], duo[2][:, i, :].rearrange("p (q n) -> p q n", q=2),
                            x1[:, 2 * i:2 * i + 2, :], ALU.add)\
                            .then_inc(sig.zs_ok, 1)
                if has(t - 1):
                    p = t - 1
                    for i in range(2):
                        dve.wait_ge(sig.o_ps, at(2 * p + i + 1))
                        dve.wait_ge(sig.xb_ok, at(p + 1))
                        nc.vector.tensor_tensor(
                            x_res[:, 2 * i:2 * i + 2, :], duo[0][:, i, :].rearrange("p (q n) -> p q n", q=2),
                            x_res[:, 2 * i:2 * i + 2, :], ALU.add)\
                            .then_inc(sig.z_ok, 1)
                    for q in range(TILES):
                        dve.wait_ge(sig.z_ok, at(2 * p + q // 2 + 1))
                        nc.vector.bn_stats(stats[:, q, :], x_res[:, q, :]).then_inc(sig.st_ok, 1)
                    for q in range(TILES):
                        dve.wait_ge(sig.st_ok, at(TILES * p + q + 1))
                        apart(dve)
                        dve.wait_ge(sig.lne_ok, at(p))
                        apart(dve)
                        nc.vector.bn_aggr(mv[:, q, :], stats[:, q, :]).then_inc(sig.mv_ok, 1)
                if has(t + 1):
                    x_lo(t + 1)
                if has(t - 1):
                    p = t - 1
                    for q in range(TILES):
                        dve.wait_ge(sig.lnr_ok, at(p + 1))
                        dve.wait_ge(sig.zs_out, at(16 * p))
                        nc.vector.tensor_scalar(x1[:, q, :], x_res[:, q, :], mv[:, q, 0:1], ln_r[:, q:q + 1],
                                                ALU.subtract, ALU.mult).then_inc(sig.x1_ok, 1)

            def split_lo(t, side):
                for e in range(2):
                    dve.wait_ge(sig.split_hi, at(4 * t + 2 * side + e + 1))
                    dve.wait_ge(sig.rot_out, at(64 * t + 32 * side))
                    nc.vector.tensor_tensor(
                        split[:, 1, e, :], prod[:, side, 3 * e, :], f32(split[:, 0, e, :]), ALU.subtract)\
                        .then_inc(sig.split_lo, 1)

            def h_lo(p, j):
                dve.wait_ge(sig.h_hi, at(FT * p + j + 1))
                nc.vector.tensor_tensor(hT[:, 1, j, :], h[:, j % 2, :], f32(hT[:, 0, j, :]), ALU.subtract)\
                    .then_inc(sig.h_lo, 1)

            pipeline(dve, step)

            dve.wait_ge(sig.lg_ok, at(PAIRS))
            dve.wait_ge(sig.zs_out, at(16 * PAIRS))
            dve.wait_ge(sig.x1_out, at(16 * PAIRS))
            dve.wait_ge(sig.dn_ps, at(2 * PAIRS))
            by_tile = logits[:, :].rearrange("p (t e) -> p t e", e=EXPERTS)
            nc.vector.tensor_reduce(top[:, :], by_tile, X, ALU.max)\
                .then_inc(sig.chain, 1)
            dve.wait_ge(sig.chain, 1)
            nc.vector.tensor_tensor(hot[:, :, :], by_tile, each(top[:, :], EXPERTS), ALU.is_equal)\
                .then_inc(sig.chain, 1)
            dve.wait_ge(sig.chain, 2)
            nc.vector.tensor_tensor(ranked[:, :, :], hot[:, :, :], over(priority[:, :], NTILE), ALU.mult)\
                .then_inc(sig.chain, 1)
            dve.wait_ge(sig.chain, 3)
            nc.vector.tensor_reduce(first_of[:, :], ranked[:, :, :], X, ALU.max)\
                .then_inc(sig.chain, 1)
            dve.wait_ge(sig.chain, 4)
            nc.vector.tensor_tensor(hot[:, :, :], ranked[:, :, :], each(first_of[:, :], EXPERTS), ALU.is_equal)\
                .then_inc(sig.hot_ok, 1)
            nc.vector.memset(nil[:, :], 0.0).then_inc(sig.nil_ok, 1)
            dve.wait_ge(sig.nil_ok, at(1))
            dve.wait_ge(sig.rank_ps, at(1))
            nc.vector.tensor_copy(total[:, :, :].rearrange("p e t -> p t e"),
                               duo[0][:, 1, 0:NTILE * EXPERTS].rearrange("p (t e) -> p t e", e=EXPERTS))\
                .then_inc(sig.chain, 1)
            dve.wait_ge(sig.chain, 5)
            flat = total[:, :, :].rearrange("p e t -> p (e t)")
            nc.vector.tensor_tensor_scan(upto[:, :, :].rearrange("p e t -> p (e t)"), flat, nil[:, :], 0.0,
                                      ALU.add, ALU.add)\
                .then_inc(sig.chain, 1)
            dve.wait_ge(sig.chain, 6)
            nc.vector.tensor_reduce(count[:, :], total[:, :, :], X, ALU.add)\
                .then_inc(sig.chain, 1)
            dve.wait_ge(sig.chain, 7)
            nc.vector.tensor_scalar(count_up[:, :], count[:, :], float(P - 1), None, ALU.add)\
                .then_inc(sig.chain, 1)
            dve.wait_ge(sig.chain, 8)
            nc.vector.tensor_scalar(slots_i[:, :], count_up[:, :], 7, None, ALU.logical_shift_right)\
                .then_inc(sig.chain, 1)
            dve.wait_ge(sig.chain, 9)
            nc.vector.tensor_copy(slots_f[:, :], slots_i[:, :])\
                .then_inc(sig.chain, 1)
            dve.wait_ge(sig.chain, 10)
            nc.vector.tensor_tensor_scan(slot_end[:, :], slots_f[:, :], nil[:, 0:EXPERTS], 0.0, ALU.add, ALU.add)\
                .then_inc(sig.chain, 1)
            dve.wait_ge(sig.chain, 11)
            nc.vector.tensor_tensor_scan(count_end[:, :], count[:, :], nil[:, 0:EXPERTS], 0.0, ALU.add, ALU.add)\
                .then_inc(sig.chain, 1)
            dve.wait_ge(sig.chain, 12)
            nc.vector.tensor_tensor(slots_f[:, :], slot_end[:, :], slots_f[:, :], ALU.subtract)\
                .then_inc(sig.chain, 1)
            dve.wait_ge(sig.chain, 13)
            nc.vector.tensor_tensor(count_end[:, :], count_end[:, :], count[:, :], ALU.subtract)\
                .then_inc(sig.chain, 1)
            dve.wait_ge(sig.chain, 14)
            nc.vector.scalar_tensor_tensor(out=shift[:, :], in0=slots_f[:, :], scalar=float(P), in1=count_end[:, :],
                                        op0=ALU.mult, op1=ALU.subtract)\
                .then_inc(sig.chain, 1)
            dve.wait_ge(sig.chain, 15)
            nc.vector.tensor_tensor(upto[:, :, :], upto[:, :, :], total[:, :, :], ALU.subtract)\
                .then_inc(sig.chain, 1)
            dve.wait_ge(sig.chain, 16)
            nc.vector.tensor_tensor(upto[:, :, :], upto[:, :, :], each(shift[:, :], NTILE), ALU.add)\
                .then_inc(sig.chain, 1)
            dve.wait_ge(sig.chain, 17)
            nc.vector.tensor_tensor(spot[:, :, :], duo[0][:, 0, 0:NTILE * EXPERTS].rearrange("p (t e) -> p t e", e=EXPERTS),
                                 upto[:, :, :].rearrange("p e t -> p t e"), ALU.add)\
                .then_inc(sig.chain, 1)
            dve.wait_ge(sig.chain, 18)
            nc.vector.tensor_tensor(spot[:, :, :], spot[:, :, :], hot[:, :, :], ALU.mult)\
                .then_inc(sig.chain, 1)
            dve.wait_ge(sig.chain, 19)
            nc.vector.tensor_reduce(place[:, :], spot[:, :, :], X, ALU.add)\
                .then_inc(sig.chain, 1)
            dve.wait_ge(sig.chain, 20)
            nc.vector.tensor_copy(place_i[:, :], place[:, :]).then_inc(sig.place_ok, 1)
            nc.vector.tensor_tensor(passed[:, :, :], each(slot_no[:, :], EXPERTS), over(slot_end[:, :], SLOTS), ALU.is_ge)\
                .then_inc(sig.chain, 1)
            dve.wait_ge(sig.chain, 21)
            nc.vector.tensor_reduce(slot_e[:, :], passed[:, :, :], X, ALU.add)\
                .then_inc(sig.chain, 1)
            dve.wait_ge(sig.chain, 22)
            nc.vector.tensor_scalar(slot_ei[:, :], slot_e[:, :], float(EXPERTS - 1), None, ALU.min)\
                .then_inc(sig.slot_e_ok, 1)

            def rows_in(s):
                if is_slot(s):
                    dve.wait_ge(sig.xsT_ps, at(s + 1))
                    dve.wait_ge(sig.eg_ps, at(2 * s))
                    nc.vector.tensor_copy(xsT[:, :, :], duo[3][:, 0, 0:D].rearrange("p (k n) -> p k n", k=KT))\
                        .then_inc(sig.xsT_ok, 1)

            def slot_step(s, parity, u):
                if is_slot(s):
                    dve.wait_ge(sig.eg_ps, at(2 * s + 2))
                    dve.wait_ge(sig.e_act_ok, at(s + 1))
                    dve.wait_ge(sig.ehT_ps, at(s))
                    nc.vector.scalar_tensor_tensor(out=eh[:, :], in0=duo[parity][:, 1, :], scalar=xs[:, parity, D:XROW],
                                                   in1=e_act[:, :], op0=ALU.mult, op1=ALU.mult).then_inc(sig.eh_ok, 1)
                if is_slot(s - 1):
                    dve.wait_ge(sig.ed_ps, at(s))
                    dve.wait_ge(sig.ys_out[1 - parity], at(16 * (u - 1 + parity)))
                    nc.vector.tensor_copy(ys[:, 1 - parity, :], duo[2][:, 1, 0:D]).then_inc(sig.ys_ok, 1)
                rows_in(s + 1)

            rows_in(0)
            slot_pipeline(dve, slot_step)

            def finish(t):
                dve.wait_ge(sig.zf_in, at(16 * (t + 1)))
                dve.wait_ge(sig.yf_in, at(16 * TILES * (t + 1)))
                dve.wait_ge(sig.out_done, at(16 * t))
                nc.vector.tensor_tensor(of[:, :, :], zf[:, :, :], yf[:, :, :], ALU.add)\
                    .then_inc(sig.sum_ok, 1)
                dve.wait_ge(sig.sum_ok, at(t + 1))
                for q in range(TILES):
                    last = nc.vector.bn_stats(st2[:, q, :], of[:, q, :])
                last.then_inc(sig.st2_ok, 1)
                dve.wait_ge(sig.st2_ok, at(t + 1))
                apart(dve)
                dve.wait_ge(sig.lne2_ok, at(t))
                apart(dve)
                for q in range(TILES):
                    nc.vector.bn_aggr(mv2[:, q, :], st2[:, q, :]).then_inc(sig.mv2_ok, 1)
                dve.wait_ge(sig.mv2_ok, at(TILES * (t + 1)))
                dve.wait_ge(sig.lnr2_ok, at(t + 1))
                for q in range(TILES):
                    nc.vector.tensor_scalar(of[:, q, :], of[:, q, :], mv2[:, q, 0:1], ln2_r[:, q:q + 1],
                                            ALU.subtract, ALU.mult).then_inc(sig.of_ok, 1)

            groups(dve, finish)

        @block.tensor
        def _(pe):
            mm = nc.tensor.matmul

            def three(out_, left, right, kt, start=True, stop=True):
                for k in range(kt):
                    for n, (a, b) in enumerate(PASSES):
                        last = mm(out_, left(a, k), right(b, k), start=start and k == 0 and n == 0,
                                  stop=stop and k == kt - 1 and n == len(PASSES) - 1)
                return last

            def x_transposes(t):
                pe.wait_ge(sig.xin, at(16 * (t + 1)))
                pe.wait_ge(sig.yT_hi, at(KT * (t - 1)))
                pe.wait_ge(sig.yT_lo, at(KT * (t - 1)))
                for k in range(KT):
                    for q in range(TILES):
                        last = nc.tensor.transpose(duo[3][:, k, q * P:(q + 1) * P], x_in[:, q, k * P:(k + 1) * P], ident[:, :])
                last.then_inc(sig.xT_ps, 1)

            pe.wait_ge(sig.c_in, at(16 * N_IN))
            x_transposes(0)
            pe.wait_ge(sig.raw_in, at(16 * 9))
            for k in range(KT):
                last = nc.tensor.transpose(duo[2][:, 0, k * EXPERTS:(k + 1) * EXPERTS], raw_r[:, k * P:(k + 1) * P],
                                           ident[0:EXPERTS, 0:EXPERTS])
            last.then_inc(sig.wrT_ps, 1)
            pe.wait_ge(sig.w_lo, at(6))

            def similarities(p, j):
                b, hp = j // 4, j % 4
                if j < 2:
                    pe.wait_ge(sig.vg_ok, at(TILES * (p + 1)))
                    pe.wait_ge(sig.sact_ok, at(FT * (p - 1)))
                    pe.wait_ge(sig.h_ok, at(FT * (p - 1)))
                    pe.wait_ge(sig.z_ok, at(2 * p))
                else:
                    pe.wait_ge(sig.s_diag, at(8 * p + j - 1))
                for i in range(2):
                    head = 2 * hp + i
                    for kb in range(2):
                        lo = SEQ * b + P * kb
                        last = mm(duo[j % 2][:, i, SEQ * kb:SEQ * (kb + 1)], stack[1][:, head, lo:lo + P],
                                  stack[0][:, head, SEQ * b:SEQ * (b + 1)], start=True, stop=True)
                last.then_inc(sig.s_ps, 1)

            def values(p, a):
                b, g = a // 2, a % 2
                pe.wait_ge(sig.s_diag, at(8 * p + 2 * a + 2))
                pe.wait_ge(sig.s_off, at(8 * p + 2 * a + 2))
                if a < 2:
                    pe.wait_ge(sig.zs_ok, at(2 * (p - 1)))
                for kb in range(2):
                    for i in range(4):
                        ring, half = (2 * a + i // 2) % 4, i % 2
                        lo = SEQ * b + P * kb
                        rhs = sims[:, ring, half, 0:2, :] if kb == 0 else sims[:, ring, half, 2:3, :]
                        last = mm(duo[2][HD * i:HD * (i + 1), g, lo:SEQ * (b + 1)],
                                  vg[:, 2 * b + kb, HD * (4 * g + i):HD * (4 * g + i + 1)],
                                  rhs.rearrange("p b q -> p (b q)"), start=(kb == 0), stop=(kb == 1),
                                  skip_group_check=True)
                last.then_inc(sig.av_ps, 1)

            def step(t):
                if has(t - 1):
                    p = t - 1
                    pe.wait_ge(sig.stack_in, at(192 * (p + 1)))
                    for j in range(8):
                        similarities(p, j)
                        if j in (3, 5, 7):
                            values(p, (j - 3) // 2)
                    values(p, 3)
                if has(t):
                    for s in range(4):
                        side, e = s // 2, s % 2
                        pe.wait_ge(sig.xT_hi, at(KT * (t + 1)))
                        pe.wait_ge(sig.xT_lo, at(KT * (t + 1)))
                        pe.wait_ge(sig.s_diag, at(8 * t))
                        three(duo[side][:, e, :], lambda part, k: wqk[:, side, part, k, e::2],
                              lambda part, k: xT[:, part, k, :], KT).then_inc(sig.qk_ps, 1)
                if has(t - 1):
                    p = t - 1
                    pe.wait_ge(sig.retT_ok, at(2 * (p + 1)))
                    pe.wait_ge(sig.xT_lo, at(KT * (p + 2) if has(p + 1) else KT * (p + 1)))
                    for g in range(2):
                        for q in range(TILES):
                            last = nc.tensor.transpose(duo[3][:, q // 2, D * (q % 2) + P * g:D * (q % 2) + P * (g + 1)],
                                                       retT[:, g, q * P:(q + 1) * P], ident[:, :])
                    last.then_inc(sig.rn_ps, 1)
                if has(t - 2):
                    p = t - 2
                    pe.wait_ge(sig.x1_ok, at(TILES * (p + 1)))
                    pe.wait_ge(sig.retT_ok, at(2 * (p + 2) if has(p + 1) else 2 * (p + 1)))
                    pe.wait_ge(sig.zs_ok, at(2 * p))
                    for k in range(KT):
                        for q in range(TILES):
                            last = nc.tensor.transpose(duo[2][:, k, q * P:(q + 1) * P], x1[:, q, k * P:(k + 1) * P], ident[:, :])
                    last.then_inc(sig.x1T_ps, 1)
                if has(t):
                    for q in range(TILES):
                        pe.wait_ge(sig.prod_ok, at(4 * t + q + 1))
                        three(duo[q // 2][:, q % 2, :], lambda part, k: xT[:, part, k, q * P:(q + 1) * P],
                              lambda part, k: wvg[:, part, k, :], KT).then_inc(sig.vg_ps, 1)
                if has(t - 2):
                    p = t - 2
                    pe.wait_ge(sig.x1T_hi, at(KT * (p + 1)))
                    pe.wait_ge(sig.x1T_lo, at(KT * (p + 1)))
                    three(duo[2][0:EXPERTS, 0, :], lambda part, k: wr[:, part, k, :],
                          lambda part, k: x1T[:, part, k, :], KT).then_inc(sig.lgT_ps, 1)
                    for j in range(FT):
                        if j < 2:
                            if has(t):
                                pe.wait_ge(sig.vg_ok, at(TILES * (t + 1)))
                            if has(t - 1):
                                pe.wait_ge(sig.s_diag, at(8 * t))
                            pe.wait_ge(sig.z_ok, at(2 * (p + 1)))
                        else:
                            pe.wait_ge(sig.sact_ok, at(FT * p + j - 1))
                            pe.wait_ge(sig.h_ok, at(FT * p + j - 1))
                        for i in range(2):
                            three(duo[j % 2][:, i, :], lambda part, k: wsgu[:, i, part, k, j * P:(j + 1) * P],
                                  lambda part, k: x1T[:, part, k, :], KT).then_inc(sig.gu_ps, 1)
                    pe.wait_ge(sig.lgT_ok, at(p + 1))
                    apart(pe)
                    for q in range(TILES):
                        last = nc.tensor.transpose(duo[2][:, 1, q * EXPERTS:(q + 1) * EXPERTS],
                                                   lgT[:, q * P:(q + 1) * P], ident[0:EXPERTS, 0:EXPERTS])
                    last.then_inc(sig.lg_ps, 1)
                if has(t - 1):
                    p = t - 1
                    pe.wait_ge(sig.y_ok, at(p + 1))
                    pe.wait_ge(sig.rn_ok, at(2 * (p + 1)))
                    for k in range(KT):
                        for q in range(TILES):
                            last = nc.tensor.transpose(duo[3][:, k, q * P:(q + 1) * P], y[:, q, k * P:(k + 1) * P], ident[:, :])
                    last.then_inc(sig.yT_ps, 1)
                if has(t - 2):
                    p = t - 2
                    pe.wait_ge(sig.h_hi, at(FT * (p + 1)))
                    pe.wait_ge(sig.h_lo, at(FT * (p + 1)))
                    pe.wait_ge(sig.lg_ok, at(p + 1))
                    for q in range(TILES):
                        last = three(duo[2][:, q // 2, D * (q % 2):D * (q % 2 + 1)],
                                     lambda part, f: hT[:, part, f, q * P:(q + 1) * P],
                                     lambda part, f: wsd[:, part, f, :], FT)
                        if q % 2:
                            last.then_inc(sig.dn_ps, 1)
                if has(t - 1):
                    p = t - 1
                    pe.wait_ge(sig.yT_hi, at(KT * (p + 1)))
                    pe.wait_ge(sig.yT_lo, at(KT * (p + 1)))
                    if has(t):
                        pe.wait_ge(sig.vg_ok, at(TILES * (t + 1)))
                    if has(t - 2):
                        pe.wait_ge(sig.h_ok, at(FT * p))
                    pe.wait_ge(sig.s_diag, at(8 * t))
                    for q in range(TILES):
                        last = three(duo[0][:, q // 2, D * (q % 2):D * (q % 2 + 1)],
                                     lambda part, k: yT[:, part, k, q * P:(q + 1) * P],
                                     lambda part, k: wo[:, part, k, :], KT)
                        if q % 2:
                            last.then_inc(sig.o_ps, 1)
                if has(t + 1):
                    x_transposes(t + 1)

            pipeline(pe, step)

            pe.wait_ge(sig.hot_ok, at(1))
            flat = hot[:, :, :].rearrange("p t e -> p (t e)")
            mm(duo[0][:, 0, 0:NTILE * EXPERTS], before[:, :], flat, start=True, stop=True)
            mm(duo[0][:, 1, 0:NTILE * EXPERTS], ones[:, :], flat, start=True, stop=True).then_inc(sig.rank_ps, 1)

            def slot_transposes(s, parity, u):
                if is_slot(s):
                    pe.wait_ge(sig.xs_in[parity], at(16 * (u + 1)))
                    pe.wait_ge(sig.xsT_ok, at(s))
                    for k in range(KT):
                        last = nc.tensor.transpose(duo[3][:, 0, k * P:(k + 1) * P], xs[:, parity, k * P:(k + 1) * P], ident[:, :])
                    last.then_inc(sig.xsT_ps, 1)

            gu_flat = w_gu[:, :, :, :].rearrange("p e k n -> p (e k n)")
            dn_flat = w_dn[:, :, :, :].rearrange("p e f n -> p (e f n)")

            def expert_of(s):
                return pe.value_load(slot_ei[0:1, one(s)], min_val=0, max_val=EXPERTS - 1)

            def slot_step(s, parity, u):
                if is_slot(s - 1):
                    pe.wait_ge(sig.eh_ok, at(s))
                    pe.wait_ge(sig.ehT_ok, at(s - 1))
                    for f in range(FT):
                        last = nc.tensor.transpose(duo[2][:, 0, f * P:(f + 1) * P], eh[:, f * P:(f + 1) * P], ident[:, :])
                    last.then_inc(sig.ehT_ps, 1)
                if is_slot(s):
                    pe.wait_ge(sig.xsT_ok, at(s + 1))
                    apart(pe)
                    pe.wait_ge(sig.eh_ok, at(s - 1))
                    apart(pe)
                    e = expert_of(s)
                    for half in range(2):
                        for k in range(KT):
                            last = mm(duo[parity][:, half, :], xsT[:, k, :],
                                      gu_flat[:, bass.ds(e * (KT * 2 * FF) + (k * 2 + half) * FF, FF)],
                                      start=(k == 0), stop=(k == KT - 1))
                        last.then_inc(sig.eg_ps, 1)
                if is_slot(s - 1):
                    pe.wait_ge(sig.ehT_ok, at(s))
                    apart(pe)
                    pe.wait_ge(sig.ys_ok, at(s - 1))
                    apart(pe)
                    e = expert_of(s - 1)
                    for f in range(FT):
                        last = mm(duo[2][:, 1, 0:D], ehT[:, f, :], dn_flat[:, bass.ds(e * (FT * D) + f * D, D)],
                                  start=(f == 0), stop=(f == FT - 1))
                    last.then_inc(sig.ed_ps, 1)
                slot_transposes(s + 1, 1 - parity, u + parity)

            pe.wait_ge(sig.slot_e_ok, at(1))
            pe.wait_ge(sig.ew_in, at(16 * 2 * EXPERTS))
            pe.wait_ge(sig.place_ok, at(1))
            slot_transposes(0, 0, 0)
            slot_pipeline(pe, slot_step)


def tables():
    f = np.float32
    start, stop = f(0.0), f(1.0)
    xs_ = np.linspace(start, stop, HALF, dtype=f)
    theta = (f(1.0) / np.power(f(10000.0), xs_)).astype(f)
    angle = (np.arange(SEQ, dtype=f)[None, :] * theta[:, None]).astype(f).astype(np.float64)
    gamma = (f(1.0) - np.exp(np.linspace(f(np.log(1 / 32)), f(np.log(1 / 64)), HEADS, dtype=f)).astype(f)).astype(f)
    n = np.arange(SEQ, dtype=np.float64)
    decay = gamma.astype(np.float64)[:, None] ** n[None, :]
    rotation = np.zeros((HEADS, HALF, 4, SEQ))
    for i, table in enumerate((np.cos(angle), np.sin(angle))):
        rotation[:, :, i] = table[None] * decay[:, None]
        rotation[:, :, 2 + i] = table[None] / decay[:, None] / np.sqrt(float(HD))
    r = np.arange(P)
    squares = np.zeros((P, 4 * P + EXPERTS + SLOTS), f)
    squares[:, 0:P] = np.eye(P)
    squares[:, P:2 * P] = r[None, :] >= r[:, None]
    squares[:, 2 * P:3 * P] = r[:, None] < r[None, :]
    squares[:, 3 * P:4 * P] = 1.0
    squares[:, 4 * P:4 * P + EXPERTS] = EXPERTS - np.arange(EXPERTS)
    squares[:, 4 * P + EXPERTS:] = np.arange(SLOTS)
    return rotation.reshape(P, 4 * SEQ).astype(f), squares


_INS = ["L0_attn_x", "L0_attn_w_q", "L0_attn_b_q", "L0_attn_w_k", "L0_attn_b_k", "L0_attn_w_v", "L0_attn_b_v",
        "L0_attn_w_g", "L0_attn_b_g", "L0_attn_w_o", "L0_attn_b_o", "L0_attn_gn_weight", "L0_attn_gn_bias",
        "L0_ffn_router_w", "L0_ffn_gate_up_proj", "L0_ffn_down_proj", "L0_ffn_shared_gate_w",
        "L0_ffn_shared_up_w", "L0_ffn_shared_down_w"]


def kernel(**inputs):
    import concourse.bacc as bacc
    from concourse.bass_utils import run_bass_kernel_spmd

    nc = bacc.Bacc("TRN2", target_bir_lowering=False, num_devices=1)
    arrays, args = {}, []

    def give(name, a):
        arrays[name] = a
        args.append(nc.dram_tensor(name, a.shape, mybir.dt.from_np(a.dtype), kind="ExternalInput").ap())

    for name in _INS:
        a = np.ascontiguousarray(inputs[name])
        give(name, a.reshape(SEQS * SEQ, D) if name == "L0_attn_x" else a)
    rotation, squares = tables()
    give("rotation", rotation)
    give("squares", squares)
    args.append(nc.dram_tensor("out_rows", (SEQS * SEQ, D), F32, kind="ExternalOutput").ap())
    build(nc, *args)
    r = run_bass_kernel_spmd(nc, [arrays], core_ids=[0])
    return r.results[0]["out_rows"].reshape(SEQS, SEQ, D)
```

```python
from contextlib import ExitStack

import numpy as np
import concourse.bass as bass
from concourse import mybir

F32 = mybir.dt.float32
F32R = mybir.dt.float32r
I32 = mybir.dt.int32
ALU = mybir.AluOpType
ACT = mybir.ActivationFunctionType
X = mybir.AxisListType.X

P = 128
SEQS, SEQ, D = 16, 256, 256
HEADS = 8
HD = D // HEADS
HALF = HD // 2
PAIRS = SEQS // 2
TOK = 2 * SEQ
TILES = TOK // P
NTILE = SEQS * SEQ // P
KT = D // P
EXPERTS, FF = 8, 512
FT = FF // P
SLOTS = NTILE + EXPERTS - 1
TOKENS = SEQS * SEQ
RING = 4
SEATS = (EXPERTS - 1) * TOKENS + SLOTS * P
SEAT = 3
EPS = 1e-5
N_IN = 13
ROUTE = 13
PASSES = ((0, 0), (0, 1), (1, 0))


def build(nc, x, w_q, b_q, w_k, b_k, w_v, b_v, w_g, b_g, w_o, b_o, gn_w, gn_b, router_w,
          gate_up, down, sh_gate, sh_up, sh_down, rotation, squares, token_seats, free_seats, out):
    ctx = ExitStack()
    with ctx:
        def scratch(name, shape, dt=F32):
            return nc.dram_tensor(name, shape, dt, kind="Internal").ap()

        def f32(ap):
            return ap.bitcast(F32)

        def tensors(stack):
            return lambda name, shape, dt=F32: stack.enter_context(nc.sbuf_tensor(name, shape, dt))

        rot_d = scratch("rot_d", [2, 2, 2, P, TOK])
        xz_d = scratch("xz_d", [TOKENS + 1, 2 * D])
        seat_d = scratch("seat_d", [SEATS, SEAT], I32)

        sb = tensors(ctx)
        ident = sb("ident", [P, P])
        causal = sb("causal", [P, P])
        before = sb("before", [P, P])
        ones = sb("ones", [P, P])
        priority = sb("priority", [P, EXPERTS])
        slot_no = sb("slot_no", [P, SLOTS])
        minus_half = sb("minus_half", [P, TILES * HEADS])
        rot = sb("rot", [P, 4, SEQ])
        bias_qk = sb("bias_qk", [P, 2, 2])
        bias_vg = sb("bias_vg", [P, 2 * D])
        bias_o = sb("bias_o", [P, D])
        norm_w = sb("norm_w", [P, D])
        norm_b = sb("norm_b", [P, D])
        wo = sb("wo", [P, 2, KT, D], F32R)
        wsgu = sb("wsgu", [P, 2, 2, KT, FF], F32R)
        wsd = sb("wsd", [P, 2, FT, D], F32R)
        wr = sb("wr", [P, 2, KT, EXPERTS], F32R)

        seats = sb("seats", [P, NTILE, SEAT], I32)
        stage = sb("stage", [P, TILES, SEAT], I32)
        place_i = sb("place_i", [P, TILES], I32)
        logits = sb("logits", [P, TILES, EXPERTS])
        top = sb("top", [P, TILES])
        hot = sb("hot", [P, TILES, EXPERTS])
        ranked = sb("ranked", [P, TILES, EXPERTS])
        first_of = sb("first_of", [P, TILES])
        start = sb("start", [P, TILES + 1, EXPERTS])
        spot = sb("spot", [P, TILES, EXPERTS])
        place = sb("place", [P, TILES])
        minus_one = sb("minus_one", [P, TILES])
        inv_e = sb("inv_e", [P, TILES])
        powed = sb("powed", [P, TILES])
        powed1 = sb("powed1", [P, TILES])
        zero = sb("zero", [P, EXPERTS])
        region = sb("region", [P, EXPERTS])

        seat = sb("seat", [P, RING, SEAT], I32)
        dest = sb("dest", [P, RING], I32)

        first = ExitStack()
        with first:
            sb = tensors(first)
            with ExitStack() as early:
                e_sb = tensors(early)
                raw_qk = e_sb("raw_qk", [P, 2, KT, D])
                raw_vg = e_sb("raw_vg", [P, KT, 2 * D])
                raw_o = e_sb("raw_o", [P, KT, D])
                raw_gu = e_sb("raw_gu", [P, 2, KT, FF])
                raw_d = e_sb("raw_d", [P, FT, D])
                raw_r = e_sb("raw_r", [EXPERTS, D])
                mean_v = e_sb("mean_v", [P, KT, HEADS])
                mean_b = e_sb("mean_b", [P, HEADS])
            with ExitStack() as shared:
                s_sb = tensors(shared)
                s_act = s_sb("s_act", [P, 2, TOK])
                h = s_sb("h", [P, 2, TOK])
                hT = s_sb("hT", [P, 2, FT, TOK], F32R)
                gate = s_sb("gate", [P, TILES, D])
            s_sb = sb
            xz = s_sb("xz", [P, RING, 2 * D])
            xsT = s_sb("xsT", [P, KT, P])
            e_act = s_sb("e_act", [P, FF])
            eh = s_sb("eh", [P, FF])
            ehT = s_sb("ehT", [P, FT, P])
            of = s_sb("of", [P, 2, D])
            st2 = s_sb("st2", [P, 6])
            mv2 = s_sb("mv2", [P, 2])
            ln2_e = s_sb("ln2_e", [P, 1])
            ln2_r = s_sb("ln2_r", [P, 1])
            rest = s_sb("rest", [P, 4 * TOK + FT * 2 * TOK - (RING * 2 * D + KT * P + 3 * FF + 2 * D + 10)])
            count = s_sb("count", [P, EXPERTS])
            count_up = s_sb("count_up", [P, EXPERTS], I32)
            slots_i = s_sb("slots_i", [P, EXPERTS], I32)
            slots_f = s_sb("slots_f", [P, EXPERTS])
            slot_end = s_sb("slot_end", [P, EXPERTS])
            skip = s_sb("skip", [P, EXPERTS])
            passed = s_sb("passed", [P, SLOTS, EXPERTS - 1])
            skipped = s_sb("skipped", [P, SLOTS, EXPERTS - 1])
            slot_e = s_sb("slot_e", [P, SLOTS])
            slot_ei = s_sb("slot_ei", [P, SLOTS], I32)
            slot_r = s_sb("slot_r", [P, SLOTS])
            slot_row = s_sb("slot_row", [P, SLOTS])
            slot_ri = s_sb("slot_ri", [P, SLOTS], I32)
            rest_of_gate = s_sb("rest_of_gate", [P, TILES * D - 2 * SLOTS * (EXPERTS - 1) - 5 * SLOTS - 6 * EXPERTS])
            x1 = sb("x1", [P, TILES, D])
            x_res = sb("x_res", [P, TILES, D])
            zs = sb("zs", [P, TILES, D])
            retT = sb("retT", [P, 2, TOK])
            var = sb("var", [P, TILES * HEADS])
            var_e = sb("var_e", [P, TILES * HEADS])
            rstd = sb("rstd", [P, TILES * HEADS])
            y = sb("y", [P, TILES, D])
            yT = sb("yT", [P, 2, KT, TOK], F32R)
            stats = sb("stats", [P, TILES, 6])
            mv = sb("mv", [P, TILES, 2])
            ln_e = sb("ln_e", [P, TILES])
            ln_r = sb("ln_r", [P, TILES])
            x1T = sb("x1T", [P, 2, KT, TOK], F32R)
            lgT = sb("lgT", [EXPERTS, TOK])

            attention = ExitStack()
            with attention:
                a_sb = tensors(attention)
                wqk = a_sb("wqk", [P, 2, 2, KT, D], F32R)
                wvg = a_sb("wvg", [P, 2, KT, 2 * D], F32R)
                stack = [a_sb("stack_q", [96, HEADS, TOK], F32R),
                         a_sb("stack_k", [96, HEADS, TOK], F32R)]
                prod = a_sb("prod", [P, 2, 4, TOK])
                vg = a_sb("vg", [P, TILES, 2 * D])
                xT = a_sb("xT", [P, 2, KT, TOK], F32R)
                sims = a_sb("sims", [P, 4, 2, 3, P])
                x_in = a_sb("x_in", [P, TILES, D])
            w_gu = sb("w_gu", [P, EXPERTS, KT, 2 * FF])
            w_dn = sb("w_dn", [P, EXPERTS, FT, D])

        duo = [ctx.enter_context(nc.psum_tensor(f"duo{i}", [P, 2, 512], F32)) for i in range(4)]

        def new(name):
            return ctx.enter_context(nc.semaphore(name))

        class sig:
            apart = new("apart")
            first_in = new("first_in")
            c_in = new("c_in")
            wqk_in = new("wqk_in")
            wvg_in = new("wvg_in")
            raw_in = new("raw_in")
            wrT_ps = new("wrT_ps")
            w_hi = new("w_hi")
            w_lo = new("w_lo")
            center = new("center")
            xin = new("xin")
            xres_in = new("xres_in")
            xT_ps = new("xT_ps")
            xT_hi = new("xT_hi")
            xT_lo = new("xT_lo")
            qk_ps = new("qk_ps")
            prod_ok = new("prod_ok")
            turned_ok = new("turned_ok")
            split_hi = new("split_hi")
            split_lo = new("split_lo")
            rot_out = new("rot_out")
            stack_in = new("stack_in")
            vg_ps = new("vg_ps")
            vg_ok = new("vg_ok")
            gate_ok = new("gate_ok")
            s_ps = new("s_ps")
            s_off = new("s_off")
            s_diag = new("s_diag")
            av_ps = new("av_ps")
            retT_ok = new("retT_ok")
            rn_ps = new("rn_ps")
            sq_ok = new("sq_ok")
            var_ok = new("var_ok")
            eps_ok = new("eps_ok")
            rstd_ok = new("rstd_ok")
            rn_ok = new("rn_ok")
            y_w = new("y_w")
            y_b = new("y_b")
            y_ok = new("y_ok")
            yT_ps = new("yT_ps")
            yT_hi = new("yT_hi")
            yT_lo = new("yT_lo")
            xb_ok = new("xb_ok")
            o_ps = new("o_ps")
            z_ok = new("z_ok")
            st_ok = new("st_ok")
            mv_ok = new("mv_ok")
            lne_ok = new("lne_ok")
            lnr_ok = new("lnr_ok")
            x1_ok = new("x1_ok")
            x1_out = new("x1_out")
            x1T_ps = new("x1T_ps")
            x1T_hi = new("x1T_hi")
            x1T_lo = new("x1T_lo")
            gu_ps = new("gu_ps")
            sact_ok = new("sact_ok")
            h_ok = new("h_ok")
            h_hi = new("h_hi")
            h_lo = new("h_lo")
            lgT_ps = new("lgT_ps")
            lgT_ok = new("lgT_ok")
            lg_ps = new("lg_ps")
            lg_ok = new("lg_ok")
            dn_ps = new("dn_ps")
            zs_ok = new("zs_ok")
            zs_out = new("zs_out")
            zero_ok = new("zero_ok")
            zrow_out = new("zrow_out")
            free_out = new("free_out")
            route = new("route")
            hot_ok = new("hot_ok")
            rank_ps = new("rank_ps")
            place_ok = new("place_ok")
            pow_ok = new("pow_ok")
            pow1_ok = new("pow1_ok")
            score_ok = new("score_ok")
            ids_ok = new("ids_ok")
            scat = new("scat")
            plan = new("plan")
            plan_ok = new("plan_ok")
            ew_in = new("ew_in")
            xsT_ps = new("xsT_ps")
            xsT_ok = new("xsT_ok")
            eg_ps = new("eg_ps")
            e_act_ok = new("e_act_ok")
            eh_ok = new("eh_ok")
            dest_ok = new("dest_ok")
            ehT_ps = new("ehT_ps")
            ehT_ok = new("ehT_ok")
            ed_ps = new("ed_ps")
            sum_ok = new("sum_ok")
            st2_ok = new("st2_ok")
            mv2_ok = new("mv2_ok")
            lne2_ok = new("lne2_ok")
            lnr2_ok = new("lnr2_ok")
            of_ok = new("of_ok")
            seat_in = [new(f"seat_in{i}") for i in range(RING)]
            xz_in = [new(f"xz_in{i}") for i in range(RING)]
            out_done = [new(f"out_done{i}") for i in range(RING)]

        def at(value):
            return max(value, 0) if isinstance(value, int) else value

        def apart(eng):
            eng.sem_inc(sig.apart, 1)

        def has(i):
            return not isinstance(i, int) or 0 <= i < PAIRS

        def is_last(t):
            return isinstance(t, int) and t == PAIRS

        def pipeline(eng, step):
            for t in range(3):
                step(t)
            with eng.Fori(3, PAIRS - 1) as t:
                step(t)
            for t in range(PAIRS - 1, PAIRS + 2):
                step(t)

        def slot_pipeline(eng, step):
            for s in range(RING):
                step(s, s % RING, s // RING)
            with eng.Fori(1, SLOTS // RING) as u:
                for r in range(RING):
                    step(RING * u + r, r, u)
            for s in range(SLOTS // RING * RING, SLOTS + 1):
                step(s, s % RING, s // RING)

        def is_slot(s):
            return not isinstance(s, int) or 0 <= s < SLOTS

        def tile_rows(dram, t, q):
            v = dram.rearrange("(t q p) d -> t p q d", q=q, p=P)
            return v[t] if isinstance(t, int) else v[bass.ds(t, 1)].rearrange("a p q d -> (a p) q d")

        def ahead(r, u, by):
            return (r + by) % RING, u + (r + by) // RING

        def one(t):
            return slice(t, t + 1) if isinstance(t, int) else bass.ds(t, 1)

        def spread(vector, n=D):
            return bass.AP(vector.tensor, 0, [[0, P], [1, n]])

        def over(ap, n):
            return bass.AP(ap.tensor, ap.offset, [list(ap.ap[0]), [0, n], *[list(a) for a in ap.ap[1:]]])

        def each(ap, n):
            return bass.AP(ap.tensor, ap.offset, [*[list(a) for a in ap.ap], [0, n]])

        block = ctx.enter_context(nc.Block())

        @block.sync
        def _(sp):
            sp.dma_start(ident[:, :], squares[:, 0:P]).then_inc(sig.first_in, 16)
            sp.dma_start(x_in[:, :, :], tile_rows(x, 0, TILES)).then_inc(sig.xin, 16)
            sp.dma_start(bias_qk[:, 0, :], b_q.rearrange("(p two) -> p two", two=2)).then_inc(sig.first_in, 16)
            sp.dma_start(bias_qk[:, 1, :], b_k.rearrange("(p two) -> p two", two=2)).then_inc(sig.first_in, 16)
            sp.dma_start(rot[:, :, :], rotation.rearrange("p (f n) -> p f n", f=4)).then_inc(sig.first_in, 16)
            sp.dma_start(causal[:, :], squares[:, P:2 * P]).then_inc(sig.c_in, 16)
            sp.dma_start(before[:, :], squares[:, 2 * P:3 * P]).then_inc(sig.c_in, 16)
            sp.dma_start(ones[:, :], squares[:, 3 * P:4 * P]).then_inc(sig.c_in, 16)
            sp.dma_start(priority[:, :], squares[:, 4 * P:4 * P + EXPERTS]).then_inc(sig.c_in, 16)
            sp.dma_start(slot_no[:, :], squares[:, 4 * P + EXPERTS:4 * P + EXPERTS + SLOTS]).then_inc(sig.c_in, 16)
            o = 4 * P + EXPERTS + SLOTS
            sp.dma_start(region[:, :], squares[:, o:o + EXPERTS]).then_inc(sig.c_in, 16)
            sp.dma_start(start[:, TILES, :], squares[:, o:o + EXPERTS]).then_inc(sig.c_in, 16)
            sp.dma_start(seats[:, :, :], token_seats.rearrange("p (t c) -> p t c", c=SEAT)).then_inc(sig.c_in, 16)
            sp.dma_start(bias_vg[:, 0:D], spread(b_v)).then_inc(sig.c_in, 16)
            sp.dma_start(bias_vg[:, D:2 * D], spread(b_g)).then_inc(sig.c_in, 16)
            sp.dma_start(bias_o[:, :], spread(b_o)).then_inc(sig.c_in, 16)
            sp.dma_start(norm_w[:, :], spread(gn_w)).then_inc(sig.c_in, 16)
            sp.dma_start(norm_b[:, :], spread(gn_b)).then_inc(sig.c_in, 16)
            sp.dma_start(seat_d, free_seats).then_inc(sig.free_out, 16)

            def step(t):
                if has(t + 1):
                    sp.wait_ge(sig.xT_ps, at(t + 1))
                    sp.dma_start(x_in[:, :, :], tile_rows(x, t + 1, TILES)).then_inc(sig.xin, 16)
                if has(t - 1):
                    sp.wait_ge(sig.x1_ok, at(TILES * (t - 1)))
                    sp.dma_start(x_res[:, :, :], tile_rows(x, t - 1, TILES)).then_inc(sig.xres_in, 16)
                if has(t - 2):
                    sp.wait_ge(sig.x1_ok, at(TILES * (t - 1)))
                    sp.dma_start(tile_rows(xz_d[0:TOKENS, 0:D], t - 2, TILES), x1[:, :, :]).then_inc(sig.x1_out, 16)
                if isinstance(t, int) and t == PAIRS:
                    sp.wait_ge(sig.av_ps, 4 * PAIRS)
                    for e in range(EXPERTS):
                        sp.dma_start(w_gu[:, e, :, :], gate_up[e].rearrange("(k p) n -> p k n", p=P))\
                            .then_inc(sig.ew_in, 16)
                        sp.dma_start(w_dn[:, e, :, :], down[e].rearrange("(k p) n -> p k n", p=P))\
                            .then_inc(sig.ew_in, 16)
                if has(t):
                    for side in range(2):
                        sp.wait_ge(sig.split_hi, at(4 * t + 2 * side + 2))
                        apart(sp)
                        sp.wait_ge(sig.split_lo, at(4 * t + 2 * side + 2))
                        apart(sp)
                        sp.wait_ge(sig.stack_in, at(192 * t))
                        for part, places in enumerate((slice(1, 3), slice(0, 4, 3))):
                            sp.dma_start(rot_d[side, part].rearrange("e p n -> p e n"), prod[:, side, places, :])\
                                .then_inc(sig.rot_out, 16)
                        sp.wait_ge(sig.rot_out, at(64 * t + 32 * side + 32))
                        apart(sp)
                        sp.wait_ge(sig.s_ps, at(8 * t))
                        for group, part in enumerate(((0, 1, 0), (0, 0, 1))[side]):
                            for e in range(2):
                                lo = HD * group + HALF * e
                                sp.dma_start(f32(stack[side][lo:lo + HALF, :, :]),
                                             rot_d[side, part, e].rearrange("(h i) n -> i h n", i=HALF))\
                                    .then_inc(sig.stack_in, 16)
                if has(t - 2):
                    sp.wait_ge(sig.zs_ok, at(2 * (t - 1)))
                    sp.dma_start(tile_rows(xz_d[0:TOKENS, D:2 * D], t - 2, TILES), zs[:, :, :]).then_inc(sig.zs_out, 16)

            pipeline(sp, step)

            def seat_load(s, r, u):
                if is_slot(s):
                    sp.wait_ge(sig.eh_ok, at(s - RING + 1))
                    apart(sp)
                    sp.wait_ge(sig.dest_ok, at(s - RING + 1))
                    apart(sp)
                    row = sp.value_load(slot_ri[0:1, one(s)], min_val=0, max_val=SEATS - P)
                    sp.dma_start(seat[:, r, :], seat_d[bass.ds(row, P), :]).then_inc(sig.seat_in[r], 16)

            def slot_step(s, r, u):
                seat_load(s + 3, *ahead(r, u, 3))

            sp.wait_ge(sig.plan_ok, 2)
            sp.wait_ge(sig.scat, 16 * NTILE)
            seat_load(0, 0, 0)
            seat_load(1, 1, 0)
            seat_load(2, 2, 0)
            slot_pipeline(sp, slot_step)
            for r in range(RING):
                sp.wait_ge(sig.out_done[r], 16 * ((SLOTS - r + RING - 1) // RING))

        @block.scalar
        def _(act):
            def k_rows(w):
                return w.rearrange("(k p) n -> p k n", p=P)

            act.dma_start(raw_qk[:, 0, :, :], k_rows(w_q)).then_inc(sig.wqk_in, 16)
            act.dma_start(raw_qk[:, 1, :, :], k_rows(w_k)).then_inc(sig.wqk_in, 16)
            act.dma_start(raw_vg[:, :, 0:D], k_rows(w_v)).then_inc(sig.wvg_in, 16)
            act.dma_start(raw_vg[:, :, D:2 * D], k_rows(w_g)).then_inc(sig.wvg_in, 16)
            act.dma_start(raw_o[:, :, :], k_rows(w_o)).then_inc(sig.raw_in, 16)
            act.dma_start(raw_gu[:, 0, :, :], k_rows(sh_gate)).then_inc(sig.raw_in, 16)
            act.dma_start(raw_gu[:, 1, :, :], k_rows(sh_up)).then_inc(sig.raw_in, 16)
            act.dma_start(raw_d[:, :, :], k_rows(sh_down)).then_inc(sig.raw_in, 16)
            act.dma_start(raw_r[:, :], router_w).then_inc(sig.raw_in, 16)

            def x_hi(t):
                for k in range(KT):
                    act.wait_ge(sig.xT_ps, at(t + 1))
                    act.wait_ge(sig.vg_ps, at(TILES * t))
                    nc.scalar.activation(xT[:, 0, k, :], duo[3][:, k, :], ACT.Copy)\
                        .then_inc(sig.xT_hi, 1)

            x_hi(0)
            act.wait_ge(sig.wqk_in, 16 * 2)
            nc.scalar.activation(wqk[:, :, 0, :, :], raw_qk[:, :, :, :], ACT.Copy)\
                .then_inc(sig.w_hi, 1)
            act.wait_ge(sig.wvg_in, 16 * 2)
            act.wait_ge(sig.center, 5)
            nc.scalar.activation(wvg[:, 0, :, :], raw_vg[:, :, :], ACT.Copy)\
                .then_inc(sig.w_hi, 1)

            def step(t):
                if has(t - 1):
                    p = t - 1
                    for j in range(8):
                        act.wait_ge(sig.s_ps, at(8 * p + j + 1))
                        act.wait_ge(sig.av_ps, at(4 * p + j // 2 - 1))
                        nc.scalar.activation(sims[:, j % 4, :, 1, :], duo[j % 2][:, :, P:2 * P], ACT.Copy)\
                            .then_inc(sig.s_off, 1)
                    for g in range(2):
                        act.wait_ge(sig.av_ps, at(4 * p + 3 + g))
                        act.wait_ge(sig.var_ok, at(2 * p))
                        nc.scalar.activation(retT[:, g, :], duo[2][:, g, :], ACT.Copy)\
                            .then_inc(sig.retT_ok, 1)
                if has(t):
                    split_hi(t, 0)
                if has(t - 1):
                    for i in range(2):
                        act.wait_ge(sig.rn_ps, at(t))
                        nc.scalar.activation(retT[:, i, :], duo[3][:, i, :], ACT.Square, scale=float(HD) ** -0.5)\
                            .then_inc(sig.sq_ok, 1)
                if isinstance(t, int) and t == 0:
                    split_hi(t, 1)
                    later_weights_hi()
                if has(t - 2):
                    p = t - 2
                    for k in range(KT):
                        act.wait_ge(sig.x1T_ps, at(p + 1))
                        act.wait_ge(sig.gu_ps, at(2 * FT * p))
                        act.wait_ge(sig.lgT_ps, at(p))
                        nc.scalar.activation(x1T[:, 0, k, :], duo[2][:, k, :], ACT.Copy)\
                            .then_inc(sig.x1T_hi, 1)
                if has(t) and not (isinstance(t, int) and t == 0):
                    split_hi(t, 1)
                if has(t - 2):
                    p = t - 2
                    act.wait_ge(sig.lgT_ps, at(p + 1))
                    act.wait_ge(sig.lg_ps, at(p))
                    nc.scalar.activation(lgT[:, :], duo[2][0:EXPERTS, 0, :], ACT.Copy).then_inc(sig.lgT_ok, 1)
                    for j in range(FT):
                        act.wait_ge(sig.gu_ps, at(2 * FT * p + 2 * j + 1))
                        act.wait_ge(sig.h_ok, at(FT * p + j - 1))
                        nc.scalar.activation(s_act[:, j % 2, :], duo[j % 2][:, 0, :], ACT.Silu)\
                            .then_inc(sig.sact_ok, 1)
                        if j:
                            h_hi(p, j - 1)
                    h_hi(p, FT - 1)
                if has(t - 1):
                    p = t - 1
                    for k in range(KT):
                        act.wait_ge(sig.yT_ps, at(p + 1))
                        act.wait_ge(sig.o_ps, at(2 * p))
                        nc.scalar.activation(yT[:, 0, k, :], duo[3][:, k, :], ACT.Copy)\
                            .then_inc(sig.yT_hi, 1)
                if has(t):
                    for q in range(TILES):
                        act.wait_ge(sig.vg_ok, at(TILES * t + q + 1))
                        act.wait_ge(sig.y_ok, at(t))
                        nc.scalar.activation(gate[:, q, :], vg[:, q, D:2 * D], ACT.Silu)\
                            .then_inc(sig.gate_ok, 1)
                if has(t + 1):
                    x_hi(t + 1)

            def later_weights_hi():
                act.wait_ge(sig.raw_in, 16 * 5)
                nc.scalar.activation(wo[:, 0, :, :], raw_o[:, :, :], ACT.Copy).then_inc(sig.w_hi, 1)
                nc.scalar.activation(wsgu[:, :, 0, :, :], raw_gu[:, :, :, :], ACT.Copy).then_inc(sig.w_hi, 1)
                nc.scalar.activation(wsd[:, 0, :, :], raw_d[:, :, :], ACT.Copy).then_inc(sig.w_hi, 1)
                act.wait_ge(sig.wrT_ps, 1)
                nc.scalar.activation(wr[:, 0, :, :], duo[2][:, 0, 0:KT * EXPERTS].rearrange("p (k e) -> p k e", k=KT),
                                     ACT.Copy).then_inc(sig.w_hi, 1)

            def split_hi(t, side):
                for e in range(2):
                    act.wait_ge(sig.turned_ok, at(4 * t + 2 * side + e + 1))
                    nc.scalar.activation(prod[:, side, 1 + e, :].bitcast(F32R), prod[:, side, 3 * e, :], ACT.Copy)\
                        .then_inc(sig.split_hi, 1)

            def h_hi(p, j):
                act.wait_ge(sig.h_ok, at(FT * p + j + 1))
                act.wait_ge(sig.dn_ps, at(2 * p))
                nc.scalar.activation(hT[:, 0, j, :], h[:, j % 2, :], ACT.Copy)\
                    .then_inc(sig.h_hi, 1)

            pipeline(act, step)

            def slot_step(s, r, u):
                if is_slot(s):
                    act.wait_ge(sig.eg_ps, at(2 * s + 1))
                    act.wait_ge(sig.eh_ok, at(s))
                    nc.scalar.activation(e_act[:, :], duo[r % 2][:, 0, :], ACT.Silu, scale=f32(seat[:, r, :])[:, 2:3])\
                        .then_inc(sig.e_act_ok, 1)
                    act.wait_ge(sig.ehT_ps, at(s + 1))
                    act.wait_ge(sig.ed_ps, at(s))
                    nc.scalar.activation(ehT[:, :, :], duo[2][:, 0, :].rearrange("p (f n) -> p f n", f=FT), ACT.Copy)\
                        .then_inc(sig.ehT_ok, 1)

            slot_pipeline(act, slot_step)

        @block.gpsimd
        def _(pool):
            nc.gpsimd.memset(minus_half[:, :], -0.5).then_inc(sig.zero_ok, 1)
            nc.gpsimd.memset(minus_one[:, :], -1.0).then_inc(sig.zero_ok, 1)
            nc.gpsimd.memset(inv_e[:, :], float(np.exp(-1.0))).then_inc(sig.zero_ok, 1)
            nc.gpsimd.memset(y[0:1, 0:2, :], 0.0).then_inc(sig.zero_ok, 1)
            pool.wait_ge(sig.zero_ok, 4)
            pool.dma_start(xz_d[TOKENS:TOKENS + 1, :], y[0:1, 0:2, :].rearrange("p q d -> p (q d)"))\
                .then_inc(sig.zrow_out, 16)
            pool.wait_ge(sig.c_in, at(16 * N_IN))

            def step(t):
                if has(t - 1):
                    p = t - 1
                    pool.wait_ge(sig.xres_in, at(16 * (p + 1)))
                    nc.gpsimd.tensor_tensor(x_res[:, :, :], x_res[:, :, :], over(bias_o[:, :], TILES),
                                            ALU.add).then_inc(sig.xb_ok, 1)
                if has(t):
                    for side in range(2):
                        pool.wait_ge(sig.prod_ok, at(4 * t + 2 * side + 2))
                        nc.gpsimd.tensor_tensor(prod[:, side, 0, :], prod[:, side, 0, :], prod[:, side, 1, :],
                                                ALU.subtract).then_inc(sig.turned_ok, 1)
                        nc.gpsimd.tensor_tensor(prod[:, side, 3, :], prod[:, side, 3, :], prod[:, side, 2, :],
                                                ALU.add).then_inc(sig.turned_ok, 1)
                if has(t - 1):
                    p = t - 1
                    pool.wait_ge(sig.var_ok, at(2 * p + 2))
                    apart(pool)
                    nc.gpsimd.tensor_scalar(var_e[:, :], var[:, :], EPS, None, ALU.add).then_inc(sig.eps_ok, 1)
                    pool.wait_ge(sig.eps_ok, at(p + 1))
                    pool.wait_ge(sig.rn_ok, at(2 * p))
                    nc.gpsimd.tensor_tensor(rstd[:, :], var_e[:, :], minus_half[:, :], ALU.pow).then_inc(sig.rstd_ok, 1)
                    pool.wait_ge(sig.rn_ok, at(2 * p + 2))
                    nc.gpsimd.tensor_tensor(y[:, :, :], y[:, :, :], over(norm_w[:, :], TILES), ALU.mult)\
                        .then_inc(sig.y_w, 1)
                    pool.wait_ge(sig.y_w, at(p + 1))
                    nc.gpsimd.tensor_tensor(y[:, :, :], y[:, :, :], over(norm_b[:, :], TILES), ALU.add)\
                        .then_inc(sig.y_b, 1)
                    pool.wait_ge(sig.y_b, at(p + 1))
                    pool.wait_ge(sig.gate_ok, at(TILES * (p + 1)))
                    nc.gpsimd.tensor_tensor(y[:, :, :], y[:, :, :], gate[:, :, :], ALU.mult).then_inc(sig.y_ok, 1)
                if has(t - 2):
                    take_seats(t - 2)
                if has(t - 1):
                    p = t - 1
                    pool.wait_ge(sig.mv_ok, at(TILES * (p + 1)))
                    apart(pool)
                    nc.gpsimd.tensor_scalar(ln_e[:, :], mv[:, :, 1], EPS, None, ALU.add).then_inc(sig.lne_ok, 1)
                    pool.wait_ge(sig.lne_ok, at(p + 1))
                    pool.wait_ge(sig.x1_ok, at(TILES * p))
                    nc.gpsimd.tensor_tensor(ln_r[:, :], ln_e[:, :], minus_half[:, 0:TILES], ALU.pow)\
                        .then_inc(sig.lnr_ok, 1)

            def take_seats(p):
                pool.wait_ge(sig.scat, at(16 * TILES * p))
                pool.wait_ge(sig.free_out, 16)
                tiles = slice(TILES * p, TILES * p + TILES) if isinstance(p, int) else bass.ds(TILES * p, TILES)
                nc.gpsimd.tensor_copy(stage[:, :, 0:2], seats[:, tiles, 0:2]).then_inc(sig.ids_ok, 1)
                pool.wait_ge(sig.route, at(ROUTE * p + 2))
                nc.gpsimd.tensor_tensor(powed[:, :], inv_e[:, :], top[:, :], ALU.pow).then_inc(sig.pow_ok, 1)
                pool.wait_ge(sig.pow_ok, at(p + 1))
                apart(pool)
                nc.gpsimd.tensor_scalar(powed1[:, :], powed[:, :], 1.0, None, ALU.add).then_inc(sig.pow1_ok, 1)
                pool.wait_ge(sig.pow1_ok, at(p + 1))
                nc.gpsimd.tensor_tensor(f32(stage[:, :, :])[:, :, 2], powed1[:, :], minus_one[:, :], ALU.pow)\
                    .then_inc(sig.score_ok, 1)
                pool.wait_ge(sig.ids_ok, at(p + 1))
                apart(pool)
                pool.wait_ge(sig.score_ok, at(p + 1))
                apart(pool)
                pool.wait_ge(sig.place_ok, at(p + 1))
                apart(pool)
                for q in range(TILES):
                    pool.indirect_dma_start(seat_d, bass.IndirectOffsetOnAxis(ap=place_i[:, q:q + 1], axis=0),
                                            stage[:, q, :], None).then_inc(sig.scat, 16)

            pipeline(pool, step)

            pool.wait_ge(sig.zrow_out, 16)
            pool.wait_ge(sig.plan_ok, 2)
            pool.wait_ge(sig.x1_out, 16 * PAIRS)
            pool.wait_ge(sig.zs_out, 16 * PAIRS)

            def gather(s, r, u):
                if is_slot(s):
                    pool.wait_ge(sig.sum_ok, at(s - RING + 1))
                    apart(pool)
                    pool.wait_ge(sig.seat_in[r], at(16 * (u + 1)))
                    apart(pool)
                    pool.indirect_dma_start(xz[:, r, :], None, xz_d,
                                            bass.IndirectOffsetOnAxis(ap=seat[:, r, 0:1], axis=0))\
                        .then_inc(sig.xz_in[r], 16)
                    pool.wait_ge(sig.out_done[r], at(16 * u))
                    apart(pool)
                    nc.gpsimd.tensor_copy(dest[:, r:r + 1], seat[:, r, 1:2]).then_inc(sig.dest_ok, 1)

            def slot_step(s, r, u):
                gather(s + 2, *ahead(r, u, 2))
                if is_slot(s - 1):
                    b, _ = ahead(r, u, -1)
                    pool.wait_ge(sig.mv2_ok, at(s))
                    apart(pool)
                    nc.gpsimd.tensor_scalar(ln2_e[:, :], mv2[:, 1:2], EPS, None, ALU.add).then_inc(sig.lne2_ok, 1)
                    pool.wait_ge(sig.lne2_ok, at(s))
                    pool.wait_ge(sig.of_ok, at(s - 1))
                    nc.gpsimd.tensor_tensor(ln2_r[:, :], ln2_e[:, :], minus_half[:, 0:1], ALU.pow)\
                        .then_inc(sig.lnr2_ok, 1)
                if is_slot(s - 1):
                    pool.wait_ge(sig.of_ok, at(s))
                    apart(pool)
                    pool.wait_ge(sig.dest_ok, at(s))
                    apart(pool)
                    if is_slot(s - 2):
                        c, turn = ahead(r, u, -2)
                        pool.wait_ge(sig.out_done[c], at(16 * (turn + 1)))
                        apart(pool)
                    pool.indirect_dma_start(out, bass.IndirectOffsetOnAxis(ap=dest[:, b:b + 1], axis=0),
                                            of[:, b % 2, :], None).then_inc(sig.out_done[b], 16)

            gather(0, 0, 0)
            gather(1, 1, 0)
            slot_pipeline(pool, slot_step)

        @block.vector
        def _(dve):
            def x_lo(t):
                for k in range(KT):
                    dve.wait_ge(sig.xT_hi, at(2 * t + k + 1))
                    dve.wait_ge(sig.vg_ps, at(TILES * t))
                    nc.vector.tensor_tensor(xT[:, 1, k, :], duo[3][:, k, :], f32(xT[:, 0, k, :]), ALU.subtract)\
                        .then_inc(sig.xT_lo, 1)

            x_lo(0)
            dve.wait_ge(sig.first_in, 16 * 4)
            dve.wait_ge(sig.wqk_in, 16 * 2)
            dve.wait_ge(sig.w_hi, 1)
            nc.vector.tensor_tensor(wqk[:, :, 1, :, :], raw_qk[:, :, :, :], f32(wqk[:, :, 0, :, :]), ALU.subtract)\
                .then_inc(sig.w_lo, 1)
            dve.wait_ge(sig.wvg_in, 16 * 2)
            dve.wait_ge(sig.c_in, at(16 * N_IN))
            v_heads = raw_vg[:, :, 0:D].rearrange("p k (h d) -> p k h d", d=HD)
            b_heads = bias_vg[:, 0:D].rearrange("p (h d) -> p h d", d=HD)
            nc.vector.tensor_reduce(mean_v[:, :, :], v_heads, X, ALU.add).then_inc(sig.center, 1)
            nc.vector.tensor_reduce(mean_b[:, :], b_heads, X, ALU.add).then_inc(sig.center, 1)
            dve.wait_ge(sig.center, at(2))
            for k in range(KT):
                nc.vector.scalar_tensor_tensor(out=v_heads[:, k], in0=each(mean_v[:, k, :], HD), scalar=-1.0 / HD,
                                               in1=v_heads[:, k], op0=ALU.mult, op1=ALU.add).then_inc(sig.center, 1)
            nc.vector.scalar_tensor_tensor(out=b_heads, in0=each(mean_b[:, :], HD), scalar=-1.0 / HD,
                                           in1=b_heads, op0=ALU.mult, op1=ALU.add).then_inc(sig.center, 1)
            dve.wait_ge(sig.w_hi, 2)
            nc.vector.tensor_tensor(wvg[:, 1, :, :], raw_vg[:, :, :], f32(wvg[:, 0, :, :]), ALU.subtract)\
                .then_inc(sig.w_lo, 1)

            def step(t):
                if has(t - 1):
                    p = t - 1
                    for j in range(8):
                        dve.wait_ge(sig.s_off, at(8 * p + j + 1))
                        dve.wait_ge(sig.av_ps, at(4 * p + j // 2 - 1))
                        src = duo[j % 2][:, :, :].rearrange("p h (b q) -> p h b q", q=P)[:, :, 0::3, :]
                        mask = bass.AP(causal[:, :].tensor, 0, [[P, P], [0, 2], [0, 2], [1, P]])
                        nc.vector.tensor_tensor(sims[:, j % 4, :, 0::2, :], src, mask, ALU.mult)\
                            .then_inc(sig.s_diag, 1)
                        if j == 1 and has(t - 2):
                            first_norm(t - 2)
                elif has(t - 2):
                    first_norm(t - 2)
                if has(t):
                    for s in range(4):
                        side, e = s // 2, s % 2
                        dve.wait_ge(sig.qk_ps, at(4 * t + s + 1))
                        dve.wait_ge(sig.rot_out, at(64 * (t - 1) + 32 * side + 32))
                        for f in range(2):
                            place_ = (0, 2)[f] if e == 0 else (3, 1)[f]
                            last = nc.vector.scalar_tensor_tensor(
                                out=prod[:, side, place_, :].rearrange("p (b n) -> p b n", b=2),
                                in0=duo[side][:, e, :].rearrange("p (b n) -> p b n", b=2),
                                scalar=bias_qk[:, side, e:e + 1],
                                in1=over(rot[:, 2 * side + f, :], 2), op0=ALU.add, op1=ALU.mult)
                        last.then_inc(sig.prod_ok, 1)
                    split_lo(t, 0)
                if has(t - 1):
                    p = t - 1
                    for i in range(2):
                        dve.wait_ge(sig.sq_ok, at(2 * p + i + 1))
                        dve.wait_ge(sig.eps_ok, at(p))
                        nc.vector.tensor_reduce(var[:, 16 * i:16 * i + 16],
                                                retT[:, i, :].rearrange("p (h d) -> p h d", d=HD), X, ALU.add)\
                            .then_inc(sig.var_ok, 1)
                if has(t - 2):
                    p = t - 2
                    for k in range(KT):
                        dve.wait_ge(sig.x1T_hi, at(KT * p + k + 1))
                        nc.vector.tensor_tensor(x1T[:, 1, k, :], duo[2][:, k, :], f32(x1T[:, 0, k, :]), ALU.subtract)\
                            .then_inc(sig.x1T_lo, 1)
                if has(t):
                    for q in range(TILES):
                        dve.wait_ge(sig.vg_ps, at(TILES * t + q + 1))
                        dve.wait_ge(sig.av_ps, at(4 * t))
                        dve.wait_ge(sig.gate_ok, at(TILES * t))
                        nc.vector.tensor_tensor(vg[:, q, :], duo[q // 2][:, q % 2, :], bias_vg[:, :], ALU.add)\
                            .then_inc(sig.vg_ok, 1)
                    split_lo(t, 1)
                if isinstance(t, int) and t == 0:
                    later_weights_lo()
                if has(t - 1):
                    p = t - 1
                    if isinstance(p, int) and p == 0:
                        dve.wait_ge(sig.zrow_out, 16)
                    for i in range(2):
                        dve.wait_ge(sig.rstd_ok, at(p + 1))
                        dve.wait_ge(sig.yT_ps, at(p))
                        nc.vector.tensor_tensor(
                            y[:, 2 * i:2 * i + 2, :].rearrange("p q (h d) -> p (q h) d", d=HD),
                            duo[3][:, i, :].rearrange("p (h d) -> p h d", d=HD),
                            each(rstd[:, 16 * i:16 * i + 16], HD), ALU.mult)\
                            .then_inc(sig.rn_ok, 1)
                if has(t - 2):
                    p = t - 2
                    for j in range(FT):
                        dve.wait_ge(sig.gu_ps, at(2 * FT * p + 2 * j + 2))
                        dve.wait_ge(sig.sact_ok, at(FT * p + j + 1))
                        dve.wait_ge(sig.h_hi, at(FT * p + j - 1))
                        dve.wait_ge(sig.h_lo, at(FT * p + j - 1))
                        nc.vector.tensor_tensor(h[:, j % 2, :], duo[j % 2][:, 1, :], s_act[:, j % 2, :], ALU.mult)\
                            .then_inc(sig.h_ok, 1)
                        if j:
                            h_lo(p, j - 1)
                        if j == 1:
                            choose(p)
                        if j == 2:
                            find_seats(p)
                    if isinstance(p, int) and p == PAIRS - 1:
                        plan_slots()
                    h_lo(p, FT - 1)
                if has(t - 1):
                    p = t - 1
                    for k in range(KT):
                        dve.wait_ge(sig.yT_hi, at(KT * p + k + 1))
                        nc.vector.tensor_tensor(yT[:, 1, k, :], duo[3][:, k, :], f32(yT[:, 0, k, :]), ALU.subtract)\
                            .then_inc(sig.yT_lo, 1)
                if is_last(t):
                    output_stats(t - 1)
                if has(t - 2):
                    shared_sum(t - 2)
                if has(t - 1) and not is_last(t):
                    output_stats(t - 1)
                if has(t + 1):
                    x_lo(t + 1)

            def shared_sum(p):
                for i in range(2):
                    dve.wait_ge(sig.dn_ps, at(2 * p + i + 1))
                    dve.wait_ge(sig.x1_ok, at(TILES * (p + 1)))
                    dve.wait_ge(sig.zs_out, at(16 * p))
                    nc.vector.tensor_tensor(
                        zs[:, 2 * i:2 * i + 2, :], duo[2][:, i, :].rearrange("p (q n) -> p q n", q=2),
                        x1[:, 2 * i:2 * i + 2, :], ALU.add)\
                        .then_inc(sig.zs_ok, 1)

            def output_stats(p):
                for i in range(2):
                    dve.wait_ge(sig.o_ps, at(2 * p + i + 1))
                    dve.wait_ge(sig.xb_ok, at(p + 1))
                    nc.vector.tensor_tensor(
                        x_res[:, 2 * i:2 * i + 2, :], duo[0][:, i, :].rearrange("p (q n) -> p q n", q=2),
                        x_res[:, 2 * i:2 * i + 2, :], ALU.add)\
                        .then_inc(sig.z_ok, 1)
                for q in range(TILES):
                    dve.wait_ge(sig.z_ok, at(2 * p + q // 2 + 1))
                    nc.vector.bn_stats(stats[:, q, :], x_res[:, q, :]).then_inc(sig.st_ok, 1)
                for q in range(TILES):
                    dve.wait_ge(sig.st_ok, at(TILES * p + q + 1))
                    apart(dve)
                    dve.wait_ge(sig.lne_ok, at(p))
                    apart(dve)
                    nc.vector.bn_aggr(mv[:, q, :], stats[:, q, :]).then_inc(sig.mv_ok, 1)

            def first_norm(p):
                for q in range(TILES):
                    dve.wait_ge(sig.lnr_ok, at(p + 1))
                    dve.wait_ge(sig.x1_out, at(16 * p))
                    dve.wait_ge(sig.x1T_ps, at(p))
                    dve.wait_ge(sig.zs_ok, at(2 * p))
                    nc.vector.tensor_scalar(x1[:, q, :], x_res[:, q, :], mv[:, q, 0:1], ln_r[:, q:q + 1],
                                            ALU.subtract, ALU.mult).then_inc(sig.x1_ok, 1)

            def later_weights_lo():
                dve.wait_ge(sig.raw_in, 16 * 5)
                for n, (lo_, raw_, hi_) in enumerate((
                        (wo[:, 1, :, :], raw_o[:, :, :], wo[:, 0, :, :]),
                        (wsgu[:, :, 1, :, :], raw_gu[:, :, :, :], wsgu[:, :, 0, :, :]),
                        (wsd[:, 1, :, :], raw_d[:, :, :], wsd[:, 0, :, :]),
                        (wr[:, 1, :, :], duo[2][:, 0, 0:KT * EXPERTS].rearrange("p (k e) -> p k e", k=KT),
                         wr[:, 0, :, :]))):
                    dve.wait_ge(sig.w_hi, n + 3)
                    nc.vector.tensor_tensor(lo_, raw_, f32(hi_), ALU.subtract).then_inc(sig.w_lo, 1)

            def split_lo(t, side):
                for e in range(2):
                    dve.wait_ge(sig.split_hi, at(4 * t + 2 * side + e + 1))
                    nc.vector.tensor_tensor(prod[:, side, 3 * e, :], prod[:, side, 3 * e, :], prod[:, side, 1 + e, :],
                                            ALU.subtract).then_inc(sig.split_lo, 1)

            def h_lo(p, j):
                dve.wait_ge(sig.h_hi, at(FT * p + j + 1))
                nc.vector.tensor_tensor(hT[:, 1, j, :], h[:, j % 2, :], f32(hT[:, 0, j, :]), ALU.subtract)\
                    .then_inc(sig.h_lo, 1)

            def plan_slots():
                dve.wait_ge(sig.route, ROUTE * PAIRS)
                nc.vector.tensor_tensor(count[:, :], start[:, TILES, :], region[:, :], ALU.subtract).then_inc(sig.plan, 1)
                nc.vector.memset(zero[:, :], 0.0).then_inc(sig.plan, 1)
                dve.wait_ge(sig.plan, 2)
                nc.vector.tensor_scalar(count_up[:, :], count[:, :], float(P - 1), None, ALU.add).then_inc(sig.plan, 1)
                dve.wait_ge(sig.plan, 3)
                nc.vector.tensor_scalar(slots_i[:, :], count_up[:, :], 7, None, ALU.logical_shift_right)\
                    .then_inc(sig.plan, 1)
                dve.wait_ge(sig.plan, 4)
                nc.vector.tensor_copy(slots_f[:, :], slots_i[:, :]).then_inc(sig.plan, 1)
                dve.wait_ge(sig.plan, 5)
                nc.vector.tensor_tensor_scan(slot_end[:, :], slots_f[:, :], zero[:, :], 0.0, ALU.add, ALU.add)\
                    .then_inc(sig.plan, 1)
                nc.vector.tensor_scalar(skip[:, :], slots_f[:, :], -float(P), float(TOKENS), ALU.mult, ALU.add)\
                    .then_inc(sig.plan, 1)
                dve.wait_ge(sig.plan, 7)
                nc.vector.tensor_tensor(passed[:, :, :], each(slot_no[:, :], EXPERTS - 1),
                                        over(slot_end[:, 0:EXPERTS - 1], SLOTS), ALU.is_ge).then_inc(sig.plan, 1)
                dve.wait_ge(sig.plan, 8)
                nc.vector.tensor_reduce(slot_e[:, :], passed[:, :, :], X, ALU.add).then_inc(sig.plan, 1)
                nc.vector.tensor_tensor(skipped[:, :, :], passed[:, :, :], over(skip[:, 0:EXPERTS - 1], SLOTS), ALU.mult)\
                    .then_inc(sig.plan, 1)
                dve.wait_ge(sig.plan, 10)
                nc.vector.tensor_copy(slot_ei[:, :], slot_e[:, :]).then_inc(sig.plan_ok, 1)
                nc.vector.tensor_reduce(slot_r[:, :], skipped[:, :, :], X, ALU.add).then_inc(sig.plan, 1)
                dve.wait_ge(sig.plan, 11)
                nc.vector.scalar_tensor_tensor(out=slot_row[:, :], in0=slot_no[:, :], scalar=float(P), in1=slot_r[:, :],
                                               op0=ALU.mult, op1=ALU.add).then_inc(sig.plan, 1)
                dve.wait_ge(sig.plan, 12)
                nc.vector.tensor_copy(slot_ri[:, :], slot_row[:, :]).then_inc(sig.plan_ok, 1)

            def choose(p):
                dve.wait_ge(sig.lg_ps, at(p + 1))
                nc.vector.tensor_copy(logits[:, :, :], duo[2][:, 1, 0:TILES * EXPERTS].rearrange("p (q e) -> p q e", e=EXPERTS))\
                    .then_inc(sig.route, 1)
                dve.wait_ge(sig.route, at(ROUTE * p + 1))
                dve.wait_ge(sig.pow_ok, at(p))
                nc.vector.tensor_reduce(top[:, :], logits[:, :, :], X, ALU.max).then_inc(sig.route, 1)
                dve.wait_ge(sig.route, at(ROUTE * p + 2))
                nc.vector.tensor_tensor(hot[:, :, :], logits[:, :, :], each(top[:, :], EXPERTS), ALU.is_equal)\
                    .then_inc(sig.route, 1)
                dve.wait_ge(sig.route, at(ROUTE * p + 3))
                nc.vector.tensor_tensor(ranked[:, :, :], hot[:, :, :], over(priority[:, :], TILES), ALU.mult)\
                    .then_inc(sig.route, 1)
                dve.wait_ge(sig.route, at(ROUTE * p + 4))
                nc.vector.tensor_reduce(first_of[:, :], ranked[:, :, :], X, ALU.max).then_inc(sig.route, 1)
                dve.wait_ge(sig.route, at(ROUTE * p + 5))
                nc.vector.tensor_tensor(hot[:, :, :], ranked[:, :, :], each(first_of[:, :], EXPERTS), ALU.is_equal)\
                    .then_inc(sig.hot_ok, 1)
                nc.vector.tensor_copy(start[:, 0, :], start[:, TILES, :]).then_inc(sig.route, 1)

            def find_seats(p):
                dve.wait_ge(sig.rank_ps, at(p + 1))
                totals = duo[2][:, 1, 2 * TILES * EXPERTS:3 * TILES * EXPERTS].rearrange("p (q e) -> p q e", e=EXPERTS)
                ranks = duo[2][:, 1, TILES * EXPERTS:2 * TILES * EXPERTS].rearrange("p (q e) -> p q e", e=EXPERTS)
                for q in range(TILES):
                    dve.wait_ge(sig.route, at(ROUTE * p + 6 + q))
                    nc.vector.tensor_tensor(start[:, q + 1, :], start[:, q, :], totals[:, q, :], ALU.add)\
                        .then_inc(sig.route, 1)
                dve.wait_ge(sig.route, at(ROUTE * p + 10))
                nc.vector.tensor_tensor(spot[:, :, :], ranks, start[:, 0:TILES, :], ALU.add).then_inc(sig.route, 1)
                dve.wait_ge(sig.route, at(ROUTE * p + 11))
                dve.wait_ge(sig.hot_ok, at(p + 1))
                nc.vector.tensor_tensor(spot[:, :, :], spot[:, :, :], hot[:, :, :], ALU.mult).then_inc(sig.route, 1)
                dve.wait_ge(sig.route, at(ROUTE * p + 12))
                nc.vector.tensor_reduce(place[:, :], spot[:, :, :], X, ALU.add).then_inc(sig.route, 1)
                dve.wait_ge(sig.route, at(ROUTE * p + 13))
                dve.wait_ge(sig.scat, at(16 * TILES * p))
                nc.vector.tensor_copy(place_i[:, :], place[:, :]).then_inc(sig.place_ok, 1)

            pipeline(dve, step)

            def rows_in(s):
                if is_slot(s):
                    dve.wait_ge(sig.xsT_ps, at(s + 1))
                    dve.wait_ge(sig.eg_ps, at(2 * s))
                    nc.vector.tensor_copy(xsT[:, :, :], duo[3][:, 0, 0:D].rearrange("p (k n) -> p k n", k=KT))\
                        .then_inc(sig.xsT_ok, 1)

            def slot_step(s, r, u):
                if is_slot(s):
                    dve.wait_ge(sig.eg_ps, at(2 * s + 2))
                    dve.wait_ge(sig.e_act_ok, at(s + 1))
                    dve.wait_ge(sig.ehT_ps, at(s))
                    nc.vector.scalar_tensor_tensor(out=eh[:, :], in0=duo[r % 2][:, 1, :], scalar=f32(seat[:, r, :])[:, 2:3],
                                                   in1=e_act[:, :], op0=ALU.mult, op1=ALU.mult).then_inc(sig.eh_ok, 1)
                rows_in(s + 1)
                if is_slot(s - 1):
                    b, turn = ahead(r, u, -1)
                    dve.wait_ge(sig.ed_ps, at(s))
                    dve.wait_ge(sig.xz_in[b], at(16 * (turn + 1)))
                    dve.wait_ge(sig.out_done[(b - 2) % RING], at(16 * (turn + 1 if b >= 2 else turn)))
                    nc.vector.tensor_tensor(of[:, b % 2, :], duo[2][:, 1, 0:D], xz[:, b, D:2 * D], ALU.add)\
                        .then_inc(sig.sum_ok, 1)
                    dve.wait_ge(sig.sum_ok, at(s))
                    nc.vector.bn_stats(st2[:, :], of[:, b % 2, :]).then_inc(sig.st2_ok, 1)
                    dve.wait_ge(sig.st2_ok, at(s))
                    apart(dve)
                    nc.vector.bn_aggr(mv2[:, :], st2[:, :]).then_inc(sig.mv2_ok, 1)
                    dve.wait_ge(sig.mv2_ok, at(s))
                    dve.wait_ge(sig.lnr2_ok, at(s))
                    nc.vector.tensor_scalar(of[:, b % 2, :], of[:, b % 2, :], mv2[:, 0:1], ln2_r[:, :],
                                            ALU.subtract, ALU.mult).then_inc(sig.of_ok, 1)

            rows_in(0)
            slot_pipeline(dve, slot_step)

        @block.tensor
        def _(pe):
            mm = nc.tensor.matmul

            def three(out_, left, right, kt, start=True, stop=True):
                for k in range(kt):
                    for n, (a, b) in enumerate(PASSES):
                        last = mm(out_, left(a, k), right(b, k), start=start and k == 0 and n == 0,
                                  stop=stop and k == kt - 1 and n == len(PASSES) - 1)
                return last

            def x_transposes(t):
                pe.wait_ge(sig.xin, at(16 * (t + 1)))
                pe.wait_ge(sig.yT_hi, at(KT * (t - 1)))
                pe.wait_ge(sig.yT_lo, at(KT * (t - 1)))
                for k in range(KT):
                    for q in range(TILES):
                        last = nc.tensor.transpose(duo[3][:, k, q * P:(q + 1) * P], x_in[:, q, k * P:(k + 1) * P], ident[:, :])
                last.then_inc(sig.xT_ps, 1)

            pe.wait_ge(sig.first_in, 16 * 4)
            x_transposes(0)
            pe.wait_ge(sig.w_lo, 1)
            def similarities(p, j):
                b, hp = j // 4, j % 4
                if j < 2:
                    pe.wait_ge(sig.vg_ok, at(TILES * (p + 1)))
                    pe.wait_ge(sig.sact_ok, at(FT * (p - 1)))
                    pe.wait_ge(sig.h_ok, at(FT * (p - 1)))
                    pe.wait_ge(sig.z_ok, at(2 * p))
                else:
                    pe.wait_ge(sig.s_diag, at(8 * p + j - 1))
                for i in range(2):
                    head = 2 * hp + i
                    for kb in range(2):
                        lo = SEQ * b + P * kb
                        last = mm(duo[j % 2][:, i, SEQ * kb:SEQ * (kb + 1)], stack[1][:, head, lo:lo + P],
                                  stack[0][:, head, SEQ * b:SEQ * (b + 1)], start=True, stop=True)
                last.then_inc(sig.s_ps, 1)

            def values(p, a):
                b, g = a // 2, a % 2
                pe.wait_ge(sig.s_diag, at(8 * p + 2 * a + 2))
                pe.wait_ge(sig.s_off, at(8 * p + 2 * a + 2))
                if a < 2:
                    pe.wait_ge(sig.zs_ok, at(2 * (p - 1)))
                for kb in range(2):
                    for i in range(4):
                        ring, half = (2 * a + i // 2) % 4, i % 2
                        lo = SEQ * b + P * kb
                        rhs = sims[:, ring, half, 0:2, :] if kb == 0 else sims[:, ring, half, 2:3, :]
                        last = mm(duo[2][HD * i:HD * (i + 1), g, lo:SEQ * (b + 1)],
                                  vg[:, 2 * b + kb, HD * (4 * g + i):HD * (4 * g + i + 1)],
                                  rhs.rearrange("p b q -> p (b q)"), start=(kb == 0), stop=(kb == 1),
                                  skip_group_check=True)
                last.then_inc(sig.av_ps, 1)

            def step(t):
                if has(t - 1):
                    p = t - 1
                    pe.wait_ge(sig.stack_in, at(192 * (p + 1)))
                    for j in range(8):
                        similarities(p, j)
                        if j in (3, 5, 7):
                            values(p, (j - 3) // 2)
                    values(p, 3)
                if has(t):
                    for s in range(4):
                        side, e = s // 2, s % 2
                        pe.wait_ge(sig.xT_hi, at(KT * (t + 1)))
                        pe.wait_ge(sig.xT_lo, at(KT * (t + 1)))
                        pe.wait_ge(sig.s_diag, at(8 * t))
                        three(duo[side][:, e, :], lambda part, k: wqk[:, side, part, k, e::2],
                              lambda part, k: xT[:, part, k, :], KT).then_inc(sig.qk_ps, 1)
                if has(t - 1):
                    p = t - 1
                    pe.wait_ge(sig.retT_ok, at(2 * (p + 1)))
                    pe.wait_ge(sig.xT_lo, at(KT * (p + 2) if has(p + 1) else KT * (p + 1)))
                    for g in range(2):
                        for q in range(TILES):
                            last = nc.tensor.transpose(duo[3][:, q // 2, D * (q % 2) + P * g:D * (q % 2) + P * (g + 1)],
                                                       retT[:, g, q * P:(q + 1) * P], ident[:, :])
                    last.then_inc(sig.rn_ps, 1)
                if has(t - 2):
                    p = t - 2
                    pe.wait_ge(sig.x1_ok, at(TILES * (p + 1)))
                    pe.wait_ge(sig.retT_ok, at(2 * (p + 2) if has(p + 1) else 2 * (p + 1)))
                    pe.wait_ge(sig.zs_ok, at(2 * p))
                    for k in range(KT):
                        for q in range(TILES):
                            last = nc.tensor.transpose(duo[2][:, k, q * P:(q + 1) * P], x1[:, q, k * P:(k + 1) * P], ident[:, :])
                    last.then_inc(sig.x1T_ps, 1)
                if isinstance(t, int) and t == 0:
                    pe.wait_ge(sig.w_lo, 2)
                if has(t):
                    for q in range(TILES):
                        pe.wait_ge(sig.prod_ok, at(4 * t + q + 1))
                        three(duo[q // 2][:, q % 2, :], lambda part, k: xT[:, part, k, q * P:(q + 1) * P],
                              lambda part, k: wvg[:, part, k, :], KT).then_inc(sig.vg_ps, 1)
                if isinstance(t, int) and t == 0:
                    pe.wait_ge(sig.raw_in, 16 * 5)
                    for k in range(KT):
                        last = nc.tensor.transpose(duo[2][:, 0, k * EXPERTS:(k + 1) * EXPERTS], raw_r[:, k * P:(k + 1) * P],
                                                   ident[0:EXPERTS, 0:EXPERTS])
                    last.then_inc(sig.wrT_ps, 1)
                if isinstance(t, int) and t == 1:
                    pe.wait_ge(sig.w_lo, 6)
                    pe.wait_ge(sig.c_in, 16 * N_IN)
                if has(t - 2):
                    p = t - 2
                    pe.wait_ge(sig.x1T_hi, at(KT * (p + 1)))
                    pe.wait_ge(sig.x1T_lo, at(KT * (p + 1)))
                    three(duo[2][0:EXPERTS, 0, :], lambda part, k: wr[:, part, k, :],
                          lambda part, k: x1T[:, part, k, :], KT).then_inc(sig.lgT_ps, 1)
                    for j in range(FT):
                        if j == 2:
                            pe.wait_ge(sig.lgT_ok, at(p + 1))
                            apart(pe)
                            for q in range(TILES):
                                last = nc.tensor.transpose(duo[2][:, 1, q * EXPERTS:(q + 1) * EXPERTS],
                                                           lgT[:, q * P:(q + 1) * P], ident[0:EXPERTS, 0:EXPERTS])
                            last.then_inc(sig.lg_ps, 1)
                        if j == 3:
                            pe.wait_ge(sig.hot_ok, at(p + 1))
                            w = TILES * EXPERTS
                            flat = hot[:, :, :].rearrange("p t e -> p (t e)")
                            mm(duo[2][:, 1, w:2 * w], before[:, :], flat, start=True, stop=True)
                            mm(duo[2][:, 1, 2 * w:3 * w], ones[:, :], flat, start=True, stop=True)\
                                .then_inc(sig.rank_ps, 1)
                        if j < 2:
                            if has(t):
                                pe.wait_ge(sig.vg_ok, at(TILES * (t + 1)))
                            if has(t - 1):
                                pe.wait_ge(sig.s_diag, at(8 * t))
                            pe.wait_ge(sig.z_ok, at(2 * (p + 1)))
                        else:
                            pe.wait_ge(sig.sact_ok, at(FT * p + j - 1))
                            pe.wait_ge(sig.h_ok, at(FT * p + j - 1))
                        for i in range(2):
                            three(duo[j % 2][:, i, :], lambda part, k: wsgu[:, i, part, k, j * P:(j + 1) * P],
                                  lambda part, k: x1T[:, part, k, :], KT).then_inc(sig.gu_ps, 1)
                if has(t - 1):
                    p = t - 1
                    pe.wait_ge(sig.y_ok, at(p + 1))
                    pe.wait_ge(sig.rn_ok, at(2 * (p + 1)))
                    for k in range(KT):
                        for q in range(TILES):
                            last = nc.tensor.transpose(duo[3][:, k, q * P:(q + 1) * P], y[:, q, k * P:(k + 1) * P], ident[:, :])
                    last.then_inc(sig.yT_ps, 1)
                if is_last(t):
                    output(t - 1)
                if has(t - 2):
                    shared_down(t - 2)
                if has(t - 1) and not is_last(t):
                    output(t - 1)
                if has(t + 1):
                    x_transposes(t + 1)

            def shared_down(p):
                pe.wait_ge(sig.h_hi, at(FT * (p + 1)))
                pe.wait_ge(sig.h_lo, at(FT * (p + 1)))
                pe.wait_ge(sig.route, at(ROUTE * p + 11))
                for q in range(TILES):
                    last = three(duo[2][:, q // 2, D * (q % 2):D * (q % 2 + 1)],
                                 lambda part, f: hT[:, part, f, q * P:(q + 1) * P],
                                 lambda part, f: wsd[:, part, f, :], FT)
                    if q % 2:
                        last.then_inc(sig.dn_ps, 1)

            def output(p):
                pe.wait_ge(sig.yT_hi, at(KT * (p + 1)))
                pe.wait_ge(sig.yT_lo, at(KT * (p + 1)))
                if has(p + 1):
                    pe.wait_ge(sig.vg_ok, at(TILES * (p + 2)))
                if has(p - 1):
                    pe.wait_ge(sig.h_ok, at(FT * p))
                pe.wait_ge(sig.s_diag, at(8 * (p + 1)))
                for q in range(TILES):
                    last = three(duo[0][:, q // 2, D * (q % 2):D * (q % 2 + 1)],
                                 lambda part, k: yT[:, part, k, q * P:(q + 1) * P],
                                 lambda part, k: wo[:, part, k, :], KT)
                    if q % 2:
                        last.then_inc(sig.o_ps, 1)

            pipeline(pe, step)

            def slot_transposes(s, r, u):
                if is_slot(s):
                    pe.wait_ge(sig.xz_in[r], at(16 * (u + 1)))
                    pe.wait_ge(sig.xsT_ok, at(s))
                    for k in range(KT):
                        last = nc.tensor.transpose(duo[3][:, 0, k * P:(k + 1) * P], xz[:, r, k * P:(k + 1) * P], ident[:, :])
                    last.then_inc(sig.xsT_ps, 1)

            gu_flat = w_gu[:, :, :, :].rearrange("p e k n -> p (e k n)")
            dn_flat = w_dn[:, :, :, :].rearrange("p e f n -> p (e f n)")

            def expert_of(s):
                return pe.value_load(slot_ei[0:1, one(s)], min_val=0, max_val=EXPERTS - 1)

            def slot_step(s, r, u):
                if is_slot(s):
                    pe.wait_ge(sig.xsT_ok, at(s + 1))
                    apart(pe)
                    pe.wait_ge(sig.eh_ok, at(s - 1))
                    apart(pe)
                    e = expert_of(s)
                    for half in range(2):
                        for k in range(KT):
                            last = mm(duo[r % 2][:, half, :], xsT[:, k, :],
                                      gu_flat[:, bass.ds(e * (KT * 2 * FF) + (k * 2 + half) * FF, FF)],
                                      start=(k == 0), stop=(k == KT - 1))
                        last.then_inc(sig.eg_ps, 1)
                slot_transposes(s + 1, *ahead(r, u, 1))
                if is_slot(s - 1):
                    pe.wait_ge(sig.ehT_ok, at(s))
                    apart(pe)
                    pe.wait_ge(sig.sum_ok, at(s - 1))
                    apart(pe)
                    e = expert_of(s - 1)
                    for f in range(FT):
                        last = mm(duo[2][:, 1, 0:D], ehT[:, f, :], dn_flat[:, bass.ds(e * (FT * D) + f * D, D)],
                                  start=(f == 0), stop=(f == FT - 1))
                    last.then_inc(sig.ed_ps, 1)
                if is_slot(s):
                    pe.wait_ge(sig.eh_ok, at(s + 1))
                    pe.wait_ge(sig.ehT_ok, at(s))
                    for f in range(FT):
                        last = nc.tensor.transpose(duo[2][:, 0, f * P:(f + 1) * P], eh[:, f * P:(f + 1) * P], ident[:, :])
                    last.then_inc(sig.ehT_ps, 1)

            pe.wait_ge(sig.plan_ok, 2)
            pe.wait_ge(sig.ew_in, 16 * 2 * EXPERTS)
            slot_transposes(0, 0, 0)
            slot_pipeline(pe, slot_step)


def tables():
    f = np.float32
    start, stop = f(0.0), f(1.0)
    xs_ = np.linspace(start, stop, HALF, dtype=f)
    theta = (f(1.0) / np.power(f(10000.0), xs_)).astype(f)
    angle = (np.arange(SEQ, dtype=f)[None, :] * theta[:, None]).astype(f).astype(np.float64)
    gamma = (f(1.0) - np.exp(np.linspace(f(np.log(1 / 32)), f(np.log(1 / 64)), HEADS, dtype=f)).astype(f)).astype(f)
    n = np.arange(SEQ, dtype=np.float64)
    decay = gamma.astype(np.float64)[:, None] ** n[None, :]
    rotation = np.zeros((HEADS, HALF, 4, SEQ))
    for i, table in enumerate((np.cos(angle), np.sin(angle))):
        rotation[:, :, i] = table[None] * decay[:, None]
        rotation[:, :, 2 + i] = table[None] / decay[:, None] / np.sqrt(float(HD))
    r = np.arange(P)
    squares = np.zeros((P, 4 * P + EXPERTS + SLOTS + EXPERTS), f)
    squares[:, 0:P] = np.eye(P)
    squares[:, P:2 * P] = r[None, :] >= r[:, None]
    squares[:, 2 * P:3 * P] = r[:, None] < r[None, :]
    squares[:, 3 * P:4 * P] = 1.0
    squares[:, 4 * P:4 * P + EXPERTS] = EXPERTS - np.arange(EXPERTS)
    squares[:, 4 * P + EXPERTS:4 * P + EXPERTS + SLOTS] = np.arange(SLOTS)
    squares[:, 4 * P + EXPERTS + SLOTS:] = TOKENS * np.arange(EXPERTS)
    token_seats = np.zeros((P, NTILE, SEAT), np.int32)
    token_seats[:, :, 0:2] = (np.arange(NTILE)[None, :] * P + r[:, None])[:, :, None]
    free_seats = np.zeros((SEATS, SEAT), np.int32)
    free_seats[:, 0] = TOKENS
    free_seats[:, 1] = TOKENS + np.arange(SEATS) % P
    return (rotation.reshape(P, 4 * SEQ).astype(f), squares, token_seats.reshape(P, NTILE * SEAT), free_seats)


_INS = ["L0_attn_x", "L0_attn_w_q", "L0_attn_b_q", "L0_attn_w_k", "L0_attn_b_k", "L0_attn_w_v", "L0_attn_b_v",
        "L0_attn_w_g", "L0_attn_b_g", "L0_attn_w_o", "L0_attn_b_o", "L0_attn_gn_weight", "L0_attn_gn_bias",
        "L0_ffn_router_w", "L0_ffn_gate_up_proj", "L0_ffn_down_proj", "L0_ffn_shared_gate_w",
        "L0_ffn_shared_up_w", "L0_ffn_shared_down_w"]


def kernel(**inputs):
    import concourse.bacc as bacc
    from concourse.bass_utils import run_bass_kernel_spmd

    nc = bacc.Bacc("TRN2", target_bir_lowering=False, num_devices=1)
    arrays, args = {}, []

    def give(name, a):
        arrays[name] = a
        args.append(nc.dram_tensor(name, a.shape, mybir.dt.from_np(a.dtype), kind="ExternalInput").ap())

    for name in _INS:
        a = np.ascontiguousarray(inputs[name])
        give(name, a.reshape(SEQS * SEQ, D) if name == "L0_attn_x" else a)
    for name, table in zip(("rotation", "squares", "token_seats", "free_seats"), tables()):
        give(name, table)
    args.append(nc.dram_tensor("out_rows", (TOKENS + P, D), F32, kind="ExternalOutput").ap())
    build(nc, *args)
    r = run_bass_kernel_spmd(nc, [arrays], core_ids=[0])
    return r.results[0]["out_rows"][:TOKENS].reshape(SEQS, SEQ, D)
```

```python
from contextlib import ExitStack

import numpy as np
import concourse.bass as bass
from concourse import mybir

F32 = mybir.dt.float32
F32R = mybir.dt.float32r
I32 = mybir.dt.int32
ALU = mybir.AluOpType
ACT = mybir.ActivationFunctionType
X = mybir.AxisListType.X

P = 128
SEQS, SEQ, D = 16, 256, 256
HEADS = 8
HD = D // HEADS
HALF = HD // 2
PAIRS = SEQS // 2
TOK = 2 * SEQ
TILES = TOK // P
NTILE = SEQS * SEQ // P
KT = D // P
EXPERTS, FF = 8, 512
FT = FF // P
SLOTS = NTILE + EXPERTS - 1
TOKENS = SEQS * SEQ
RING = 4
SEATS = (EXPERTS - 1) * TOKENS + SLOTS * P
SEAT = 3
EPS = 1e-5
N_IN = 11
ROUTE = 13
PASSES = ((0, 0), (0, 1), (1, 0))


def build(nc, x, w_q, b_q, w_k, b_k, w_v, b_v, w_g, b_g, w_o, b_o, gn_w, gn_b, router_w,
          gate_up, down, sh_gate, sh_up, sh_down, rotation, squares, token_seats, free_seats, out):
    ctx = ExitStack()
    with ctx:
        def scratch(name, shape, dt=F32):
            return nc.dram_tensor(name, shape, dt, kind="Internal").ap()

        def f32(ap):
            return ap.bitcast(F32)

        def tensors(stack):
            return lambda name, shape, dt=F32: stack.enter_context(nc.sbuf_tensor(name, shape, dt))

        rot_d = scratch("rot_d", [2, 2, 2, P, TOK])
        x1_d = scratch("x1_d", [TOKENS + 1, D])
        xz_d = scratch("xz_d", [TOKENS + 1, 2 * D])
        seat_d = scratch("seat_d", [SEATS, SEAT], I32)

        sb = tensors(ctx)
        ident = sb("ident", [P, P])
        causal = sb("causal", [P, P])
        before = sb("before", [P, P])
        ones = sb("ones", [P, P])
        priority = sb("priority", [P, EXPERTS])
        slot_no = sb("slot_no", [P, SLOTS])
        minus_half = sb("minus_half", [P, TILES * HEADS])
        bias_qk = sb("bias_qk", [P, 2, 2])
        bias_vg = sb("bias_vg", [P, 2 * D])
        bias_o = sb("bias_o", [P, D])
        norm_w = sb("norm_w", [P, D])
        norm_b = sb("norm_b", [P, D])
        wr = sb("wr", [P, 2, KT, EXPERTS], F32R)

        seats = sb("seats", [P, NTILE, SEAT], I32)
        stage = sb("stage", [P, TILES, SEAT], I32)
        place_i = sb("place_i", [P, TILES], I32)
        logits = sb("logits", [P, TILES, EXPERTS])
        top = sb("top", [P, TILES])
        hot = sb("hot", [P, TILES, EXPERTS])
        ranked = sb("ranked", [P, TILES, EXPERTS])
        first_of = sb("first_of", [P, TILES])
        start = sb("start", [P, TILES + 1, EXPERTS])
        spot = sb("spot", [P, TILES, EXPERTS])
        place = sb("place", [P, TILES])
        minus_one = sb("minus_one", [P, TILES])
        inv_e = sb("inv_e", [P, TILES])
        powed = sb("powed", [P, TILES])
        powed1 = sb("powed1", [P, TILES])
        zero = sb("zero", [P, EXPERTS])
        region = sb("region", [P, EXPERTS])

        seat = sb("seat", [P, RING, SEAT], I32)
        dest = sb("dest", [P, RING], I32)

        places = ExitStack()
        with places:
            p_sb = tensors(places)
            retT = p_sb("retT", [P, 2, TOK])
            y = p_sb("y", [P, TILES, D])
            yT = p_sb("yT", [P, 2, KT, TOK], F32R)
            x_res = p_sb("x_res", [P, TILES, D])
            x1T = p_sb("x1T", [P, 2, KT, TOK], F32R)
            x1 = p_sb("x1", [P, TILES, D])
            wqk = p_sb("wqk", [P, 2, 2, KT, D], F32R)
            wvg = p_sb("wvg", [P, 2, KT, 2 * D], F32R)
            stack = [p_sb("stack_q", [96, HEADS, TOK], F32R),
                     p_sb("stack_k", [96, HEADS, TOK], F32R)]
            prod = p_sb("prod", [P, 2, 4, TOK])
            vg = p_sb("vg", [P, TILES, 2 * D])
            xT = p_sb("xT", [P, 2, KT, TOK], F32R)
            sims = p_sb("sims", [P, 4, 2, 3, P])
            x_in = p_sb("x_in", [P, TILES, D])
            rot = p_sb("rot", [P, 4, SEQ])
            wo = p_sb("wo", [P, 2, KT, D], F32R)
            wsgu = p_sb("wsgu", [P, 2, 2, KT, FF], F32R)
            wsd = p_sb("wsd", [P, 2, FT, D], F32R)
        sb = tensors(ctx)
        w_dn = sb("w_dn", [P, EXPERTS, FT, D])
        w_gu = sb("w_gu", [P, EXPERTS, KT, 2 * FF])
        w_gu_hi = sb("w_gu_hi", [P, EXPERTS, KT, 2 * FF], F32R)

        first = ExitStack()
        with first:
            sb = tensors(first)
            with ExitStack() as early:
                e_sb = tensors(early)
                raw_qk = e_sb("raw_qk", [P, 2, KT, D])
                raw_vg = e_sb("raw_vg", [P, KT, 2 * D])
                raw_o = e_sb("raw_o", [P, KT, D])
                raw_gu = e_sb("raw_gu", [P, 2, KT, FF])
                raw_d = e_sb("raw_d", [P, FT, D])
                raw_r = e_sb("raw_r", [EXPERTS, D])
                mean_v = e_sb("mean_v", [P, KT, HEADS])
                mean_b = e_sb("mean_b", [P, HEADS])
            with ExitStack() as shared:
                s_sb = tensors(shared)
                s_act = s_sb("s_act", [P, 2, TOK])
                h = s_sb("h", [P, 2, TOK])
                hT = s_sb("hT", [P, 2, FT, TOK], F32R)
                gate = s_sb("gate", [P, TILES, D])
            s_sb = sb
            xz = s_sb("xz", [P, RING, 2 * D])
            xsT = s_sb("xsT", [P, 2, KT, P], F32R)
            e_act = s_sb("e_act", [P, FF])
            eh = s_sb("eh", [P, FF])
            ehT = s_sb("ehT", [P, FT, P])
            of = s_sb("of", [P, 2, D])
            st2 = s_sb("st2", [P, 6])
            mv2 = s_sb("mv2", [P, 2])
            ln2_e = s_sb("ln2_e", [P, 1])
            ln2_r = s_sb("ln2_r", [P, 1])
            rest = s_sb("rest", [P, 4 * TOK + FT * 2 * TOK - (RING * 2 * D + 2 * KT * P + 3 * FF + 2 * D + 10)])
            count = s_sb("count", [P, EXPERTS])
            count_up = s_sb("count_up", [P, EXPERTS], I32)
            slots_i = s_sb("slots_i", [P, EXPERTS], I32)
            slots_f = s_sb("slots_f", [P, EXPERTS])
            slot_end = s_sb("slot_end", [P, EXPERTS])
            skip = s_sb("skip", [P, EXPERTS])
            passed = s_sb("passed", [P, SLOTS, EXPERTS - 1])
            skipped = s_sb("skipped", [P, SLOTS, EXPERTS - 1])
            slot_e = s_sb("slot_e", [P, SLOTS])
            slot_ei = s_sb("slot_ei", [P, SLOTS], I32)
            slot_r = s_sb("slot_r", [P, SLOTS])
            slot_row = s_sb("slot_row", [P, SLOTS])
            slot_ri = s_sb("slot_ri", [P, SLOTS], I32)
            rest_of_gate = s_sb("rest_of_gate", [P, TILES * D - 2 * SLOTS * (EXPERTS - 1) - 5 * SLOTS - 6 * EXPERTS])
            zs = sb("zs", [P, TILES, D])
            var = sb("var", [P, TILES * HEADS])
            var_e = sb("var_e", [P, TILES * HEADS])
            rstd = sb("rstd", [P, TILES * HEADS])
            stats = sb("stats", [P, TILES, 6])
            mv = sb("mv", [P, TILES, 2])
            ln_e = sb("ln_e", [P, TILES])
            ln_r = sb("ln_r", [P, TILES])
            nm = sb("nm", [P, TILES])
            nmr = sb("nmr", [P, TILES])
            lgT = sb("lgT", [EXPERTS, TOK])


        duo = [ctx.enter_context(nc.psum_tensor(f"duo{i}", [P, 2, 512], F32)) for i in range(4)]
        sim_duo = (duo[1], duo[3], duo[0])

        def new(name):
            return ctx.enter_context(nc.semaphore(name))

        class sig:
            apart = new("apart")
            ident_in = new("ident_in")
            first_in = new("first_in")
            bias_in = new("bias_in")
            c_in = new("c_in")
            wqk_in = new("wqk_in")
            wvg_in = new("wvg_in")
            raw_in = new("raw_in")
            wrT_ps = new("wrT_ps")
            w_hi = new("w_hi")
            w_lo = new("w_lo")
            center = new("center")
            xin = new("xin")
            xres_in = new("xres_in")
            xT_ps = new("xT_ps")
            xT_hi = new("xT_hi")
            xT_lo = new("xT_lo")
            qk_ps = new("qk_ps")
            prod_ok = new("prod_ok")
            turned_ok = new("turned_ok")
            split_hi = new("split_hi")
            split_lo = new("split_lo")
            rot_out = [new("rot_out_q"), new("rot_out_k")]
            stack_in = new("stack_in")
            vg_ps = new("vg_ps")
            vg_ok = new("vg_ok")
            gate_ok = new("gate_ok")
            s_ps = new("s_ps")
            s_off = new("s_off")
            s_diag = new("s_diag")
            av_ps = new("av_ps")
            retT_ok = new("retT_ok")
            rn_ps = new("rn_ps")
            sq_ok = new("sq_ok")
            var_ok = new("var_ok")
            eps_ok = new("eps_ok")
            rstd_ok = new("rstd_ok")
            rn_ok = new("rn_ok")
            y_w = new("y_w")
            y_b = new("y_b")
            y_ok = new("y_ok")
            yT_ps = new("yT_ps")
            yT_hi = new("yT_hi")
            yT_lo = new("yT_lo")
            xb_ok = new("xb_ok")
            o_ps = new("o_ps")
            z_ok = new("z_ok")
            st_ok = new("st_ok")
            mv_ok = new("mv_ok")
            lne_ok = new("lne_ok")
            lnr_ok = new("lnr_ok")
            nm_ok = new("nm_ok")
            nmr_ok = new("nmr_ok")
            x1_ok = new("x1_ok")
            x1_out = new("x1_out")
            x1T_ps = new("x1T_ps")
            x1T_hi = new("x1T_hi")
            x1T_lo = new("x1T_lo")
            gu_ps = new("gu_ps")
            sact_ok = new("sact_ok")
            h_ok = new("h_ok")
            h_hi = new("h_hi")
            h_lo = new("h_lo")
            lgT_ps = new("lgT_ps")
            lgT_ok = new("lgT_ok")
            lg_ps = new("lg_ps")
            lg_ok = new("lg_ok")
            dn_ps = new("dn_ps")
            zs_ok = new("zs_ok")
            zs_out = new("zs_out")
            zero_ok = new("zero_ok")
            zrow_out = new("zrow_out")
            free_out = new("free_out")
            route = new("route")
            hot_ok = new("hot_ok")
            rank_ps = new("rank_ps")
            place_ok = new("place_ok")
            pow_ok = new("pow_ok")
            pow1_ok = new("pow1_ok")
            score_ok = new("score_ok")
            ids_ok = new("ids_ok")
            scat = new("scat")
            plan = new("plan")
            plan_ok = new("plan_ok")
            egu_in = [new(f"egu_in{e}") for e in range(EXPERTS)]
            edn_in = new("edn_in")
            ew_hi = new("ew_hi")
            ew_lo = new("ew_lo")
            ew_lo2 = new("ew_lo2")
            xsT_ps = new("xsT_ps")
            xsT_hi = new("xsT_hi")
            xsT_lo = new("xsT_lo")
            eg_ps = new("eg_ps")
            e_act_ok = new("e_act_ok")
            eh_ok = new("eh_ok")
            dest_ok = new("dest_ok")
            ehT_ps = new("ehT_ps")
            ehT_ok = new("ehT_ok")
            ed_ps = new("ed_ps")
            sum_ok = new("sum_ok")
            st2_ok = new("st2_ok")
            mv2_ok = new("mv2_ok")
            lne2_ok = new("lne2_ok")
            lnr2_ok = new("lnr2_ok")
            of_ok = new("of_ok")
            seat_in = [new(f"seat_in{i}") for i in range(RING)]
            xz_in = [new(f"xz_in{i}") for i in range(RING)]
            x_only_in = [new(f"x_only_in{i}") for i in range(2)]
            out_done = [new(f"out_done{i}") for i in range(RING)]

        def at(value):
            return max(value, 0) if isinstance(value, int) else value

        def apart(eng):
            eng.sem_inc(sig.apart, 1)

        def has(i):
            return not isinstance(i, int) or 0 <= i < PAIRS

        def is_short(t):
            return isinstance(t, int) and t in (1, PAIRS)

        def x1_of(p):
            return x_res if isinstance(p, int) and p == PAIRS - 1 else x1

        def is_last(t):
            return isinstance(t, int) and t == PAIRS

        def pipeline(eng, step):
            for t in range(3):
                step(t)
            with eng.Fori(3, PAIRS - 1) as t:
                step(t)
            for t in range(PAIRS - 1, PAIRS + 2):
                step(t)

        def slot_pipeline(eng, step):
            for s in range(RING):
                step(s, s % RING, s // RING)
            with eng.Fori(1, SLOTS // RING) as u:
                for r in range(RING):
                    step(RING * u + r, r, u)
            for s in range(SLOTS // RING * RING, SLOTS + 1):
                step(s, s % RING, s // RING)

        def is_slot(s):
            return not isinstance(s, int) or 0 <= s < SLOTS

        def tile_rows(dram, t, q):
            v = dram.rearrange("(t q p) d -> t p q d", q=q, p=P)
            return v[t] if isinstance(t, int) else v[bass.ds(t, 1)].rearrange("a p q d -> (a p) q d")

        def ahead(r, u, by):
            return (r + by) % RING, u + (r + by) // RING

        def one(t):
            return slice(t, t + 1) if isinstance(t, int) else bass.ds(t, 1)

        def spread(vector, n=D):
            return bass.AP(vector.tensor, 0, [[0, P], [1, n]])

        def over(ap, n):
            return bass.AP(ap.tensor, ap.offset, [list(ap.ap[0]), [0, n], *[list(a) for a in ap.ap[1:]]])

        def each(ap, n):
            return bass.AP(ap.tensor, ap.offset, [*[list(a) for a in ap.ap], [0, n]])

        block = ctx.enter_context(nc.Block())

        @block.sync
        def _(sp):
            sp.dma_start(ident[:, :], squares[:, 0:P]).then_inc(sig.ident_in, 16)
            sp.dma_start(x_in[:, :, :], tile_rows(x, 0, TILES)).then_inc(sig.xin, 16)
            sp.dma_start(bias_qk[:, 0, :], b_q.rearrange("(p two) -> p two", two=2)).then_inc(sig.first_in, 16)
            sp.dma_start(bias_qk[:, 1, :], b_k.rearrange("(p two) -> p two", two=2)).then_inc(sig.first_in, 16)
            sp.dma_start(rot[:, :, :], rotation.rearrange("p (f n) -> p f n", f=4)).then_inc(sig.first_in, 16)
            sp.dma_start(bias_vg[:, 0:D], spread(b_v)).then_inc(sig.bias_in, 16)
            sp.dma_start(bias_vg[:, D:2 * D], spread(b_g)).then_inc(sig.bias_in, 16)
            sp.dma_start(raw_o[:, :, :], w_o.rearrange("(k p) n -> p k n", p=P)).then_inc(sig.raw_in, 16)
            sp.dma_start(raw_gu[:, 0, :, :], sh_gate.rearrange("(k p) n -> p k n", p=P)).then_inc(sig.raw_in, 16)
            sp.dma_start(raw_gu[:, 1, :, :], sh_up.rearrange("(k p) n -> p k n", p=P)).then_inc(sig.raw_in, 16)
            sp.dma_start(raw_d[:, :, :], sh_down.rearrange("(k p) n -> p k n", p=P)).then_inc(sig.raw_in, 16)
            sp.dma_start(raw_r[:, :], router_w).then_inc(sig.raw_in, 16)
            sp.dma_start(causal[:, :], squares[:, P:2 * P]).then_inc(sig.c_in, 16)
            sp.dma_start(before[:, :], squares[:, 2 * P:3 * P]).then_inc(sig.c_in, 16)
            sp.dma_start(ones[:, :], squares[:, 3 * P:4 * P]).then_inc(sig.c_in, 16)
            sp.dma_start(priority[:, :], squares[:, 4 * P:4 * P + EXPERTS]).then_inc(sig.c_in, 16)
            sp.dma_start(slot_no[:, :], squares[:, 4 * P + EXPERTS:4 * P + EXPERTS + SLOTS]).then_inc(sig.c_in, 16)
            o = 4 * P + EXPERTS + SLOTS
            sp.dma_start(region[:, :], squares[:, o:o + EXPERTS]).then_inc(sig.c_in, 16)
            sp.dma_start(start[:, TILES, :], squares[:, o:o + EXPERTS]).then_inc(sig.c_in, 16)
            sp.dma_start(seats[:, :, :], token_seats.rearrange("p (t c) -> p t c", c=SEAT)).then_inc(sig.c_in, 16)
            sp.dma_start(bias_o[:, :], spread(b_o)).then_inc(sig.c_in, 16)
            sp.dma_start(norm_w[:, :], spread(gn_w)).then_inc(sig.c_in, 16)
            sp.dma_start(norm_b[:, :], spread(gn_b)).then_inc(sig.c_in, 16)
            sp.dma_start(seat_d, free_seats).then_inc(sig.free_out, 16)

            def down_in(first_, after):
                for e in range(first_, after):
                    sp.dma_start(w_dn[:, e, :, :], down[e].rearrange("(k p) n -> p k n", p=P))\
                        .then_inc(sig.edn_in, 16)

            def step(t):
                if has(t + 1):
                    sp.wait_ge(sig.xT_ps, at(t + 1))
                    sp.dma_start(x_in[:, :, :], tile_rows(x, t + 1, TILES)).then_inc(sig.xin, 16)
                if has(t - 1):
                    sp.wait_ge(sig.x1_ok, at(TILES * (t - 1)))
                    sp.dma_start(x_res[:, :, :], tile_rows(x, t - 1, TILES)).then_inc(sig.xres_in, 16)
                if has(t - 2):
                    sp.wait_ge(sig.x1_ok, at(TILES * (t - 1)))
                    sp.dma_start(tile_rows(xz_d[0:TOKENS, 0:D], t - 2, TILES), x1_of(t - 2)[:, :, :])\
                        .then_inc(sig.x1_out, 16)
                    sp.dma_start(tile_rows(x1_d[0:TOKENS, :], t - 2, TILES), x1_of(t - 2)[:, :, :])\
                        .then_inc(sig.x1_out, 16)
                if isinstance(t, int) and t == PAIRS:
                    sp.wait_ge(sig.av_ps, 4 * PAIRS)
                    for e in range(EXPERTS):
                        sp.dma_start(w_gu[:, e, :, :], gate_up[e].rearrange("(k p) n -> p k n", p=P))\
                            .then_inc(sig.egu_in[e], 16)
                    sp.wait_ge(sig.o_ps, 2 * PAIRS)
                    down_in(0, 4)
                if isinstance(t, int) and t == PAIRS + 1:
                    sp.wait_ge(sig.x1_out, 32 * PAIRS)
                    sp.wait_ge(sig.zs_ok, 2 * (PAIRS - 1))
                    down_in(7, 8)
                    sp.wait_ge(sig.gu_ps, 2 * FT * PAIRS)
                    down_in(5, 7)
                if has(t):
                    for side in range(2):
                        sp.wait_ge(sig.split_hi, at(4 * t + 2 * side + 2))
                        apart(sp)
                        sp.wait_ge(sig.split_lo, at(4 * t + 2 * side + 2))
                        apart(sp)
                        sp.wait_ge(sig.stack_in, at(192 * t))
                        for part, places in enumerate((slice(1, 3), slice(0, 4, 3))):
                            sp.dma_start(rot_d[side, part].rearrange("e p n -> p e n"), prod[:, side, places, :])\
                                .then_inc(sig.rot_out[side], 16)
                    for side in range(2):
                        sp.wait_ge(sig.rot_out[side], at(32 * (t + 1)))
                        apart(sp)
                        sp.wait_ge(sig.s_ps, at(8 * t))
                        for group, part in enumerate(((0, 1, 0), (0, 0, 1))[side]):
                            for e in range(2):
                                lo = HD * group + HALF * e
                                sp.dma_start(f32(stack[side][lo:lo + HALF, :, :]),
                                             rot_d[side, part, e].rearrange("(h i) n -> i h n", i=HALF))\
                                    .then_inc(sig.stack_in, 16)
                if has(t - 2) and has(t - 1):
                    sums_out(t - 2)

            def sums_out(p):
                sp.wait_ge(sig.zs_ok, at(2 * (p + 1)))
                sp.dma_start(tile_rows(xz_d[0:TOKENS, D:2 * D], p, TILES), zs[:, :, :]).then_inc(sig.zs_out, 16)

            pipeline(sp, step)

            def seat_load(s, r, u):
                if is_slot(s):
                    sp.wait_ge(sig.xz_in[r], at(16 * u))
                    apart(sp)
                    sp.wait_ge(sig.eh_ok, at(s - RING + 1))
                    apart(sp)
                    sp.wait_ge(sig.dest_ok, at(s - RING + 1))
                    apart(sp)
                    row = sp.value_load(slot_ri[0:1, one(s)], min_val=0, max_val=SEATS - P)
                    sp.dma_start(seat[:, r, :], seat_d[bass.ds(row, P), :]).then_inc(sig.seat_in[r], 16)

            def slot_step(s, r, u):
                seat_load(s + 3, *ahead(r, u, 3))

            sp.wait_ge(sig.plan_ok, 2)
            sp.wait_ge(sig.scat, 16 * NTILE)
            seat_load(0, 0, 0)
            seat_load(1, 1, 0)
            seat_load(2, 2, 0)
            sums_out(PAIRS - 1)
            sp.wait_ge(sig.x1_out, 32 * PAIRS)
            down_in(4, 5)
            slot_pipeline(sp, slot_step)
            for r in range(RING):
                sp.wait_ge(sig.out_done[r], 16 * ((SLOTS - r + RING - 1) // RING))

        @block.scalar
        def _(act):
            def k_rows(w):
                return w.rearrange("(k p) n -> p k n", p=P)

            act.dma_start(raw_qk[:, 0, :, :], k_rows(w_q)).then_inc(sig.wqk_in, 16)
            act.dma_start(raw_qk[:, 1, :, :], k_rows(w_k)).then_inc(sig.wqk_in, 16)
            act.dma_start(raw_vg[:, :, 0:D], k_rows(w_v)).then_inc(sig.wvg_in, 16)
            act.dma_start(raw_vg[:, :, D:2 * D], k_rows(w_g)).then_inc(sig.wvg_in, 16)

            def x_hi(t):
                for k in range(KT):
                    act.wait_ge(sig.xT_ps, at(t + 1))
                    act.wait_ge(sig.vg_ps, at(TILES * t))
                    nc.scalar.activation(xT[:, 0, k, :], duo[3][:, k, :], ACT.Copy)\
                        .then_inc(sig.xT_hi, 1)

            x_hi(0)
            act.wait_ge(sig.wqk_in, 16 * 2)
            nc.scalar.activation(wqk[:, :, 0, :, :], raw_qk[:, :, :, :], ACT.Copy)\
                .then_inc(sig.w_hi, 1)
            act.wait_ge(sig.wvg_in, 16 * 2)
            act.wait_ge(sig.center, 5)
            nc.scalar.activation(wvg[:, 0, :, :], raw_vg[:, :, :], ACT.Copy)\
                .then_inc(sig.w_hi, 1)

            def step(t):
                if has(t - 1):
                    p = t - 1
                    for j in range(8):
                        act.wait_ge(sig.s_ps, at(8 * p + j + 1))
                        act.wait_ge(sig.av_ps, at(4 * p + j // 2 - 1))
                        nc.scalar.activation(sims[:, j % 4, :, 1, :], sim_duo[j % 3][:, :, P:2 * P], ACT.Copy)\
                            .then_inc(sig.s_off, 1)
                    for g in range(2):
                        act.wait_ge(sig.av_ps, at(4 * p + 3 + g))
                        act.wait_ge(sig.var_ok, at(2 * p))
                        nc.scalar.activation(retT[:, g, :], duo[2][:, g, :], ACT.Copy)\
                            .then_inc(sig.retT_ok, 1)
                if has(t - 2) and has(t - 1):
                    first_norm(t - 2)
                if has(t):
                    split_hi(t, 0)
                if has(t - 1):
                    for i in range(2):
                        act.wait_ge(sig.rn_ps, at(t))
                        nc.scalar.activation(retT[:, i, :], duo[3][:, i, :], ACT.Square, scale=float(HD) ** -0.5)\
                            .then_inc(sig.sq_ok, 1)
                if isinstance(t, int) and t == 0:
                    split_hi(t, 1)
                    later_weights_hi()
                if has(t - 2):
                    p = t - 2
                    for k in range(KT):
                        act.wait_ge(sig.x1T_ps, at(p + 1))
                        act.wait_ge(sig.gu_ps, at(2 * FT * p))
                        act.wait_ge(sig.lgT_ps, at(p))
                        nc.scalar.activation(x1T[:, 0, k, :], duo[2][:, k, :], ACT.Copy)\
                            .then_inc(sig.x1T_hi, 1)
                if isinstance(t, int) and t == PAIRS + 1:
                    act.wait_ge(sig.o_ps, 2 * PAIRS)
                    expert_hi(4)
                if has(t) and not (isinstance(t, int) and t == 0):
                    split_hi(t, 1)
                if has(t - 2):
                    p = t - 2
                    act.wait_ge(sig.lgT_ps, at(p + 1))
                    act.wait_ge(sig.lg_ps, at(p))
                    nc.scalar.activation(lgT[:, :], duo[2][0:EXPERTS, 0, :], ACT.Copy).then_inc(sig.lgT_ok, 1)
                    for j in range(FT):
                        act.wait_ge(sig.gu_ps, at(2 * FT * p + 2 * j + 1))
                        act.wait_ge(sig.h_ok, at(FT * p + j - 1))
                        nc.scalar.activation(s_act[:, j % 2, :], duo[j % 2][:, 0, :], ACT.Silu)\
                            .then_inc(sig.sact_ok, 1)
                        if j:
                            h_hi(p, j - 1)
                        if j == 2 and is_last(t):
                            y_hi(t - 1)
                    h_hi(p, FT - 1)
                if has(t - 1) and not is_last(t):
                    y_hi(t - 1)
                if has(t):
                    for q in range(TILES):
                        act.wait_ge(sig.vg_ok, at(TILES * t + q + 1))
                        act.wait_ge(sig.y_ok, at(2 * t))
                        nc.scalar.activation(gate[:, q, :], vg[:, q, D:2 * D], ACT.Silu)\
                            .then_inc(sig.gate_ok, 1)
                if has(t + 1):
                    x_hi(t + 1)
                if is_last(t):
                    act.wait_ge(sig.av_ps, 4 * PAIRS)
                    for e in range(4):
                        expert_hi(e)
                    first_norm(t - 1)

            def y_hi(p):
                for k in range(KT):
                    act.wait_ge(sig.yT_ps, at(p + 1))
                    act.wait_ge(sig.o_ps, at(2 * p))
                    nc.scalar.activation(yT[:, 0, k, :], duo[3][:, k, :], ACT.Copy)\
                        .then_inc(sig.yT_hi, 1)

            def first_norm(p):
                act.wait_ge(sig.nmr_ok, at(p + 1))
                if x1_of(p) is x1:
                    act.wait_ge(sig.x1_out, at(32 * p))
                    act.wait_ge(sig.x1T_ps, at(p))
                    act.wait_ge(sig.zs_ok, at(2 * p))
                for q in range(TILES):
                    nc.scalar.activation(x1_of(p)[:, q, :], x_res[:, q, :], ACT.Identity, bias=nmr[:, q:q + 1],
                                         scale=ln_r[:, q:q + 1]).then_inc(sig.x1_ok, 1)

            def expert_hi(e):
                act.wait_ge(sig.egu_in[e], 16)
                nc.scalar.activation(w_gu_hi[:, e, :, :], w_gu[:, e, :, :], ACT.Copy).then_inc(sig.ew_hi, 1)

            def later_weights_hi():
                act.wait_ge(sig.raw_in, 16 * 5)
                nc.scalar.activation(wo[:, 0, :, :], raw_o[:, :, :], ACT.Copy).then_inc(sig.w_hi, 1)
                nc.scalar.activation(wsgu[:, :, 0, :, :], raw_gu[:, :, :, :], ACT.Copy).then_inc(sig.w_hi, 1)
                nc.scalar.activation(wsd[:, 0, :, :], raw_d[:, :, :], ACT.Copy).then_inc(sig.w_hi, 1)
                act.wait_ge(sig.wrT_ps, 1)
                nc.scalar.activation(wr[:, 0, :, :], duo[2][:, 0, 0:KT * EXPERTS].rearrange("p (k e) -> p k e", k=KT),
                                     ACT.Copy).then_inc(sig.w_hi, 1)

            def split_hi(t, side):
                for e in range(2):
                    act.wait_ge(sig.turned_ok, at(4 * t + 2 * side + e + 1))
                    nc.scalar.activation(prod[:, side, 1 + e, :].bitcast(F32R), prod[:, side, 3 * e, :], ACT.Copy)\
                        .then_inc(sig.split_hi, 1)

            def h_hi(p, j):
                act.wait_ge(sig.h_ok, at(FT * p + j + 1))
                act.wait_ge(sig.dn_ps, at(2 * p))
                nc.scalar.activation(hT[:, 0, j, :], h[:, j % 2, :], ACT.Copy)\
                    .then_inc(sig.h_hi, 1)

            pipeline(act, step)

            act.wait_ge(sig.gu_ps, 2 * FT * PAIRS)
            expert_hi(5)
            expert_hi(6)
            act.wait_ge(sig.dn_ps, 2 * PAIRS)
            for k in range(KT):
                act.wait_ge(sig.egu_in[EXPERTS - 1], 16)
                nc.scalar.activation(w_gu_hi[:, EXPERTS - 1, k, :], w_gu[:, EXPERTS - 1, k, :], ACT.Copy)\
                    .then_inc(sig.ew_hi, 1)

            def rows_hi(s):
                if is_slot(s):
                    act.wait_ge(sig.xsT_ps, at(s + 1))
                    act.wait_ge(sig.eg_ps, at(2 * s))
                    nc.scalar.activation(xsT[:, 0, :, :], duo[3][:, 0, 0:D].rearrange("p (k n) -> p k n", k=KT),
                                         ACT.Copy).then_inc(sig.xsT_hi, 1)

            def slot_step(s, r, u):
                if is_slot(s):
                    act.wait_ge(sig.eg_ps, at(2 * s + 1))
                    act.wait_ge(sig.eh_ok, at(s))
                    nc.scalar.activation(e_act[:, :], duo[r % 2][:, 0, :], ACT.Silu, scale=f32(seat[:, r, :])[:, 2:3])\
                        .then_inc(sig.e_act_ok, 1)
                rows_hi(s + 1)
                if is_slot(s):
                    act.wait_ge(sig.ehT_ps, at(s + 1))
                    act.wait_ge(sig.ed_ps, at(s))
                    nc.scalar.activation(ehT[:, :, :], duo[2][:, 0, :].rearrange("p (f n) -> p f n", f=FT), ACT.Copy)\
                        .then_inc(sig.ehT_ok, 1)

            rows_hi(0)
            slot_pipeline(act, slot_step)

        @block.gpsimd
        def _(pool):
            nc.gpsimd.memset(minus_half[:, :], -0.5).then_inc(sig.zero_ok, 1)
            nc.gpsimd.memset(minus_one[:, :], -1.0).then_inc(sig.zero_ok, 1)
            nc.gpsimd.memset(inv_e[:, :], float(np.exp(-1.0))).then_inc(sig.zero_ok, 1)
            nc.gpsimd.memset(y[0:1, 0:2, :], 0.0).then_inc(sig.zero_ok, 1)
            pool.wait_ge(sig.zero_ok, 4)
            pool.dma_start(xz_d[TOKENS:TOKENS + 1, :], y[0:1, 0:2, :].rearrange("p q d -> p (q d)"))\
                .then_inc(sig.zrow_out, 16)
            pool.dma_start(x1_d[TOKENS:TOKENS + 1, :], y[0:1, 0, :]).then_inc(sig.zrow_out, 16)
            pool.wait_ge(sig.c_in, at(16 * N_IN))

            def step(t):
                if has(t):
                    for side in range(2):
                        pool.wait_ge(sig.prod_ok, at(4 * t + 2 * side + 2))
                        nc.gpsimd.tensor_tensor(prod[:, side, 0, :], prod[:, side, 0, :], prod[:, side, 1, :],
                                                ALU.subtract).then_inc(sig.turned_ok, 1)
                        nc.gpsimd.tensor_tensor(prod[:, side, 3, :], prod[:, side, 3, :], prod[:, side, 2, :],
                                                ALU.add).then_inc(sig.turned_ok, 1)
                if has(t - 1):
                    p = t - 1
                    pool.wait_ge(sig.var_ok, at(2 * p + 2))
                    apart(pool)
                    nc.gpsimd.tensor_scalar(var_e[:, :], var[:, :], EPS, None, ALU.add).then_inc(sig.eps_ok, 1)
                    pool.wait_ge(sig.eps_ok, at(p + 1))
                    pool.wait_ge(sig.rn_ok, at(2 * p))
                    for i in range(2):
                        half = slice(16 * i, 16 * i + 16)
                        nc.gpsimd.tensor_tensor(rstd[:, half], var_e[:, half], minus_half[:, half], ALU.pow)\
                            .then_inc(sig.rstd_ok, 1)
                    if not is_short(t):
                        for i in range(2):
                            two = y[:, 2 * i:2 * i + 2, :]
                            pool.wait_ge(sig.rn_ok, at(2 * p + i + 1))
                            nc.gpsimd.tensor_tensor(two, two, over(norm_w[:, :], 2), ALU.mult).then_inc(sig.y_w, 1)
                            pool.wait_ge(sig.y_w, at(2 * p + i + 1))
                            nc.gpsimd.tensor_tensor(two, two, over(norm_b[:, :], 2), ALU.add).then_inc(sig.y_b, 1)
                            pool.wait_ge(sig.y_b, at(2 * p + i + 1))
                            pool.wait_ge(sig.gate_ok, at(TILES * (p + 1)))
                            nc.gpsimd.tensor_tensor(two, two, gate[:, 2 * i:2 * i + 2, :], ALU.mult)\
                                .then_inc(sig.y_ok, 1)
                    pool.wait_ge(sig.xres_in, at(16 * (p + 1)))
                    nc.gpsimd.tensor_tensor(x_res[:, :, :], x_res[:, :, :], over(bias_o[:, :], TILES),
                                            ALU.add).then_inc(sig.xb_ok, 1)
                if isinstance(t, int) and t == PAIRS + 1:
                    expert_rest(3)
                    expert_rest(4)
                if has(t - 2):
                    take_seats(t - 2)
                if has(t - 1):
                    p = t - 1
                    pool.wait_ge(sig.mv_ok, at(TILES * (p + 1)))
                    apart(pool)
                    nc.gpsimd.tensor_scalar(ln_e[:, :], mv[:, :, 1], EPS, None, ALU.add).then_inc(sig.lne_ok, 1)
                    nc.gpsimd.tensor_tensor(nm[:, :], mv[:, :, 0], minus_one[:, :], ALU.mult).then_inc(sig.nm_ok, 1)
                    pool.wait_ge(sig.lne_ok, at(p + 1))
                    pool.wait_ge(sig.x1_ok, at(TILES * p))
                    nc.gpsimd.tensor_tensor(ln_r[:, :], ln_e[:, :], minus_half[:, 0:TILES], ALU.pow)\
                        .then_inc(sig.lnr_ok, 1)
                    pool.wait_ge(sig.nm_ok, at(p + 1))
                    pool.wait_ge(sig.lnr_ok, at(p + 1))
                    nc.gpsimd.tensor_tensor(nmr[:, :], nm[:, :], ln_r[:, :], ALU.mult).then_inc(sig.nmr_ok, 1)
                if is_last(t):
                    expert_rest(1)

            def expert_rest(e):
                pool.wait_ge(sig.ew_hi, e + 1)
                nc.gpsimd.tensor_tensor(w_gu[:, e, :, :].bitcast(F32R), w_gu[:, e, :, :], f32(w_gu_hi[:, e, :, :]),
                                        ALU.subtract).then_inc(sig.ew_lo2, 1)

            def take_seats(p):
                pool.wait_ge(sig.scat, at(16 * TILES * p))
                pool.wait_ge(sig.free_out, 16)
                tiles = slice(TILES * p, TILES * p + TILES) if isinstance(p, int) else bass.ds(TILES * p, TILES)
                nc.gpsimd.tensor_copy(stage[:, :, 0:2], seats[:, tiles, 0:2]).then_inc(sig.ids_ok, 1)
                pool.wait_ge(sig.route, at(ROUTE * p + 2))
                nc.gpsimd.tensor_tensor(powed[:, :], inv_e[:, :], top[:, :], ALU.pow).then_inc(sig.pow_ok, 1)
                pool.wait_ge(sig.pow_ok, at(p + 1))
                apart(pool)
                nc.gpsimd.tensor_scalar(powed1[:, :], powed[:, :], 1.0, None, ALU.add).then_inc(sig.pow1_ok, 1)
                pool.wait_ge(sig.pow1_ok, at(p + 1))
                nc.gpsimd.tensor_tensor(f32(stage[:, :, :])[:, :, 2], powed1[:, :], minus_one[:, :], ALU.pow)\
                    .then_inc(sig.score_ok, 1)
                pool.wait_ge(sig.ids_ok, at(p + 1))
                apart(pool)
                pool.wait_ge(sig.score_ok, at(p + 1))
                apart(pool)
                pool.wait_ge(sig.place_ok, at(p + 1))
                apart(pool)
                for q in range(TILES):
                    pool.indirect_dma_start(seat_d, bass.IndirectOffsetOnAxis(ap=place_i[:, q:q + 1], axis=0),
                                            stage[:, q, :], None).then_inc(sig.scat, 16)

            pipeline(pool, step)

            expert_rest(5)

            pool.wait_ge(sig.zrow_out, 32)
            pool.wait_ge(sig.plan_ok, 2)
            pool.wait_ge(sig.x1_out, 32 * PAIRS)

            def gather(s, r, u):
                if is_slot(s):
                    pool.wait_ge(sig.sum_ok, at(s - RING + 1))
                    apart(pool)
                    pool.wait_ge(sig.seat_in[r], at(16 * (u + 1)))
                    apart(pool)
                    pool.indirect_dma_start(xz[:, r, :], None, xz_d,
                                            bass.IndirectOffsetOnAxis(ap=seat[:, r, 0:1], axis=0))\
                        .then_inc(sig.xz_in[r], 16)
                    pool.wait_ge(sig.out_done[r], at(16 * u))
                    apart(pool)
                    nc.gpsimd.tensor_copy(dest[:, r:r + 1], seat[:, r, 1:2]).then_inc(sig.dest_ok, 1)

            def slot_step(s, r, u):
                gather(s + 2, *ahead(r, u, 2))
                if is_slot(s - 1):
                    b, _ = ahead(r, u, -1)
                    pool.wait_ge(sig.mv2_ok, at(s))
                    apart(pool)
                    nc.gpsimd.tensor_scalar(ln2_e[:, :], mv2[:, 1:2], EPS, None, ALU.add).then_inc(sig.lne2_ok, 1)
                    pool.wait_ge(sig.lne2_ok, at(s))
                    pool.wait_ge(sig.of_ok, at(s - 1))
                    nc.gpsimd.tensor_tensor(ln2_r[:, :], ln2_e[:, :], minus_half[:, 0:1], ALU.pow)\
                        .then_inc(sig.lnr2_ok, 1)
                if is_slot(s - 1):
                    pool.wait_ge(sig.of_ok, at(s))
                    apart(pool)
                    pool.wait_ge(sig.dest_ok, at(s))
                    apart(pool)
                    if is_slot(s - 2):
                        c, turn = ahead(r, u, -2)
                        pool.wait_ge(sig.out_done[c], at(16 * (turn + 1)))
                        apart(pool)
                    pool.indirect_dma_start(out, bass.IndirectOffsetOnAxis(ap=dest[:, b:b + 1], axis=0),
                                            of[:, b % 2, :], None).then_inc(sig.out_done[b], 16)

            for s in range(2):
                pool.wait_ge(sig.seat_in[s], 16)
                pool.indirect_dma_start(xz[:, s, 0:D], None, x1_d,
                                        bass.IndirectOffsetOnAxis(ap=seat[:, s, 0:1], axis=0))\
                    .then_inc(sig.x_only_in[s], 16)
                nc.gpsimd.tensor_copy(dest[:, s:s + 1], seat[:, s, 1:2]).then_inc(sig.dest_ok, 1)
            pool.wait_ge(sig.zs_out, 16 * PAIRS)
            for s in range(2):
                pool.wait_ge(sig.xsT_ps, s + 1)
                pool.indirect_dma_start(xz[:, s, :], None, xz_d,
                                        bass.IndirectOffsetOnAxis(ap=seat[:, s, 0:1], axis=0))\
                    .then_inc(sig.xz_in[s], 16)
            slot_pipeline(pool, slot_step)

        @block.vector
        def _(dve):
            def x_lo(t):
                for k in range(KT):
                    dve.wait_ge(sig.xT_hi, at(2 * t + k + 1))
                    dve.wait_ge(sig.vg_ps, at(TILES * t))
                    nc.vector.tensor_tensor(xT[:, 1, k, :], duo[3][:, k, :], f32(xT[:, 0, k, :]), ALU.subtract)\
                        .then_inc(sig.xT_lo, 1)

            x_lo(0)
            dve.wait_ge(sig.first_in, 16 * 3)
            dve.wait_ge(sig.wqk_in, 16 * 2)
            dve.wait_ge(sig.w_hi, 1)
            nc.vector.tensor_tensor(wqk[:, :, 1, :, :], raw_qk[:, :, :, :], f32(wqk[:, :, 0, :, :]), ALU.subtract)\
                .then_inc(sig.w_lo, 1)
            dve.wait_ge(sig.wvg_in, 16 * 2)
            dve.wait_ge(sig.bias_in, 16 * 2)
            v_heads = raw_vg[:, :, 0:D].rearrange("p k (h d) -> p k h d", d=HD)
            b_heads = bias_vg[:, 0:D].rearrange("p (h d) -> p h d", d=HD)
            nc.vector.tensor_reduce(mean_v[:, :, :], v_heads, X, ALU.add).then_inc(sig.center, 1)
            nc.vector.tensor_reduce(mean_b[:, :], b_heads, X, ALU.add).then_inc(sig.center, 1)
            dve.wait_ge(sig.center, at(2))
            for k in range(KT):
                nc.vector.scalar_tensor_tensor(out=v_heads[:, k], in0=each(mean_v[:, k, :], HD), scalar=-1.0 / HD,
                                               in1=v_heads[:, k], op0=ALU.mult, op1=ALU.add).then_inc(sig.center, 1)
            nc.vector.scalar_tensor_tensor(out=b_heads, in0=each(mean_b[:, :], HD), scalar=-1.0 / HD,
                                           in1=b_heads, op0=ALU.mult, op1=ALU.add).then_inc(sig.center, 1)
            dve.wait_ge(sig.w_hi, 2)
            nc.vector.tensor_tensor(wvg[:, 1, :, :], raw_vg[:, :, :], f32(wvg[:, 0, :, :]), ALU.subtract)\
                .then_inc(sig.w_lo, 1)

            def step(t):
                if has(t - 1):
                    p = t - 1
                    for j in range(8):
                        dve.wait_ge(sig.s_off, at(8 * p + j + 1))
                        dve.wait_ge(sig.av_ps, at(4 * p + j // 2 - 1))
                        src = sim_duo[j % 3][:, :, :].rearrange("p h (b q) -> p h b q", q=P)[:, :, 0::3, :]
                        mask = bass.AP(causal[:, :].tensor, 0, [[P, P], [0, 2], [0, 2], [1, P]])
                        nc.vector.tensor_tensor(sims[:, j % 4, :, 0::2, :], src, mask, ALU.mult)\
                            .then_inc(sig.s_diag, 1)
                if has(t - 2) and (has(t - 1) or has(t)):
                    statistics(t - 2)
                if isinstance(t, int) and t == PAIRS + 1:
                    expert_lo(0)
                if has(t):
                    for s in range(4):
                        side, e = s // 2, s % 2
                        dve.wait_ge(sig.qk_ps, at(4 * t + s + 1))
                        dve.wait_ge(sig.rot_out[side], at(32 * t))
                        for f in range(2):
                            place_ = (0, 2)[f] if e == 0 else (3, 1)[f]
                            last = nc.vector.scalar_tensor_tensor(
                                out=prod[:, side, place_, :].rearrange("p (b n) -> p b n", b=2),
                                in0=duo[side][:, e, :].rearrange("p (b n) -> p b n", b=2),
                                scalar=bias_qk[:, side, e:e + 1],
                                in1=over(rot[:, 2 * side + f, :], 2), op0=ALU.add, op1=ALU.mult)
                        last.then_inc(sig.prod_ok, 1)
                    split_lo(t, 0)
                if has(t - 1):
                    p = t - 1
                    for i in range(2):
                        dve.wait_ge(sig.sq_ok, at(2 * p + i + 1))
                        dve.wait_ge(sig.eps_ok, at(p))
                        nc.vector.tensor_reduce(var[:, 16 * i:16 * i + 16],
                                                retT[:, i, :].rearrange("p (h d) -> p h d", d=HD), X, ALU.add)\
                            .then_inc(sig.var_ok, 1)
                if has(t - 2):
                    p = t - 2
                    for k in range(KT):
                        dve.wait_ge(sig.x1T_hi, at(KT * p + k + 1))
                        nc.vector.tensor_tensor(x1T[:, 1, k, :], duo[2][:, k, :], f32(x1T[:, 0, k, :]), ALU.subtract)\
                            .then_inc(sig.x1T_lo, 1)
                    if isinstance(t, int) and t == PAIRS + 1:
                        expert_lo(2)
                if has(t):
                    starting = isinstance(t, int) and t == 0
                    if starting:
                        split_lo(t, 1)
                    for q in range(TILES):
                        dve.wait_ge(sig.vg_ps, at(TILES * t + q + 1))
                        dve.wait_ge(sig.av_ps, at(4 * t))
                        dve.wait_ge(sig.gate_ok, at(TILES * t))
                        nc.vector.tensor_tensor(vg[:, q, :], duo[q // 2][:, q % 2, :], bias_vg[:, :], ALU.add)\
                            .then_inc(sig.vg_ok, 1)
                    if not starting:
                        split_lo(t, 1)
                if isinstance(t, int) and t == 0:
                    later_weights_lo()
                if has(t - 1):
                    p = t - 1
                    if isinstance(p, int) and p == 0:
                        dve.wait_ge(sig.zrow_out, 32)
                    for i in range(2):
                        dve.wait_ge(sig.rstd_ok, at(2 * p + i + 1))
                        dve.wait_ge(sig.yT_ps, at(p))
                        nc.vector.tensor_tensor(
                            y[:, 2 * i:2 * i + 2, :].rearrange("p q (h d) -> p (q h) d", d=HD),
                            duo[3][:, i, :].rearrange("p (h d) -> p h d", d=HD),
                            each(rstd[:, 16 * i:16 * i + 16], HD), ALU.mult)\
                            .then_inc(sig.rn_ok, 1)
                        if is_short(t):
                            two = y[:, 2 * i:2 * i + 2, :]
                            dve.wait_ge(sig.rn_ok, 2 * p + i + 1)
                            nc.vector.tensor_tensor(two, two, over(norm_w[:, :], 2), ALU.mult).then_inc(sig.y_w, 1)
                            dve.wait_ge(sig.y_w, 2 * p + i + 1)
                            nc.vector.tensor_tensor(two, two, over(norm_b[:, :], 2), ALU.add).then_inc(sig.y_b, 1)
                            dve.wait_ge(sig.y_b, 2 * p + i + 1)
                            dve.wait_ge(sig.gate_ok, TILES * (p + 1))
                            nc.vector.tensor_tensor(two, two, gate[:, 2 * i:2 * i + 2, :], ALU.mult)\
                                .then_inc(sig.y_ok, 1)
                if has(t - 2):
                    p = t - 2
                    for j in range(FT):
                        dve.wait_ge(sig.gu_ps, at(2 * FT * p + 2 * j + 2))
                        dve.wait_ge(sig.sact_ok, at(FT * p + j + 1))
                        dve.wait_ge(sig.h_hi, at(FT * p + j - 1))
                        dve.wait_ge(sig.h_lo, at(FT * p + j - 1))
                        nc.vector.tensor_tensor(h[:, j % 2, :], duo[j % 2][:, 1, :], s_act[:, j % 2, :], ALU.mult)\
                            .then_inc(sig.h_ok, 1)
                        if j:
                            h_lo(p, j - 1)
                        if j == 1:
                            choose(p)
                        if j == 2:
                            find_seats(p)
                            if is_last(t):
                                y_lo(t - 1)
                    h_lo(p, FT - 1)
                    if isinstance(p, int) and p == PAIRS - 1:
                        plan_slots()
                if has(t - 1) and not is_last(t):
                    y_lo(t - 1)
                if is_last(t):
                    output_sum(t - 1)
                    statistics(t - 1)
                if has(t - 2) and has(t - 1):
                    for i in range(2):
                        shared_sum(t - 2, i)
                if has(t + 1):
                    x_lo(t + 1)
                if has(t - 1) and not is_last(t):
                    output_sum(t - 1)

            def expert_lo(e):
                dve.wait_ge(sig.ew_hi, e + 1)
                nc.vector.tensor_tensor(w_gu[:, e, :, :].bitcast(F32R), w_gu[:, e, :, :], f32(w_gu_hi[:, e, :, :]),
                                        ALU.subtract).then_inc(sig.ew_lo, 1)

            def y_lo(p):
                for k in range(KT):
                    dve.wait_ge(sig.yT_hi, at(KT * p + k + 1))
                    nc.vector.tensor_tensor(yT[:, 1, k, :], duo[3][:, k, :], f32(yT[:, 0, k, :]), ALU.subtract)\
                        .then_inc(sig.yT_lo, 1)

            def shared_sum(p, i):
                dve.wait_ge(sig.dn_ps, at(2 * p + i + 1))
                dve.wait_ge(sig.x1_ok, at(TILES * (p + 1)))
                dve.wait_ge(sig.zs_out, at(16 * p))
                nc.vector.tensor_tensor(
                    zs[:, 2 * i:2 * i + 2, :], duo[2][:, i, :].rearrange("p (q n) -> p q n", q=2),
                    x1_of(p)[:, 2 * i:2 * i + 2, :], ALU.add)\
                    .then_inc(sig.zs_ok, 1)

            def output_sum(p):
                for i in range(2):
                    dve.wait_ge(sig.o_ps, at(2 * p + i + 1))
                    dve.wait_ge(sig.xb_ok, at(p + 1))
                    nc.vector.tensor_tensor(
                        x_res[:, 2 * i:2 * i + 2, :], duo[0][:, i, :].rearrange("p (q n) -> p q n", q=2),
                        x_res[:, 2 * i:2 * i + 2, :], ALU.add)\
                        .then_inc(sig.z_ok, 1)

            def statistics(p):
                for q in range(TILES):
                    dve.wait_ge(sig.z_ok, at(2 * p + q // 2 + 1))
                    nc.vector.bn_stats(stats[:, q, :], x_res[:, q, :]).then_inc(sig.st_ok, 1)
                for q in range(TILES):
                    dve.wait_ge(sig.st_ok, at(TILES * p + q + 1))
                    apart(dve)
                    dve.wait_ge(sig.nm_ok, at(p))
                    apart(dve)
                    nc.vector.bn_aggr(mv[:, q, :], stats[:, q, :]).then_inc(sig.mv_ok, 1)

            def later_weights_lo():
                dve.wait_ge(sig.raw_in, 16 * 5)
                dve.wait_ge(sig.c_in, 16 * N_IN)
                for n, (lo_, raw_, hi_) in enumerate((
                        (wo[:, 1, :, :], raw_o[:, :, :], wo[:, 0, :, :]),
                        (wsgu[:, :, 1, :, :], raw_gu[:, :, :, :], wsgu[:, :, 0, :, :]),
                        (wsd[:, 1, :, :], raw_d[:, :, :], wsd[:, 0, :, :]),
                        (wr[:, 1, :, :], duo[2][:, 0, 0:KT * EXPERTS].rearrange("p (k e) -> p k e", k=KT),
                         wr[:, 0, :, :]))):
                    dve.wait_ge(sig.w_hi, n + 3)
                    nc.vector.tensor_tensor(lo_, raw_, f32(hi_), ALU.subtract).then_inc(sig.w_lo, 1)

            def split_lo(t, side):
                for e in range(2):
                    dve.wait_ge(sig.split_hi, at(4 * t + 2 * side + e + 1))
                    nc.vector.tensor_tensor(prod[:, side, 3 * e, :], prod[:, side, 3 * e, :], prod[:, side, 1 + e, :],
                                            ALU.subtract).then_inc(sig.split_lo, 1)

            def h_lo(p, j):
                dve.wait_ge(sig.h_hi, at(FT * p + j + 1))
                nc.vector.tensor_tensor(hT[:, 1, j, :], h[:, j % 2, :], f32(hT[:, 0, j, :]), ALU.subtract)\
                    .then_inc(sig.h_lo, 1)

            def plan_slots():
                dve.wait_ge(sig.route, ROUTE * PAIRS)
                nc.vector.tensor_tensor(count[:, :], start[:, TILES, :], region[:, :], ALU.subtract).then_inc(sig.plan, 1)
                nc.vector.memset(zero[:, :], 0.0).then_inc(sig.plan, 1)
                dve.wait_ge(sig.plan, 2)
                nc.vector.tensor_scalar(count_up[:, :], count[:, :], float(P - 1), None, ALU.add).then_inc(sig.plan, 1)
                dve.wait_ge(sig.plan, 3)
                nc.vector.tensor_scalar(slots_i[:, :], count_up[:, :], 7, None, ALU.logical_shift_right)\
                    .then_inc(sig.plan, 1)
                dve.wait_ge(sig.plan, 4)
                nc.vector.tensor_copy(slots_f[:, :], slots_i[:, :]).then_inc(sig.plan, 1)
                dve.wait_ge(sig.plan, 5)
                nc.vector.tensor_tensor_scan(slot_end[:, :], slots_f[:, :], zero[:, :], 0.0, ALU.add, ALU.add)\
                    .then_inc(sig.plan, 1)
                nc.vector.tensor_scalar(skip[:, :], slots_f[:, :], -float(P), float(TOKENS), ALU.mult, ALU.add)\
                    .then_inc(sig.plan, 1)
                dve.wait_ge(sig.plan, 7)
                nc.vector.tensor_tensor(passed[:, :, :], each(slot_no[:, :], EXPERTS - 1),
                                        over(slot_end[:, 0:EXPERTS - 1], SLOTS), ALU.is_ge).then_inc(sig.plan, 1)
                dve.wait_ge(sig.plan, 8)
                nc.vector.tensor_reduce(slot_e[:, :], passed[:, :, :], X, ALU.add).then_inc(sig.plan, 1)
                nc.vector.tensor_tensor(skipped[:, :, :], passed[:, :, :], over(skip[:, 0:EXPERTS - 1], SLOTS), ALU.mult)\
                    .then_inc(sig.plan, 1)
                dve.wait_ge(sig.plan, 10)
                nc.vector.tensor_copy(slot_ei[:, :], slot_e[:, :]).then_inc(sig.plan_ok, 1)
                nc.vector.tensor_reduce(slot_r[:, :], skipped[:, :, :], X, ALU.add).then_inc(sig.plan, 1)
                dve.wait_ge(sig.plan, 11)
                nc.vector.scalar_tensor_tensor(out=slot_row[:, :], in0=slot_no[:, :], scalar=float(P), in1=slot_r[:, :],
                                               op0=ALU.mult, op1=ALU.add).then_inc(sig.plan, 1)
                dve.wait_ge(sig.plan, 12)
                nc.vector.tensor_copy(slot_ri[:, :], slot_row[:, :]).then_inc(sig.plan_ok, 1)

            def choose(p):
                dve.wait_ge(sig.lg_ps, at(p + 1))
                nc.vector.tensor_copy(logits[:, :, :], duo[2][:, 1, 0:TILES * EXPERTS].rearrange("p (q e) -> p q e", e=EXPERTS))\
                    .then_inc(sig.route, 1)
                dve.wait_ge(sig.route, at(ROUTE * p + 1))
                dve.wait_ge(sig.pow_ok, at(p))
                nc.vector.tensor_reduce(top[:, :], logits[:, :, :], X, ALU.max).then_inc(sig.route, 1)
                dve.wait_ge(sig.route, at(ROUTE * p + 2))
                nc.vector.tensor_tensor(hot[:, :, :], logits[:, :, :], each(top[:, :], EXPERTS), ALU.is_equal)\
                    .then_inc(sig.route, 1)
                dve.wait_ge(sig.route, at(ROUTE * p + 3))
                nc.vector.tensor_tensor(ranked[:, :, :], hot[:, :, :], over(priority[:, :], TILES), ALU.mult)\
                    .then_inc(sig.route, 1)
                dve.wait_ge(sig.route, at(ROUTE * p + 4))
                nc.vector.tensor_reduce(first_of[:, :], ranked[:, :, :], X, ALU.max).then_inc(sig.route, 1)
                dve.wait_ge(sig.route, at(ROUTE * p + 5))
                nc.vector.tensor_tensor(hot[:, :, :], ranked[:, :, :], each(first_of[:, :], EXPERTS), ALU.is_equal)\
                    .then_inc(sig.hot_ok, 1)
                nc.vector.tensor_copy(start[:, 0, :], start[:, TILES, :]).then_inc(sig.route, 1)

            def find_seats(p):
                dve.wait_ge(sig.rank_ps, at(p + 1))
                totals = duo[2][:, 1, 2 * TILES * EXPERTS:3 * TILES * EXPERTS].rearrange("p (q e) -> p q e", e=EXPERTS)
                ranks = duo[2][:, 1, TILES * EXPERTS:2 * TILES * EXPERTS].rearrange("p (q e) -> p q e", e=EXPERTS)
                for q in range(TILES):
                    dve.wait_ge(sig.route, at(ROUTE * p + 6 + q))
                    nc.vector.tensor_tensor(start[:, q + 1, :], start[:, q, :], totals[:, q, :], ALU.add)\
                        .then_inc(sig.route, 1)
                dve.wait_ge(sig.route, at(ROUTE * p + 10))
                nc.vector.tensor_tensor(spot[:, :, :], ranks, start[:, 0:TILES, :], ALU.add).then_inc(sig.route, 1)
                dve.wait_ge(sig.route, at(ROUTE * p + 11))
                dve.wait_ge(sig.hot_ok, at(p + 1))
                nc.vector.tensor_tensor(spot[:, :, :], spot[:, :, :], hot[:, :, :], ALU.mult).then_inc(sig.route, 1)
                dve.wait_ge(sig.route, at(ROUTE * p + 12))
                nc.vector.tensor_reduce(place[:, :], spot[:, :, :], X, ALU.add).then_inc(sig.route, 1)
                dve.wait_ge(sig.route, at(ROUTE * p + 13))
                dve.wait_ge(sig.scat, at(16 * TILES * p))
                nc.vector.tensor_copy(place_i[:, :], place[:, :]).then_inc(sig.place_ok, 1)

            pipeline(dve, step)

            expert_lo(6)
            shared_sum(PAIRS - 1, 0)
            for k in range(KT):
                dve.wait_ge(sig.ew_hi, EXPERTS + k)
                nc.vector.tensor_tensor(w_gu[:, EXPERTS - 1, k, :].bitcast(F32R), w_gu[:, EXPERTS - 1, k, :],
                                        f32(w_gu_hi[:, EXPERTS - 1, k, :]), ALU.subtract).then_inc(sig.ew_lo, 1)

            def rows_lo(s):
                if is_slot(s):
                    dve.wait_ge(sig.xsT_hi, at(s + 1))
                    nc.vector.tensor_tensor(xsT[:, 1, :, :], duo[3][:, 0, 0:D].rearrange("p (k n) -> p k n", k=KT),
                                            f32(xsT[:, 0, :, :]), ALU.subtract).then_inc(sig.xsT_lo, 1)

            def slot_step(s, r, u):
                if is_slot(s):
                    dve.wait_ge(sig.eg_ps, at(2 * s + 2))
                    dve.wait_ge(sig.e_act_ok, at(s + 1))
                    dve.wait_ge(sig.ehT_ps, at(s))
                    nc.vector.scalar_tensor_tensor(out=eh[:, :], in0=duo[r % 2][:, 1, :], scalar=f32(seat[:, r, :])[:, 2:3],
                                                   in1=e_act[:, :], op0=ALU.mult, op1=ALU.mult).then_inc(sig.eh_ok, 1)
                rows_lo(s + 1)
                if is_slot(s - 1):
                    b, turn = ahead(r, u, -1)
                    dve.wait_ge(sig.ed_ps, at(s))
                    dve.wait_ge(sig.xz_in[b], at(16 * (turn + 1)))
                    dve.wait_ge(sig.out_done[(b - 2) % RING], at(16 * (turn + 1 if b >= 2 else turn)))
                    nc.vector.tensor_tensor(of[:, b % 2, :], duo[2][:, 1, 0:D], xz[:, b, D:2 * D], ALU.add)\
                        .then_inc(sig.sum_ok, 1)
                    dve.wait_ge(sig.sum_ok, at(s))
                    nc.vector.bn_stats(st2[:, :], of[:, b % 2, :]).then_inc(sig.st2_ok, 1)
                    dve.wait_ge(sig.st2_ok, at(s))
                    apart(dve)
                    nc.vector.bn_aggr(mv2[:, :], st2[:, :]).then_inc(sig.mv2_ok, 1)
                    dve.wait_ge(sig.mv2_ok, at(s))
                    dve.wait_ge(sig.lnr2_ok, at(s))
                    nc.vector.tensor_scalar(of[:, b % 2, :], of[:, b % 2, :], mv2[:, 0:1], ln2_r[:, :],
                                            ALU.subtract, ALU.mult).then_inc(sig.of_ok, 1)

            rows_lo(0)
            shared_sum(PAIRS - 1, 1)
            slot_pipeline(dve, slot_step)

        @block.tensor
        def _(pe):
            mm = nc.tensor.matmul

            def three(out_, left, right, kt, start=True, stop=True):
                for k in range(kt):
                    for n, (a, b) in enumerate(PASSES):
                        last = mm(out_, left(a, k), right(b, k), start=start and k == 0 and n == 0,
                                  stop=stop and k == kt - 1 and n == len(PASSES) - 1)
                return last

            def x_transposes(t):
                pe.wait_ge(sig.xin, at(16 * (t + 1)))
                pe.wait_ge(sig.yT_hi, at(KT * (t - 1)))
                pe.wait_ge(sig.yT_lo, at(KT * (t - 1)))
                for k in range(KT):
                    for q in range(TILES):
                        last = nc.tensor.transpose(duo[3][:, k, q * P:(q + 1) * P], x_in[:, q, k * P:(k + 1) * P], ident[:, :])
                last.then_inc(sig.xT_ps, 1)

            pe.wait_ge(sig.ident_in, 16)
            x_transposes(0)
            pe.wait_ge(sig.w_lo, 1)
            def similarities(p, j):
                b, hp = j // 4, j % 4
                if j == 0:
                    pe.wait_ge(sig.vg_ok, at(TILES * (p + 1)))
                    pe.wait_ge(sig.sact_ok, at(FT * (p - 1)))
                    pe.wait_ge(sig.h_ok, at(FT * (p - 1)))
                elif j == 1:
                    pe.wait_ge(sig.xT_lo, at(KT * (p + 2) if has(p + 1) else KT * (p + 1)))
                    pe.wait_ge(sig.yT_lo, at(KT * p))
                elif j == 2:
                    pe.wait_ge(sig.z_ok, at(2 * p))
                else:
                    pe.wait_ge(sig.s_diag, at(8 * p + j - 2))
                for i in range(2):
                    head = 2 * hp + i
                    for kb in range(2):
                        lo = SEQ * b + P * kb
                        last = mm(sim_duo[j % 3][:, i, SEQ * kb:SEQ * (kb + 1)], stack[1][:, head, lo:lo + P],
                                  stack[0][:, head, SEQ * b:SEQ * (b + 1)], start=True, stop=True)
                last.then_inc(sig.s_ps, 1)

            def values(p, a):
                b, g = a // 2, a % 2
                pe.wait_ge(sig.s_diag, at(8 * p + 2 * a + 2))
                pe.wait_ge(sig.s_off, at(8 * p + 2 * a + 2))
                if a < 2:
                    pe.wait_ge(sig.zs_ok, at(2 * (p - 1)))
                for kb in range(2):
                    for i in range(4):
                        ring, half = (2 * a + i // 2) % 4, i % 2
                        lo = SEQ * b + P * kb
                        rhs = sims[:, ring, half, 0:2, :] if kb == 0 else sims[:, ring, half, 2:3, :]
                        last = mm(duo[2][HD * i:HD * (i + 1), g, lo:SEQ * (b + 1)],
                                  vg[:, 2 * b + kb, HD * (4 * g + i):HD * (4 * g + i + 1)],
                                  rhs.rearrange("p b q -> p (b q)"), start=(kb == 0), stop=(kb == 1),
                                  skip_group_check=True)
                last.then_inc(sig.av_ps, 1)

            def project(t, s):
                side, e = s // 2, s % 2
                pe.wait_ge(sig.xT_hi, at(KT * (t + 1)))
                pe.wait_ge(sig.xT_lo, at(KT * (t + 1)))
                pe.wait_ge(sig.s_diag, at(8 * t - 2 + side))
                three(duo[side][:, e, :], lambda part, k: wqk[:, side, part, k, e::2],
                      lambda part, k: xT[:, part, k, :], KT).then_inc(sig.qk_ps, 1)

            def step(t):
                if has(t - 1):
                    p = t - 1
                    pe.wait_ge(sig.stack_in, at(192 * (p + 1)))
                    for j in range(8):
                        similarities(p, j)
                        if j in (3, 5, 7):
                            values(p, (j - 3) // 2)
                if has(t):
                    project(t, 0)
                if has(t - 1):
                    values(t - 1, 3)
                if has(t):
                    for s in range(1, 4):
                        project(t, s)
                if has(t - 1):
                    p = t - 1
                    pe.wait_ge(sig.retT_ok, at(2 * (p + 1)))
                    pe.wait_ge(sig.s_diag, at(8 * t))
                    pe.wait_ge(sig.xT_lo, at(KT * (p + 2) if has(p + 1) else KT * (p + 1)))
                    for g in range(2):
                        for q in range(TILES):
                            last = nc.tensor.transpose(duo[3][:, q // 2, D * (q % 2) + P * g:D * (q % 2) + P * (g + 1)],
                                                       retT[:, g, q * P:(q + 1) * P], ident[:, :])
                    last.then_inc(sig.rn_ps, 1)
                if has(t - 2):
                    p = t - 2
                    pe.wait_ge(sig.x1_ok, at(TILES * (p + 1)))
                    pe.wait_ge(sig.retT_ok, at(2 * (p + 2) if has(p + 1) else 2 * (p + 1)))
                    pe.wait_ge(sig.zs_ok, at(2 * p))
                    for k in range(KT):
                        for q in range(TILES):
                            last = nc.tensor.transpose(duo[2][:, k, q * P:(q + 1) * P], x1_of(p)[:, q, k * P:(k + 1) * P],
                                                       ident[:, :])
                    last.then_inc(sig.x1T_ps, 1)
                if isinstance(t, int) and t == 0:
                    pe.wait_ge(sig.w_lo, 2)
                if has(t):
                    for q in range(TILES):
                        pe.wait_ge(sig.prod_ok, at(4 * t + q + 1))
                        three(duo[q // 2][:, q % 2, :], lambda part, k: xT[:, part, k, q * P:(q + 1) * P],
                              lambda part, k: wvg[:, part, k, :], KT).then_inc(sig.vg_ps, 1)
                if isinstance(t, int) and t == 0:
                    pe.wait_ge(sig.raw_in, 16 * 5)
                    for k in range(KT):
                        last = nc.tensor.transpose(duo[2][:, 0, k * EXPERTS:(k + 1) * EXPERTS], raw_r[:, k * P:(k + 1) * P],
                                                   ident[0:EXPERTS, 0:EXPERTS])
                    last.then_inc(sig.wrT_ps, 1)
                if isinstance(t, int) and t == 1:
                    pe.wait_ge(sig.w_lo, 6)
                    pe.wait_ge(sig.c_in, 16 * N_IN)
                if has(t - 2):
                    p = t - 2
                    pe.wait_ge(sig.x1T_hi, at(KT * (p + 1)))
                    pe.wait_ge(sig.x1T_lo, at(KT * (p + 1)))
                    three(duo[2][0:EXPERTS, 0, :], lambda part, k: wr[:, part, k, :],
                          lambda part, k: x1T[:, part, k, :], KT).then_inc(sig.lgT_ps, 1)
                    for j in range(FT):
                        if j == 2:
                            pe.wait_ge(sig.lgT_ok, at(p + 1))
                            apart(pe)
                            for q in range(TILES):
                                last = nc.tensor.transpose(duo[2][:, 1, q * EXPERTS:(q + 1) * EXPERTS],
                                                           lgT[:, q * P:(q + 1) * P], ident[0:EXPERTS, 0:EXPERTS])
                            last.then_inc(sig.lg_ps, 1)
                        if j == 3:
                            pe.wait_ge(sig.hot_ok, at(p + 1))
                            w = TILES * EXPERTS
                            flat = hot[:, :, :].rearrange("p t e -> p (t e)")
                            mm(duo[2][:, 1, w:2 * w], before[:, :], flat, start=True, stop=True)
                            mm(duo[2][:, 1, 2 * w:3 * w], ones[:, :], flat, start=True, stop=True)\
                                .then_inc(sig.rank_ps, 1)
                            if is_last(t):
                                y_transposes(t - 1)
                        if j < 2:
                            if has(t):
                                pe.wait_ge(sig.vg_ok, at(TILES * (t + 1)))
                            if has(t - 1):
                                pe.wait_ge(sig.s_diag, at(8 * t))
                            pe.wait_ge(sig.z_ok, at(2 * (p + 1)))
                        else:
                            pe.wait_ge(sig.sact_ok, at(FT * p + j - 1))
                            pe.wait_ge(sig.h_ok, at(FT * p + j - 1))
                        for i in range(2):
                            three(duo[j % 2][:, i, :], lambda part, k: wsgu[:, i, part, k, j * P:(j + 1) * P],
                                  lambda part, k: x1T[:, part, k, :], KT).then_inc(sig.gu_ps, 1)
                if has(t - 1) and not is_last(t):
                    y_transposes(t - 1)
                if is_last(t):
                    output(t - 1)
                if has(t - 2):
                    shared_down(t - 2)
                if has(t + 1):
                    x_transposes(t + 1)
                if has(t - 1) and not is_last(t):
                    output(t - 1)

            def y_transposes(p):
                pe.wait_ge(sig.y_ok, at(2 * (p + 1)))
                pe.wait_ge(sig.rn_ok, at(2 * (p + 1)))
                for k in range(KT):
                    for q in range(TILES):
                        last = nc.tensor.transpose(duo[3][:, k, q * P:(q + 1) * P], y[:, q, k * P:(k + 1) * P], ident[:, :])
                last.then_inc(sig.yT_ps, 1)

            def shared_down(p):
                pe.wait_ge(sig.route, at(ROUTE * p + 11))

                def down_part(q, parts):
                    for f in parts:
                        last = three(duo[2][:, q // 2, D * (q % 2):D * (q % 2 + 1)],
                                     lambda part, k: hT[:, part, f, q * P:(q + 1) * P],
                                     lambda part, k: wsd[:, part, f, :], 1, start=(f == 0), stop=(f == FT - 1))
                    return last

                pe.wait_ge(sig.h_hi, at(FT * (p + 1) - 2))
                pe.wait_ge(sig.h_lo, at(FT * (p + 1) - 2))
                down_part(0, range(FT - 2))
                down_part(2, range(FT - 2))
                pe.wait_ge(sig.h_hi, at(FT * (p + 1) - 1))
                pe.wait_ge(sig.h_lo, at(FT * (p + 1) - 1))
                down_part(0, [FT - 2])
                down_part(2, [FT - 2])
                pe.wait_ge(sig.h_hi, at(FT * (p + 1)))
                pe.wait_ge(sig.h_lo, at(FT * (p + 1)))
                down_part(0, [FT - 1])
                down_part(1, range(FT)).then_inc(sig.dn_ps, 1)
                down_part(2, [FT - 1])
                down_part(3, range(FT)).then_inc(sig.dn_ps, 1)

            def output(p):
                pe.wait_ge(sig.yT_hi, at(KT * (p + 1)))
                pe.wait_ge(sig.yT_lo, at(KT * (p + 1)))
                if has(p + 1):
                    pe.wait_ge(sig.vg_ok, at(TILES * (p + 2)))
                if has(p - 1):
                    pe.wait_ge(sig.h_ok, at(FT * p))
                pe.wait_ge(sig.s_diag, at(8 * (p + 1)))
                for q in range(TILES):
                    last = three(duo[0][:, q // 2, D * (q % 2):D * (q % 2 + 1)],
                                 lambda part, k: yT[:, part, k, q * P:(q + 1) * P],
                                 lambda part, k: wo[:, part, k, :], KT)
                    if q % 2:
                        last.then_inc(sig.o_ps, 1)

            pipeline(pe, step)

            def slot_transposes(s, r, u):
                if is_slot(s):
                    if isinstance(s, int) and s < 2:
                        pe.wait_ge(sig.x_only_in[s], 16)
                    else:
                        pe.wait_ge(sig.xz_in[r], at(16 * (u + 1)))
                    pe.wait_ge(sig.xsT_lo, at(s))
                    for k in range(KT):
                        last = nc.tensor.transpose(duo[3][:, 0, k * P:(k + 1) * P], xz[:, r, k * P:(k + 1) * P], ident[:, :])
                    last.then_inc(sig.xsT_ps, 1)

            gu_flat = (w_gu_hi[:, :, :, :].rearrange("p e k n -> p (e k n)"),
                       w_gu[:, :, :, :].rearrange("p e k n -> p (e k n)").bitcast(F32R))
            dn_flat = w_dn[:, :, :, :].rearrange("p e f n -> p (e f n)")

            def expert_of(s):
                return pe.value_load(slot_ei[0:1, one(s)], min_val=0, max_val=EXPERTS - 1)

            def slot_step(s, r, u):
                if is_slot(s):
                    pe.wait_ge(sig.xsT_lo, at(s + 1))
                    apart(pe)
                    pe.wait_ge(sig.eh_ok, at(s - 1))
                    apart(pe)
                    e = expert_of(s)
                    for half in range(2):
                        three(duo[r % 2][:, half, :], lambda part, k: xsT[:, part, k, :],
                              lambda part, k: gu_flat[part][:, bass.ds(e * (KT * 2 * FF) + (k * 2 + half) * FF, FF)],
                              KT).then_inc(sig.eg_ps, 1)
                slot_transposes(s + 1, *ahead(r, u, 1))
                if is_slot(s - 1):
                    pe.wait_ge(sig.ehT_ok, at(s))
                    apart(pe)
                    pe.wait_ge(sig.sum_ok, at(s - 1))
                    apart(pe)
                    if isinstance(s, int) and s == 1:
                        pe.wait_ge(sig.edn_in, 16 * EXPERTS)
                    e = expert_of(s - 1)
                    for f in range(FT):
                        last = mm(duo[2][:, 1, 0:D], ehT[:, f, :], dn_flat[:, bass.ds(e * (FT * D) + f * D, D)],
                                  start=(f == 0), stop=(f == FT - 1))
                    last.then_inc(sig.ed_ps, 1)
                if is_slot(s):
                    pe.wait_ge(sig.eh_ok, at(s + 1))
                    pe.wait_ge(sig.ehT_ok, at(s))
                    for f in range(FT):
                        last = nc.tensor.transpose(duo[2][:, 0, f * P:(f + 1) * P], eh[:, f * P:(f + 1) * P], ident[:, :])
                    last.then_inc(sig.ehT_ps, 1)

            pe.wait_ge(sig.plan_ok, 2)
            slot_transposes(0, 0, 0)
            pe.wait_ge(sig.ew_hi, EXPERTS + 1)
            pe.wait_ge(sig.ew_lo, 5)
            pe.wait_ge(sig.ew_lo2, 4)
            slot_pipeline(pe, slot_step)


def tables():
    f = np.float32
    start, stop = f(0.0), f(1.0)
    xs_ = np.linspace(start, stop, HALF, dtype=f)
    theta = (f(1.0) / np.power(f(10000.0), xs_)).astype(f)
    angle = (np.arange(SEQ, dtype=f)[None, :] * theta[:, None]).astype(f).astype(np.float64)
    gamma = (f(1.0) - np.exp(np.linspace(f(np.log(1 / 32)), f(np.log(1 / 64)), HEADS, dtype=f)).astype(f)).astype(f)
    n = np.arange(SEQ, dtype=np.float64)
    decay = gamma.astype(np.float64)[:, None] ** n[None, :]
    rotation = np.zeros((HEADS, HALF, 4, SEQ))
    for i, table in enumerate((np.cos(angle), np.sin(angle))):
        rotation[:, :, i] = table[None] * decay[:, None]
        rotation[:, :, 2 + i] = table[None] / decay[:, None] / np.sqrt(float(HD))
    r = np.arange(P)
    squares = np.zeros((P, 4 * P + EXPERTS + SLOTS + EXPERTS), f)
    squares[:, 0:P] = np.eye(P)
    squares[:, P:2 * P] = r[None, :] >= r[:, None]
    squares[:, 2 * P:3 * P] = r[:, None] < r[None, :]
    squares[:, 3 * P:4 * P] = 1.0
    squares[:, 4 * P:4 * P + EXPERTS] = EXPERTS - np.arange(EXPERTS)
    squares[:, 4 * P + EXPERTS:4 * P + EXPERTS + SLOTS] = np.arange(SLOTS)
    squares[:, 4 * P + EXPERTS + SLOTS:] = TOKENS * np.arange(EXPERTS)
    token_seats = np.zeros((P, NTILE, SEAT), np.int32)
    token_seats[:, :, 0:2] = (np.arange(NTILE)[None, :] * P + r[:, None])[:, :, None]
    free_seats = np.zeros((SEATS, SEAT), np.int32)
    free_seats[:, 0] = TOKENS
    free_seats[:, 1] = TOKENS + np.arange(SEATS) % P
    return (rotation.reshape(P, 4 * SEQ).astype(f), squares, token_seats.reshape(P, NTILE * SEAT), free_seats)


_INS = ["L0_attn_x", "L0_attn_w_q", "L0_attn_b_q", "L0_attn_w_k", "L0_attn_b_k", "L0_attn_w_v", "L0_attn_b_v",
        "L0_attn_w_g", "L0_attn_b_g", "L0_attn_w_o", "L0_attn_b_o", "L0_attn_gn_weight", "L0_attn_gn_bias",
        "L0_ffn_router_w", "L0_ffn_gate_up_proj", "L0_ffn_down_proj", "L0_ffn_shared_gate_w",
        "L0_ffn_shared_up_w", "L0_ffn_shared_down_w"]


def kernel(**inputs):
    import concourse.bacc as bacc
    from concourse.bass_utils import run_bass_kernel_spmd

    nc = bacc.Bacc("TRN2", target_bir_lowering=False, num_devices=1)
    arrays, args = {}, []

    def give(name, a):
        arrays[name] = a
        args.append(nc.dram_tensor(name, a.shape, mybir.dt.from_np(a.dtype), kind="ExternalInput").ap())

    for name in _INS:
        a = np.ascontiguousarray(inputs[name])
        give(name, a.reshape(SEQS * SEQ, D) if name == "L0_attn_x" else a)
    for name, table in zip(("rotation", "squares", "token_seats", "free_seats"), tables()):
        give(name, table)
    args.append(nc.dram_tensor("out_rows", (TOKENS + P, D), F32, kind="ExternalOutput").ap())
    build(nc, *args)
    r = run_bass_kernel_spmd(nc, [arrays], core_ids=[0])
    return r.results[0]["out_rows"][:TOKENS].reshape(SEQS, SEQ, D)
```
